# Optimizing a Trainium2 kernel written in Bass

```python
import numpy as np
import jax
import jax.numpy as jnp

def _softmax(x, axis=-1):
    return jax.nn.softmax(x, axis=axis)

def _gelu(x):
    return jax.nn.gelu(x, approximate=True)

def _silu(x):
    return jax.nn.silu(x)

def _sigmoid(x):
    return jax.nn.sigmoid(x)

def _layernorm(x, axis=-1, eps=1e-05):
    m = jnp.mean(x, axis=axis, keepdims=True)
    v = jnp.var(x, axis=axis, keepdims=True)
    return (x - m) / jnp.sqrt(v + eps)

def _scatter_add(tgt, idx, src, axis=0):
    return tgt.at[idx].add(src)

def _segment_sum(src, seg, n):
    return jax.ops.segment_sum(src, seg, n)
kernel_name = 'mk_conv_attn_hybrid_d2_conv_nhwc384_r4_f24f1f'

def setup_inputs(seed: int=0):
    np.random.seed(seed)
    _w = jnp.asarray

    def _rec_inputs():
        import jax
        import jax.numpy as jnp
        _gk = jax.random.key(seed)
        x = -4.65e-05 + 0.9999 * jax.random.normal(jax.random.fold_in(_gk, 1), (32, 16, 16, 96), jnp.float32)
        return x
    x = _rec_inputs()

    def _L0_conv_setup():
        import jax, jax.numpy as jnp
        import numpy as np
        B, H, W, C = (32, 16, 16, 96)
        WS = 8
        NH = 12
        HD = C // NH
        SCALE = HD ** (-0.5)
        key = jax.random.key(seed)
        ks = jax.random.split(key, 5)
        std = 0.02
        return {'x': jax.random.normal(ks[0], (B, H, W, C), dtype=jnp.float32), 'w_qkv': jax.random.normal(ks[1], (C, 3 * C), dtype=jnp.float32) * std, 'b_qkv': jnp.zeros((3 * C,), dtype=jnp.float32), 'w_proj': jax.random.normal(ks[2], (C, C), dtype=jnp.float32) * std, 'b_proj': jnp.zeros((C,), dtype=jnp.float32)}
    _L0_conv_all = _L0_conv_setup()
    _L0_conv_in = {k: v for k, v in _L0_conv_all.items() if k in ('w_qkv', 'b_qkv', 'w_proj', 'b_proj')}
    del _L0_conv_all

    def _L1_attn_setup():
        import jax, jax.numpy as jnp
        import numpy as np
        import math
        NUM_HEADS = 12
        LAMBDA_INIT = 0.8 - 0.6 * math.exp(-0.3 * (2 - 1))
        SIGMA = 0.5

        def _feature_map(t):
            return jnp.where(t >= 0, t + 1.0, jnp.exp(t))
        key = jax.random.key(seed)
        ks = jax.random.split(key, 9)
        B_, N, C, H = (512, 16, 96, NUM_HEADS)
        d = C // H
        s = 0.02
        return {'x': jax.random.normal(ks[0], (B_, N, C), dtype=jnp.float32), 'qkv_w': jax.random.normal(ks[1], (C, 3 * C), dtype=jnp.float32) * s, 'qkv_b': jax.random.normal(ks[2], (3 * C,), dtype=jnp.float32) * s, 'proj_w': jax.random.normal(ks[3], (C, C), dtype=jnp.float32) * s, 'proj_b': jax.random.normal(ks[4], (C,), dtype=jnp.float32) * s, 'lambda_k1': jax.random.normal(ks[5], (H, d), dtype=jnp.float32) * 0.1, 'lambda_v1': jax.random.normal(ks[6], (H, d), dtype=jnp.float32) * 0.1, 'lambda_k2': jax.random.normal(ks[7], (H, d), dtype=jnp.float32) * 0.1, 'lambda_v2': jax.random.normal(ks[8], (H, d), dtype=jnp.float32) * 0.1}
    _L1_attn_all = _L1_attn_setup()
    _L1_attn_in = {k: v for k, v in _L1_attn_all.items() if k in ('qkv_w', 'qkv_b', 'proj_w', 'proj_b', 'lambda_k1', 'lambda_v1', 'lambda_k2', 'lambda_v2')}
    del _L1_attn_all

    def _L1_ffn_setup():
        import jax, jax.numpy as jnp
        import numpy as np
        NUM_EXPERTS = 4
        TOP_K = 2
        DIM = 96
        HID = 4 * DIM
        key = jax.random.key(seed)
        ks = jax.random.split(key, 5)
        B, S = (16, 512)
        scale_in = 1.0 / np.sqrt(DIM)
        scale_hid = 1.0 / np.sqrt(HID)
        return {'x': jax.random.normal(ks[0], (B, S, DIM), dtype=jnp.float32), 'gate_w': jax.random.normal(ks[1], (DIM, NUM_EXPERTS), dtype=jnp.float32) * scale_in, 'gate_b': jnp.zeros((NUM_EXPERTS,), dtype=jnp.float32), 'w1': jax.random.normal(ks[2], (NUM_EXPERTS, DIM, HID), dtype=jnp.float32) * scale_in, 'b1': jnp.zeros((NUM_EXPERTS, HID), dtype=jnp.float32), 'w2': jax.random.normal(ks[3], (NUM_EXPERTS, HID, DIM), dtype=jnp.float32) * scale_hid, 'b2': jnp.zeros((NUM_EXPERTS, DIM), dtype=jnp.float32)}
    _L1_ffn_all = _L1_ffn_setup()
    _L1_ffn_in = {k: v for k, v in _L1_ffn_all.items() if k in ('gate_w', 'gate_b', 'w1', 'b1', 'w2', 'b2')}
    del _L1_ffn_all
    return {'x': x, 'L0_conv_w_qkv': _L0_conv_in['w_qkv'], 'L0_conv_b_qkv': _L0_conv_in['b_qkv'], 'L0_conv_w_proj': _L0_conv_in['w_proj'], 'L0_conv_b_proj': _L0_conv_in['b_proj'], 'L1_attn_qkv_w': _L1_attn_in['qkv_w'], 'L1_attn_qkv_b': _L1_attn_in['qkv_b'], 'L1_attn_proj_w': _L1_attn_in['proj_w'], 'L1_attn_proj_b': _L1_attn_in['proj_b'], 'L1_attn_lambda_k1': _L1_attn_in['lambda_k1'], 'L1_attn_lambda_v1': _L1_attn_in['lambda_v1'], 'L1_attn_lambda_k2': _L1_attn_in['lambda_k2'], 'L1_attn_lambda_v2': _L1_attn_in['lambda_v2'], 'L1_ffn_gate_w': _L1_ffn_in['gate_w'], 'L1_ffn_gate_b': _L1_ffn_in['gate_b'], 'L1_ffn_w1': _L1_ffn_in['w1'], 'L1_ffn_b1': _L1_ffn_in['b1'], 'L1_ffn_w2': _L1_ffn_in['w2'], 'L1_ffn_b2': _L1_ffn_in['b2']}

def reference(x, L0_conv_w_qkv, L0_conv_b_qkv, L0_conv_w_proj, L0_conv_b_proj, L1_attn_qkv_w, L1_attn_qkv_b, L1_attn_proj_w, L1_attn_proj_b, L1_attn_lambda_k1, L1_attn_lambda_v1, L1_attn_lambda_k2, L1_attn_lambda_v2, L1_ffn_gate_w, L1_ffn_gate_b, L1_ffn_w1, L1_ffn_b1, L1_ffn_w2, L1_ffn_b2):
    import jax
    import jax.numpy as jnp

    def _L0_conv_ref(x, w_qkv, b_qkv, w_proj, b_proj):
        import jax, jax.numpy as jnp
        import numpy as np
        B, H, W, C = (32, 16, 16, 96)
        WS = 8
        NH = 12
        HD = C // NH
        SCALE = HD ** (-0.5)
        b, h, w, c = x.shape
        nh_win, nw_win = (h // WS, w // WS)
        xw = x.reshape(b, nh_win, WS, nw_win, WS, c)
        xw = xw.transpose(0, 1, 3, 2, 4, 5).reshape(b * nh_win * nw_win, WS * WS, c)
        nW, T = (xw.shape[0], WS * WS)
        qkv = xw @ w_qkv + b_qkv
        qkv = qkv.reshape(nW, T, 3, NH, HD).transpose(2, 0, 3, 1, 4)
        q, k, v = (qkv[0], qkv[1], qkv[2])
        attn = jnp.einsum('wntd,wnsd->wnts', q, k) * SCALE
        attn = jax.nn.softmax(attn, axis=-1)
        out = jnp.einsum('wnts,wnsd->wntd', attn, v)
        out = out.transpose(0, 2, 1, 3).reshape(nW, T, c)
        out = out @ w_proj + b_proj
        out = out.reshape(b, nh_win, nw_win, WS, WS, c)
        out = out.transpose(0, 1, 3, 2, 4, 5).reshape(b, h, w, c)
        return out

    def _L1_attn_ref(x, qkv_w, qkv_b, proj_w, proj_b, lambda_k1, lambda_v1, lambda_k2, lambda_v2):
        import jax, jax.numpy as jnp
        import numpy as np
        import math
        NUM_HEADS = 12
        LAMBDA_INIT = 0.8 - 0.6 * math.exp(-0.3 * (2 - 1))
        SIGMA = 0.5

        def _feature_map(t):
            return jnp.where(t >= 0, t + 1.0, jnp.exp(t))
        B_, N, C = x.shape
        H = NUM_HEADS
        d = C // H
        scale = d ** (-0.5)
        qkv = (x @ qkv_w + qkv_b).reshape(B_, N, 3, H, d).transpose(2, 0, 3, 1, 4)
        q, k, v = (qkv[0], qkv[1], qkv[2])
        q = q * scale
        lam1 = jnp.exp(jnp.sum(lambda_k1 * lambda_v1, axis=-1))
        lam2 = jnp.exp(jnp.sum(lambda_k2 * lambda_v2, axis=-1))
        lambda_full = lam1 - lam2 + LAMBDA_INIT
        fk = _feature_map(jnp.swapaxes(k, -1, -2))
        fv = _feature_map(v)
        idx = jnp.arange(d, dtype=jnp.float32)
        gauss = jnp.exp(-(idx[:, None] - idx[None, :]) ** 2 / (2.0 * SIGMA ** 2))
        A = jnp.einsum('bhdn,bhne->bhde', fk, fv) * gauss
        attn = A - lambda_full[None, :, None, None] * A
        out = jnp.einsum('bhnd,bhde->bhne', q, attn)
        out = jnp.swapaxes(out, 1, 2).reshape(B_, N, C)
        return out @ proj_w + proj_b

    def _L1_ffn_ref(x, gate_w, gate_b, w1, b1, w2, b2):
        import jax, jax.numpy as jnp
        import numpy as np
        NUM_EXPERTS = 4
        TOP_K = 2
        DIM = 96
        HID = 4 * DIM
        scores = jnp.einsum('bsd,de->bse', x, gate_w) + gate_b
        probs = jax.nn.softmax(scores, axis=-1)
        topk_vals, topk_idx = jax.lax.top_k(probs, TOP_K)
        mask = jnp.sum(jax.nn.one_hot(topk_idx, NUM_EXPERTS, dtype=probs.dtype), axis=-2)
        masked = probs * mask
        masked = masked / (jnp.sum(masked, axis=-1, keepdims=True) + 1e-09)
        h = jax.nn.gelu(jnp.einsum('bsd,edh->ebsh', x, w1) + b1[:, None, None, :], approximate=False)
        y = jnp.einsum('ebsh,ehd->ebsd', h, w2) + b2[:, None, None, :]
        out = jnp.einsum('bse,ebsd->bsd', masked, y)
        return out

    def _gn(v, G=32, eps=1e-05):
        B_, H_, W_, C_ = v.shape
        g = v.reshape(B_, H_, W_, G, C_ // G)
        m = jnp.mean(g, axis=(1, 2, 4), keepdims=True)
        s = jnp.var(g, axis=(1, 2, 4), keepdims=True)
        return ((g - m) / jnp.sqrt(s + eps)).reshape(v.shape)

    def _ln_c(v, eps=1e-06):
        m = jnp.mean(v, axis=-1, keepdims=True)
        s = jnp.var(v, axis=-1, keepdims=True)
        return (v - m) / jnp.sqrt(s + eps)

    def _ln_t(v, eps=1e-05):
        m = jnp.mean(v, axis=-1, keepdims=True)
        s = jnp.var(v, axis=-1, keepdims=True)
        return (v - m) / jnp.sqrt(s + eps)

    def _to_tokens(v):
        B_, H_, W_, C_ = v.shape
        return v.reshape(B_, H_ * W_, C_)

    def _from_tokens(t, like):
        return t.reshape(like.shape)
    x = x + _L0_conv_ref(_gn(x), L0_conv_w_qkv, L0_conv_b_qkv, L0_conv_w_proj, L0_conv_b_proj)
    t = _to_tokens(x)
    t = t + _L1_attn_ref(_ln_t(t), L1_attn_qkv_w, L1_attn_qkv_b, L1_attn_proj_w, L1_attn_proj_b, L1_attn_lambda_k1, L1_attn_lambda_v1, L1_attn_lambda_k2, L1_attn_lambda_v2)
    t = t + _L1_ffn_ref(_ln_t(t), L1_ffn_gate_w, L1_ffn_gate_b, L1_ffn_w1, L1_ffn_b1, L1_ffn_w2, L1_ffn_b2)
    x = _from_tokens(t, x)
    return x

_drawn_inputs = setup_inputs


def setup_inputs(seed=0):
    import zlib

    import numpy as np

    out = dict(_drawn_inputs(seed))
    spreads = {'L0_conv_b_qkv': (0.0, 0.336),
     'L0_conv_b_proj': (0.0, 0.1),
     'L1_ffn_gate_b': (0.0, 0.294),
     'L1_ffn_b1': (0.0, 0.413),
     'L1_ffn_b2': (0.0, 0.268)}
    factors = {'L0_conv_w_qkv': 8.0, 'L1_attn_proj_b': 4.963}
    for name, (base, spread) in spreads.items():
        noise = np.random.default_rng([zlib.crc32(name.encode()), seed]).standard_normal(out[name].shape)
        drawn = base * np.exp(spread * noise) if base else spread * noise
        out[name] = jnp.asarray(drawn.astype(out[name].dtype))
    for name, factor in factors.items():
        out[name] = (out[name] * factor).astype(out[name].dtype)
    return out
```

```python
from contextlib import ExitStack
import math

import numpy as np
import concourse.bass as bass
from concourse import mybir

F32 = mybir.dt.float32
I32 = mybir.dt.int32
ALU = mybir.AluOpType
ACT = mybir.ActivationFunctionType
AX = mybir.AxisListType

B, HI, WI, C = 32, 16, 16, 96
WS = 8
NH, HD = 12, 8
T = WS * WS
TP = 2 * T
NP = HI * WI // TP
N = HI * WI
NW = N // T
HP = NH // 2
GC = C // 32
SCALE = HD ** -0.5
LAMBDA_INIT = 0.8 - 0.6 * math.exp(-0.3)
GN_EPS, LN_EPS = 1e-5, 1e-5
NE, HID = 4, 4 * C
CH = HID // 128
FT = 512
NFT = B * N // FT
FP = FT // TP
NPA = B * NP
VW = 32


def build(nc, x, w0, b0, wp0, bp0, w1a, b1a, wp1, bp1, lk1, lv1, lk2, lv2, gw, gb, ew1, eb1, ew2, eb2, out):
    with ExitStack() as ctx:
        def sb(name, shape, dt=F32):
            return ctx.enter_context(nc.sbuf_tensor(name, shape, dt))

        def sem(name):
            return ctx.enter_context(nc.semaphore(name))

        ident = sb("ident", [128, 128])
        group_mean = sb("group_mean", [C, C])
        head_of = sb("head_of", [C, NH])
        head_rows = sb("head_rows", [NH, C])
        block = sb("block", [C, C])
        offsets = sb("offsets", [C, C], I32)
        offsets_f = sb("offsets_f", [C, C])
        offsets_sq = sb("offsets_sq", [C, C])
        gauss = sb("gauss", [C, C])
        attn_mask = sb("attn_mask", [C, C])
        lower = sb("lower", [128, NE, NE])
        minus_half = sb("minus_half", [128, NP])
        ln_eps = sb("ln_eps", [128, NP])
        wqkv0 = sb("wqkv0", [C + 1, 3 * C])
        wproj0 = sb("wproj0", [C + 1, C])
        wqkv1 = sb("wqkv1", [C + 1, 3 * C])
        wq1T = sb("wq1T", [C, C + 1])
        wproj1 = sb("wproj1", [C, C])
        bproj1 = sb("bproj1", [C + 1, C])
        gate_w = sb("gate_w", [C + 1, NE])
        up_w = sb("up_w", [C + 1, NE, HID])
        down_w = sb("down_w", [128, NE, CH, C])
        down_b = sb("down_b", [C, NE])
        lam_in = sb("lam_in", [NH, 4, HD])
        lam_prod = sb("lam_prod", [NH, 2, HD])
        lam_sum = sb("lam_sum", [NH, 2])
        lam_exp = sb("lam_exp", [NH, 2])
        lam_dif = sb("lam_dif", [NH, 1])
        lam_keep = sb("lam_keep", [NH, 1])
        lam_col = sb("lam_col", [C, 1])

        x_in = [sb(f"x_in{u}", [128, NP, C]) for u in range(2)]
        x_res = [sb(f"x_res{u}", [128, NP, C]) for u in range(2)]
        gn_stats = sb("gn_stats", [C, 6])
        gn_mv = sb("gn_mv", [C, 2])
        gn_mean = sb("gn_mean", [C, 1])
        gn_dif = sb("gn_dif", [C, 1])
        gn_spread = sb("gn_spread", [C, 1])
        gn_var = sb("gn_var", [C, 1])
        gn_rstd = sb("gn_rstd", [C, 1])
        xh = sb("xh", [C + 1, N])
        qk = [sb(f"qk{u}", [C, 2, N]) for u in range(2)]
        k_heads = [sb(f"k_heads{u}", [C, NH, N]) for u in range(2)]
        v_heads = [sb(f"v_heads{u}", [128, NW, HP, VW]) for u in range(2)]
        score_max = sb("score_max", [128, NH])
        shifted = [sb(f"shifted{p}", [128, NH, T]) for p in range(NP)]
        probs = [sb(f"probs{p}", [128, HP, TP]) for p in range(NP)]
        o_sb = sb("o_sb", [C, 2 * N])
        o_rden = sb("o_rden", [128, NP * NH])
        o_norm = sb("o_norm", [128, NP * NH, HD])
        oT_sb = sb("oT_sb", [C + 1, N])
        t1 = [sb(f"t1_{u}", [128, NP, C]) for u in range(2)]
        ln1_stats = sb("ln1_stats", [128, NP, 6])
        ln1_mv = sb("ln1_mv", [128, NP, 2])
        ln1_var = sb("ln1_var", [128, NP])
        ln1_rstd = sb("ln1_rstd", [128, NP])
        h1 = sb("h1", [128, NP, C])
        h1T = sb("h1T", [C + 1, N])
        kv_neg = sb("kv_neg", [128, NP, 2 * C])
        kv_exp = sb("kv_exp", [128, NP, 2 * C])
        feat = sb("feat", [128, NP, 2 * C])
        attn_sb = sb("attn_sb", [C, C])
        attn_proj = sb("attn_proj", [C, C])
        fold_w = sb("fold_w", [C + 1, C])
        ln2_stats = sb("ln2_stats", [128, NP, 6])
        ln2_mv = sb("ln2_mv", [128, NP, 2])
        ln2_var = sb("ln2_var", [128, NP])
        ln2_rstd = sb("ln2_rstd", [128, NP])
        h2 = sb("h2", [128, NP, C])
        h2T = sb("h2T", [C + 1, N])
        t2_all = sb("t2_all", [128, NPA, C])
        h2T_all = sb("h2T_all", [C + 1, B * N])
        scores = sb("scores", [128, NPA, NE])

        g_max = sb("g_max", [128, NPA])
        g_shift = sb("g_shift", [128, NPA, NE])
        g_exp = sb("g_exp", [128, NPA, NE])
        g_sum = sb("g_sum", [128, NPA])
        g_rsum = sb("g_rsum", [128, NPA])
        g_prob = sb("g_prob", [128, NPA, NE])
        g_above = sb("g_above", [128, NPA, NE, NE])
        g_equal = sb("g_equal", [128, NPA, NE, NE])
        g_rank = sb("g_rank", [128, NPA * NE])
        g_mix = sb("g_mix", [128, NPA * NE])
        mixT = sb("mixT", [128, 2, 128])
        mix_rows = [sb(f"mix_rows{u}", [C, FP, NE, 128]) for u in range(2)]
        hidden = [sb(f"hidden{n}", [128, FT]) for n in range(4)]
        y_scaled = sb("y_scaled", [C, FT])
        y_acc = [sb(f"y_acc{u}", [C, FT]) for u in range(2)]
        out_sb = [sb(f"out_sb{u}", [128, FP, C]) for u in range(2)]
        mix_dram = nc.dram_tensor("mix_dram", [NPA, NE, 128], F32, kind="Internal").ap()

        ps = ctx.enter_context(nc.psum_tensor("ps", [128, 8, 512], F32))
        FRONT, TAIL_A, TAIL_B, OUT_B = 0, 1, 2, 7
        S_BANKS, P_BANKS = 3, 5
        xT_ps = ps[0:C, FRONT, 0:N]
        gmean_ps = ps[0:C, FRONT, N:N + 1]
        gvar_ps = ps[0:C, FRONT, N + 2:N + 3]
        qk_ps = ps[0:C, FRONT, 0:2 * N]
        v_ps = ps[:, FRONT, 0:NW * HP * HD].rearrange("p (w a d) -> p w a d", w=NW, d=HD)
        s_ps = ps[:, S_BANKS:S_BANKS + 2, 0:HP * T].rearrange("p b (h s) -> p b h s", s=T)
        pT_ps = ps[:, P_BANKS:P_BANKS + 2, 0:3 * TP]
        o_ps = ps[0:C, OUT_B, :]
        oT1_ps = ps[:, TAIL_A, 0:NP * NH * 16].rearrange("p (h d) -> p h d", d=16)
        oT2_ps = ps[0:C, TAIL_B, 0:N]
        y0_ps = ps[:, TAIL_A, 0:NP * C].rearrange("p (q c) -> p q c", q=NP)
        h1T_ps = ps[0:C, TAIL_B, 0:N]
        kv_ps = ps[:, TAIL_A, 0:NP * 2 * C].rearrange("p (q c) -> p q c", q=NP)
        attn_ps = ps[0:C, TAIL_B, 0:C]
        aproj_ps = ps[0:C, TAIL_A, 0:C]
        fold_ps = ps[0:C + 1, TAIL_B, 0:C]
        y1_ps = ps[:, TAIL_A, 0:NP * C].rearrange("p (q c) -> p q c", q=NP)
        h2T_ps = ps[0:C, TAIL_B, 0:N]
        gate_ps = ps[:, TAIL_A, 0:NP * NE].rearrange("p (q e) -> p q e", q=NP)
        up_ps = [ps[:, n, :] for n in range(4)]
        down_ps = [ps[0:C, 4 + n, :] for n in range(2)]
        final_ps = ps[:, 6, 0:FP * C].rearrange("p (q c) -> p q c", q=FP)
        mixT_ps = ps[:, 7, 0:256].rearrange("p (q c) -> p q c", q=2)

        weights_loaded = sem("weights_loaded")
        experts_loaded = sem("experts_loaded")
        x_loaded = [sem(f"x_loaded{u}") for u in range(2)]
        xres_loaded = [sem(f"xres_loaded{u}") for u in range(2)]
        mix_stored = sem("mix_stored")
        mix_loaded = [sem(f"mix_loaded{u}") for u in range(2)]
        out_stored = [sem(f"out_stored{u}") for u in range(2)]
        pool_const = sem("pool_const")
        zeros_set = sem("zeros_set")
        consts_ready = sem("consts_ready")
        setup_step = sem("setup_step")
        lam_sums = sem("lam_sums")
        lam_exps = sem("lam_exps")
        offs_sq_ready = sem("offs_sq_ready")
        gauss_ready = sem("gauss_ready")
        wq1T_ready = sem("wq1T_ready")
        lam_keep_ready = sem("lam_keep_ready")
        lam_col_ready = sem("lam_col_ready")
        lam_col_copied = sem("lam_col_copied")
        wq1T_copied = sem("wq1T_copied")
        xT_ready = sem("xT_ready")
        gn_stat_step = sem("gn_stat_step")
        gn_stats_ready = sem("gn_stats_ready")
        gmean_ready = sem("gmean_ready")
        gn_mean_ready = sem("gn_mean_ready")
        gn_dif_ready = sem("gn_dif_ready")
        spread_ready = sem("spread_ready")
        gvar_ready = sem("gvar_ready")
        gn_var_ready = sem("gn_var_ready")
        gn_rstd_ready = sem("gn_rstd_ready")
        xh_ready = sem("xh_ready")
        qk_ready = sem("qk_ready")
        qk_copied = sem("qk_copied")
        k_heads_ready = sem("k_heads_ready")
        v_ready = sem("v_ready")
        v_copied = sem("v_copied")
        scores_ready = sem("scores_ready")
        max_ready = sem("max_ready")
        shifted_ready = sem("shifted_ready")
        pT_ready = sem("pT_ready")
        probs_ready = sem("probs_ready")
        pv_done = sem("pv_done")
        o_copied = sem("o_copied")
        oT1_ready = sem("oT1_ready")
        o_rden_ready = sem("o_rden_ready")
        o_norm_ready = sem("o_norm_ready")
        oT2_ready = sem("oT2_ready")
        oT_copied = sem("oT_copied")
        y0_ready = sem("y0_ready")
        t1_ready = sem("t1_ready")
        ln1_bn_ready = sem("ln1_bn_ready")
        ln1_mv_ready = sem("ln1_mv_ready")
        ln1_var_ready = sem("ln1_var_ready")
        ln1_rstd_ready = sem("ln1_rstd_ready")
        h1_ready = sem("h1_ready")
        h1T_ready = sem("h1T_ready")
        h1T_copied = sem("h1T_copied")
        kv_ready = sem("kv_ready")
        kv_neg_ready = sem("kv_neg_ready")
        kv_exp_ready = sem("kv_exp_ready")
        feat_ready = sem("feat_ready")
        attn_ready = sem("attn_ready")
        attn_masked = sem("attn_masked")
        aproj_ready = sem("aproj_ready")
        aproj_copied = sem("aproj_copied")
        fold_ready = sem("fold_ready")
        fold_copied = sem("fold_copied")
        y1_ready = sem("y1_ready")
        t2_ready = sem("t2_ready")
        ln2_bn_ready = sem("ln2_bn_ready")
        ln2_mv_ready = sem("ln2_mv_ready")
        ln2_var_ready = sem("ln2_var_ready")
        ln2_rstd_ready = sem("ln2_rstd_ready")
        h2_ready = sem("h2_ready")
        h2T_ready = sem("h2T_ready")
        h2T_copied = sem("h2T_copied")
        h2T_kept = sem("h2T_kept")
        gate_ready = sem("gate_ready")
        gate_copied = sem("gate_copied")
        g_step = sem("g_step")
        g_shift_ready = sem("g_shift_ready")
        g_exp_ready = sem("g_exp_ready")
        g_mix_ready = sem("g_mix_ready")
        mixT_ready = sem("mixT_ready")
        mixT_copied = sem("mixT_copied")
        up_ready = sem("up_ready")
        gelu_ready = sem("gelu_ready")
        down_done = sem("down_done")
        scaled_step = sem("scaled_step")
        final_ready = sem("final_ready")
        out_ready = sem("out_ready")

        blk = ctx.enter_context(nc.Block())

        def nth(k, u):
            return 2 * k + u + 1

        def met(eng):
            eng.wait_ge(pool_const, 19)

        def before(k, u):
            return (k, 0) if u else (k - 1, 1)

        def is_first(t):
            return isinstance(t, int) and t == 0

        def schedule(eng, iteration):
            for i in range(2):
                iteration(0, i, True, True, i >= 1, False)
            with eng.Fori(1, B // 2 - 1) as k:
                for u in range(2):
                    iteration(k, u, True, True, True, True)
            for i in range(B - 2, B + 2):
                iteration(i // 2, i % 2, i + 1 < B, i < B, i - 1 < B, True)

        @blk.sync
        def _(sp):
            def load(dst, src, s):
                sp.dma_start(dst, src).then_inc(s, 16)

            def load_image(dst, k, u, s):
                for wc in range(2):
                    for wr in range(2):
                        src = x[bass.ds(2 * k + u, 1), wr * WS:(wr + 1) * WS, wc * WS:(wc + 1) * WS, :]
                        load(dst[wc * T:(wc + 1) * T, wr, :], src.rearrange("b i j c -> (b i) j c"), s)

            load_image(x_in[0], 0, 0, x_loaded[0])
            load(wqkv0[0:C, :], w0, weights_loaded)
            load(wqkv0[C:C + 1, :], b0.rearrange("(a n) -> a n", a=1), weights_loaded)
            load_image(x_in[1], 0, 1, x_loaded[1])
            load(wproj0[0:C, :], wp0, weights_loaded)
            load(wproj0[C:C + 1, :], bp0.rearrange("(a n) -> a n", a=1), weights_loaded)
            load(wqkv1[0:C, :], w1a, weights_loaded)
            load(wqkv1[C:C + 1, :], b1a.rearrange("(a n) -> a n", a=1), weights_loaded)
            load(wproj1[:, :], wp1, weights_loaded)
            for n, a in enumerate((lk1, lv1, lk2, lv2)):
                load(lam_in[:, n, :], a, weights_loaded)
            load(gate_w[0:C, :], gw, weights_loaded)
            load(gate_w[C:C + 1, :], gb.rearrange("(a n) -> a n", a=1), weights_loaded)
            sp.wait_ge(zeros_set, 3)
            load(bproj1[C:C + 1, :], bp1.rearrange("(a n) -> a n", a=1), weights_loaded)
            load_image(x_res[0], 0, 0, xres_loaded[0])
            load_image(x_res[1], 0, 1, xres_loaded[1])
            load(up_w[0:C, :, :], ew1.rearrange("e c n -> c e n"), experts_loaded)
            load(up_w[C:C + 1, :, :], eb1.rearrange("(a e) n -> a e n", a=1), experts_loaded)
            load(down_w[:, :, :, :].rearrange("p e c n -> p (e c) n"),
                 ew2.rearrange("e (c p) n -> p (e c) n", p=128), experts_loaded)
            sp.dma_start(down_b[:, :], eb2.rearrange("e n -> n e"), allow_slow_non_contiguous=True)\
                .then_inc(experts_loaded, 16)

            with sp.Fori(1, B // 2) as k:
                for u in range(2):
                    sp.wait_ge(xT_ready, nth(k, u) - 2)
                    load_image(x_in[u], k, u, x_loaded[u])
                    sp.wait_ge(t1_ready, nth(k, u) - 2)
                    load_image(x_res[u], k, u, xres_loaded[u])

            sp.wait_ge(mixT_copied, 1)
            mix_v = mix_dram.rearrange("(b t) e n -> (t e) b n", b=2)
            sp.dma_start(mix_v, mixT[:, :, :]).then_inc(mix_stored, 16)
            sp.wait_ge(mix_stored, 16)

            def load_mix(t, u):
                src = mix_dram[bass.ds(t * FP, FP), :, :].rearrange("(a t) e n -> a (t e n)", a=1)
                load(mix_rows[u][:, :, :, :].rearrange("p t e n -> p (t e n)"), src.broadcast_to([C, FP * NE * 128]),
                     mix_loaded[u])

            def store(k, u):
                sp.wait_ge(out_ready, nth(k, u))
                for im in range(2):
                    for wc in range(2):
                        for wr in range(2):
                            dst = out[bass.ds(2 * (2 * k + u) + im, 1), wr * WS:(wr + 1) * WS,
                                      wc * WS:(wc + 1) * WS, :]
                            sp.dma_start(dst.rearrange("b i j c -> (b i) j c"),
                                         out_sb[u][wc * T:(wc + 1) * T, im * NP + wr, :]).then_inc(out_stored[u], 16)

            load_mix(0, 0)
            load_mix(1, 1)
            for u in range(2):
                sp.wait_ge(scaled_step, 7 * (u + 1))
                load_mix(2 + u, u)
                store(0, u)
            with sp.Fori(1, NFT // 2 - 1) as k:
                for u in range(2):
                    sp.wait_ge(scaled_step, 7 * nth(k, u))
                    load_mix(2 * k + u + 2, u)
                    store(k, u)
            for u in range(2):
                store(NFT // 2 - 1, u)
            for u in range(2):
                sp.wait_ge(out_stored[u], 16 * 8 * (NFT // 2))

        @blk.gpsimd
        def _(pool):
            pool.memset(ident[:, :], 0.0).then_inc(pool_const, 1)
            pool.memset(group_mean[:, :], 1.0 / GC).then_inc(pool_const, 1)
            pool.memset(head_of[:, :], 1.0).then_inc(pool_const, 1)
            pool.memset(head_rows[:, :], 1.0).then_inc(pool_const, 1)
            pool.memset(block[:, :], 1.0).then_inc(pool_const, 1)
            pool.memset(lower[:, :, :], 1.0).then_inc(pool_const, 1)
            pool.iota(offsets[:, :], pattern=[[-1, C]], base=0, channel_multiplier=1).then_inc(pool_const, 1)
            pool.memset(minus_half[:, :], -0.5).then_inc(pool_const, 1)
            pool.memset(ln_eps[:, :], LN_EPS).then_inc(pool_const, 1)
            pool.wait_ge(pool_const, 9)

            def keep(t, view, pattern, base, mult, n):
                pool.affine_select(out=view, in_=view, compare_op=ALU.is_ge, fill=0.0, base=base,
                                   pattern=pattern, channel_multiplier=mult).then_inc(pool_const, 1)

            pool.affine_select(out=ident[:, :], in_=ident[:, :], compare_op=ALU.not_equal, fill=1.0, base=0,
                               pattern=[[-1, 128]], channel_multiplier=1).then_inc(pool_const, 1)
            groups = group_mean[:, :].rearrange("p (g c) -> p g c", c=GC)
            blocks = block[:, :].rearrange("p (h d) -> p h d", d=HD)
            keep(group_mean, groups, [[-GC, C // GC], [0, GC]], 0, 1, 0)
            keep(head_of, head_of[:, :], [[-HD, NH]], 0, 1, 0)
            keep(head_rows, head_rows[:, :], [[1, C]], 0, -HD, 0)
            keep(block, blocks, [[-HD, NH], [0, HD]], 0, 1, 0)
            keep(lower, lower[:, :, :], [[1, NE], [-1, NE]], -1, 0, 0)
            pool.wait_ge(pool_const, 15)
            keep(group_mean, groups, [[GC, C // GC], [0, GC]], GC - 1, -1, 0)
            keep(head_of, head_of[:, :], [[HD, NH]], HD - 1, -1, 0)
            keep(head_rows, head_rows[:, :], [[-1, C]], HD - 1, HD, 0)
            keep(block, blocks, [[HD, NH], [0, HD]], HD - 1, -1, 0)
            pool.wait_ge(pool_const, 19)
            pool.memset(xh[C:C + 1, :], 1.0).then_inc(consts_ready, 1)
            pool.memset(oT_sb[C:C + 1, :], 1.0).then_inc(consts_ready, 1)
            pool.memset(h1T[C:C + 1, :], 1.0).then_inc(consts_ready, 1)
            pool.memset(h2T[C:C + 1, :], 1.0).then_inc(consts_ready, 1)
            pool.memset(h2T_all[C:C + 1, :], 1.0).then_inc(consts_ready, 1)

            def gn_rstd_of(k, u):
                pool.wait_ge(gn_var_ready, nth(k, u))
                pool.tensor_tensor(gn_rstd[:, :], gn_var[:, :], minus_half[0:C, 0:1], ALU.pow).then_inc(gn_rstd_ready, 1)

            def ln_rstd(k, u, mv, var, rstd, mv_ready, var_ready, rstd_ready):
                pool.wait_ge(mv_ready, nth(k, u))
                pool.tensor_tensor(var[:, :], mv[:, :, 1], ln_eps[:, :], ALU.add).then_inc(var_ready, 1)
                pool.wait_ge(var_ready, nth(k, u))
                pool.tensor_tensor(rstd[:, :], var[:, :], minus_half[:, :], ALU.pow).then_inc(rstd_ready, 1)

            def iteration(k, u, front, attn, tail_a, tail_b):
                ka, ua = before(k, u)
                if tail_b:
                    ln_rstd(k - 1, u, ln2_mv, ln2_var, ln2_rstd, ln2_mv_ready, ln2_var_ready, ln2_rstd_ready)
                if front:
                    gn_rstd_of(*((k, 1) if u == 0 else (k + 1, 0)))
                if tail_b:
                    pool.wait_ge(h2T_copied, nth(k - 1, u))
                    pool.tensor_copy(h2T_all[0:C, bass.ds((2 * (k - 1) + u) * N, N)],
                                     h2T[0:C, :]).then_inc(h2T_kept, 1)
                if tail_a:
                    ln_rstd(ka, ua, ln1_mv, ln1_var, ln1_rstd, ln1_mv_ready, ln1_var_ready, ln1_rstd_ready)

            gn_rstd_of(0, 0)
            schedule(pool, iteration)

        @blk.tensor
        def _(pe):
            def xT(k, u):
                pe.wait_ge(x_loaded[u], 16 * 4 * (k + 1))
                pe.wait_ge(v_copied, nth(k, u) - 1)
                for p in range(NP):
                    last = pe.transpose(xT_ps[:, p * TP:(p + 1) * TP], x_in[u][:, p, :], ident[:, :])
                last.then_inc(xT_ready, 1)

            def gmean(k, u):
                pe.wait_ge(gn_stats_ready, nth(k, u))
                pe.matmul(gmean_ps, group_mean[:, :], gn_mv[:, 0:1], start=True, stop=True).then_inc(gmean_ready, 1)

            def gvar(k, u):
                pe.wait_ge(spread_ready, nth(k, u))
                pe.matmul(gvar_ps, group_mean[:, :], gn_spread[:, :], start=True, stop=True).then_inc(gvar_ready, 1)

            def qk_proj(k, u):
                pe.wait_ge(xh_ready, nth(k, u))
                for n in range(2):
                    last = pe.matmul(qk_ps[:, n * N:(n + 1) * N], wqkv0[:, n * C:(n + 1) * C], xh[:, :],
                                     start=True, stop=True)
                last.then_inc(qk_ready, 1)

            def v_proj(k, u):
                pe.wait_ge(qk_copied, nth(k, u))
                wv = wqkv0[:, 2 * C:3 * C].rearrange("p (a b d) -> p a b d", b=2, d=HD)
                for w in range(NW):
                    for odd in range(2):
                        last = pe.matmul(v_ps[odd * T:(odd + 1) * T, w, :, :], xh[:, w * T:(w + 1) * T],
                                         wv[:, :, odd, :], start=True, stop=True)
                last.then_inc(v_ready, 1)

            def s_piece(k, u, p, n):
                w2, half = n // 2, n % 2
                if n == 0:
                    pe.wait_ge(k_heads_ready, nth(k, u))
                    pe.wait_ge(shifted_ready, 2 * (2 * k + u) + p)
                w = 2 * p + w2
                mm = pe.matmul(s_ps[w2 * T:(w2 + 1) * T, half, :, :], qk[u][:, 0, w * T:(w + 1) * T],
                               k_heads[u][:, half * HP:(half + 1) * HP, w * T:(w + 1) * T], start=True, stop=True)
                if n == 3:
                    mm.then_inc(scores_ready, 1)

            def p_transpose(k, u, p):
                done = 2 * (2 * k + u) + p
                pe.wait_ge(shifted_ready, done + 1)
                pe.wait_ge(probs_ready, done)
                for hp in range(HP):
                    last = pe.transpose(pT_ps[:, hp // 3, (hp % 3) * TP:(hp % 3 + 1) * TP],
                                        shifted[p][:, 2 * hp:2 * hp + 2, :], ident[:, :])
                last.then_inc(pT_ready, 1)

            def pv(k, u, p, w2):
                if w2 == 0:
                    pe.wait_ge(probs_ready, 2 * (2 * k + u) + p + 1)
                    pe.wait_ge(v_copied, nth(k, u))
                    if p == 0:
                        pe.wait_ge(o_copied, nth(k, u) - 1)
                w = 2 * p + w2
                for hp in range(HP):
                    g, r = hp % 3, hp // 3
                    last = pe.matmul(o_ps[g * VW:(g + 1) * VW, r * N + w * T:r * N + (w + 1) * T],
                                     v_heads[u][:, w, hp, :], probs[p][:, hp, w2 * T:(w2 + 1) * T],
                                     start=True, stop=True)
                if w2 == 1:
                    last.then_inc(pv_done, 1)

            def oT1(k, u):
                pe.wait_ge(o_copied, nth(k, u))
                pe.wait_ge(gate_copied, nth(k, u) - 1)
                for p in range(NP):
                    for r in range(2):
                        last = pe.transpose(ps[:, TAIL_A, (2 * p + r) * C:(2 * p + r + 1) * C],
                                            o_sb[:, r * N + p * TP:r * N + (p + 1) * TP], ident[0:C, 0:C])
                last.then_inc(oT1_ready, 1)

            def oT2(k, u):
                pe.wait_ge(o_norm_ready, nth(k, u))
                for p in range(NP):
                    last = pe.transpose(oT2_ps[:, p * TP:(p + 1) * TP],
                                        o_norm[:, p * NH:(p + 1) * NH, :].rearrange("p h d -> p (h d)"), ident[:, :])
                last.then_inc(oT2_ready, 1)

            def per_pair(psum, lhs, rhs, done):
                for p in range(NP):
                    last = pe.matmul(psum[:, p, :], lhs[:, p * TP:(p + 1) * TP], rhs, start=True, stop=True)
                last.then_inc(done, 1)

            def y0(k, u):
                pe.wait_ge(oT_copied, nth(k, u))
                per_pair(y0_ps, oT_sb, wproj0[:, :], y0_ready)

            def h1T_of(k, u):
                pe.wait_ge(h1_ready, nth(k, u))
                for p in range(NP):
                    last = pe.transpose(h1T_ps[:, p * TP:(p + 1) * TP], h1[:, p, :], ident[:, :])
                last.then_inc(h1T_ready, 1)

            def kv(k, u):
                pe.wait_ge(h1T_copied, nth(k, u))
                per_pair(kv_ps, h1T, wqkv1[:, C:3 * C], kv_ready)

            def attn_sum(k, u):
                pe.wait_ge(feat_ready, nth(k, u))
                for p in range(NP):
                    last = pe.matmul(attn_ps, feat[:, p, C:2 * C], feat[:, p, 0:C], start=p == 0, stop=p == NP - 1)
                last.then_inc(attn_ready, 1)

            def attn_times_proj(k, u):
                pe.wait_ge(attn_masked, nth(k, u))
                pe.matmul(aproj_ps, attn_sb[:, :], wproj1[:, :], start=True, stop=True).then_inc(aproj_ready, 1)

            def fold(k, u):
                pe.wait_ge(aproj_copied, nth(k, u))
                pe.matmul(fold_ps, wq1T[:, :], attn_proj[:, :], start=True, stop=True).then_inc(fold_ready, 1)

            def y1(k, u):
                pe.wait_ge(fold_copied, nth(k, u))
                per_pair(y1_ps, h1T, fold_w[:, :], y1_ready)

            def h2T_of(k, u):
                pe.wait_ge(h2_ready, nth(k, u))
                for p in range(NP):
                    last = pe.transpose(h2T_ps[:, p * TP:(p + 1) * TP], h2[:, p, :], ident[:, :])
                last.then_inc(h2T_ready, 1)

            def gate(k, u):
                pe.wait_ge(h2T_copied, nth(k, u))
                per_pair(gate_ps, h2T, gate_w[:, :], gate_ready)

            def iteration(k, u, front, attn, tail_a, tail_b):
                kf, uf = (k, 1) if u == 0 else (k + 1, 0)
                ka, ua = before(k, u)
                kb, ub = k - 1, u

                if attn:
                    s_piece(k, u, 0, 0)
                if front:
                    xT(kf, uf)
                if attn:
                    s_piece(k, u, 0, 1)
                if tail_b:
                    attn_sum(kb, ub)
                if attn:
                    s_piece(k, u, 0, 2)
                if tail_b:
                    attn_times_proj(kb, ub)
                if attn:
                    s_piece(k, u, 0, 3)
                if front:
                    gmean(kf, uf)
                if tail_b:
                    fold(kb, ub)
                if tail_a:
                    p_transpose(ka, ua, 1)
                if tail_b:
                    y1(kb, ub)
                if front:
                    gvar(kf, uf)
                if tail_a:
                    pv(ka, ua, 1, 0)
                    pv(ka, ua, 1, 1)
                if attn:
                    s_piece(k, u, 1, 0)
                if tail_b:
                    h2T_of(kb, ub)
                if front:
                    qk_proj(kf, uf)
                if attn:
                    s_piece(k, u, 1, 1)
                if tail_b:
                    gate(kb, ub)
                if attn:
                    s_piece(k, u, 1, 2)
                if tail_a:
                    oT1(ka, ua)
                if attn:
                    s_piece(k, u, 1, 3)
                if tail_a:
                    oT2(ka, ua)
                if attn:
                    p_transpose(k, u, 0)
                if front:
                    v_proj(kf, uf)
                if tail_a:
                    y0(ka, ua)
                if attn:
                    pv(k, u, 0, 0)
                if tail_a:
                    h1T_of(ka, ua)
                if attn:
                    pv(k, u, 0, 1)
                if tail_a:
                    kv(ka, ua)

            pe.wait_ge(pool_const, 19)
            xT(0, 0)
            gmean(0, 0)
            gvar(0, 0)
            pe.wait_ge(weights_loaded, 16 * 14)
            pe.wait_ge(consts_ready, 5)
            pe.transpose(ps[0:C, TAIL_A, 0:C + 1], wqkv1[:, 0:C], ident[0:C + 1, 0:C + 1]).then_inc(wq1T_ready, 1)
            qk_proj(0, 0)
            pe.wait_ge(lam_keep_ready, 1)
            pe.matmul(ps[0:C, TAIL_B, 0:1], head_rows[:, :], lam_keep[:, :], start=True, stop=True)\
                .then_inc(lam_col_ready, 1)
            v_proj(0, 0)
            pe.wait_ge(wq1T_copied, 1)
            pe.wait_ge(lam_col_copied, 1)
            schedule(pe, iteration)

            def up(t, n):
                e, c = n // CH, n % CH
                if n >= 4 or not is_first(t):
                    pe.wait_ge(gelu_ready, t * NE * CH + n - 3)
                pe.matmul(up_ps[n % 4], up_w[:, e, c * 128:(c + 1) * 128], h2T_all[:, bass.ds(t * FT, FT)],
                          start=True, stop=True).then_inc(up_ready, 1)

            def down(t, n):
                e, c = n // CH, n % CH
                pe.wait_ge(gelu_ready, t * NE * CH + n + 1)
                if c == 0 and (e >= 2 or not is_first(t)):
                    step = (1, 2, 4, 6)[(e + 2) % 4]
                    pe.wait_ge(scaled_step, 7 * t + step - (7 if e < 2 else 0))
                pe.matmul(down_ps[e % 2], down_w[:, e, c, :], hidden[n % 4][:, :], start=c == 0, stop=c == CH - 1)\
                    .then_inc(down_done, 1)

            def final(t, u):
                pe.wait_ge(scaled_step, 7 * (t + 1))
                if not is_first(t):
                    pe.wait_ge(out_ready, t)
                for p in range(FP):
                    last = pe.transpose(final_ps[:, p, :], y_acc[u][:, p * TP:(p + 1) * TP], ident[0:C, 0:C])
                last.then_inc(final_ready, 1)

            def mix_transpose():
                pe.wait_ge(g_mix_ready, 1)
                for b in range(2):
                    last = pe.transpose(mixT_ps[:, b, :], g_mix[:, b * 128:(b + 1) * 128], ident[:, :])
                last.then_inc(mixT_ready, 1)

            def tile(t, u, first):
                for n in range(NE * CH):
                    up(t, n)
                    if n >= 2:
                        down(t, n - 2)
                    if n == 5 and first:
                        mix_transpose()
                    elif n == 5:
                        final(t - 1, 1 - u)
                down(t, NE * CH - 2)
                down(t, NE * CH - 1)

            pe.wait_ge(experts_loaded, 16 * 4)
            pe.wait_ge(h2T_kept, B)
            pe.wait_ge(gate_copied, B)
            tile(0, 0, True)
            tile(1, 1, False)
            with pe.Fori(1, NFT // 2) as k:
                for u in range(2):
                    tile(2 * k + u, u, False)
            final(NFT - 1, 1)

        @blk.scalar
        def _(act):
            def copy_qk(k, u):
                act.wait_ge(qk_ready, nth(k, u))
                if not is_first(k):
                    act.wait_ge(scores_ready, 2 * nth(k, u) - 4)
                act.activation(qk[u][:, :, :], qk_ps.rearrange("p (a n) -> p a n", a=2), ACT.Copy).then_inc(qk_copied, 1)

            def copy_v(k, u):
                act.wait_ge(v_ready, nth(k, u))
                if not is_first(k):
                    act.wait_ge(pv_done, 2 * nth(k, u) - 4)
                for odd in range(2):
                    last = act.activation(v_heads[u][odd * T:(odd + 1) * T, :, :, odd * 16:odd * 16 + HD],
                                          v_ps[odd * T:(odd + 1) * T, :, :, :], ACT.Copy)
                last.then_inc(v_copied, 1)

            def exp_probs(k, u, p):
                done = 2 * (2 * k + u) + p
                act.wait_ge(pT_ready, done + 1)
                if not (is_first(k) and u == 0):
                    act.wait_ge(pv_done, done - 1)
                act.activation(probs[p][:, :, :].rearrange("p (b h) t -> p b (h t)", b=2), pT_ps, ACT.Exp,
                               scale=SCALE).then_inc(probs_ready, 1)

            def copy_o(k, u):
                act.wait_ge(pv_done, 2 * nth(k, u))
                act.wait_ge(oT1_ready, nth(k, u) - 1)
                act.activation(o_sb[:, :], o_ps, ACT.Copy).then_inc(o_copied, 1)

            def copy_oT(k, u):
                act.wait_ge(oT2_ready, nth(k, u))
                act.wait_ge(y0_ready, nth(k, u) - 1)
                act.activation(oT_sb[0:C, :], oT2_ps, ACT.Copy).then_inc(oT_copied, 1)

            def copy_h1T(k, u):
                act.wait_ge(h1T_ready, nth(k, u))
                act.wait_ge(y1_ready, nth(k, u) - 1)
                act.activation(h1T[0:C, :], h1T_ps, ACT.Copy).then_inc(h1T_copied, 1)

            def exp_kv(k, u):
                act.wait_ge(kv_neg_ready, nth(k, u))
                act.wait_ge(feat_ready, nth(k, u) - 1)
                act.activation(kv_exp[:, :, :], kv_neg[:, :, :], ACT.Exp).then_inc(kv_exp_ready, 1)

            def copy_aproj(k, u):
                act.wait_ge(aproj_ready, nth(k, u))
                act.wait_ge(fold_ready, nth(k, u) - 1)
                act.activation(attn_proj[:, :], aproj_ps, ACT.Copy).then_inc(aproj_copied, 1)

            def copy_h2T(k, u):
                act.wait_ge(h2T_ready, nth(k, u))
                act.wait_ge(gate_ready, nth(k, u) - 1)
                act.wait_ge(h2T_kept, nth(k, u) - 1)
                act.activation(h2T[0:C, :], h2T_ps, ACT.Copy).then_inc(h2T_copied, 1)

            def iteration(k, u, front, attn, tail_a, tail_b):
                kf, uf = (k, 1) if u == 0 else (k + 1, 0)
                ka, ua = before(k, u)
                kb, ub = k - 1, u
                if tail_b:
                    copy_aproj(kb, ub)
                if tail_a:
                    exp_probs(ka, ua, 1)
                    copy_o(ka, ua)
                if tail_b:
                    copy_h2T(kb, ub)
                if front:
                    copy_qk(kf, uf)
                if tail_a:
                    copy_oT(ka, ua)
                if attn:
                    exp_probs(k, u, 0)
                if front:
                    copy_v(kf, uf)
                if tail_a:
                    copy_h1T(ka, ua)
                    exp_kv(ka, ua)

            act.wait_ge(lam_sums, 1)
            act.activation(lam_exp[:, :], lam_sum[:, :], ACT.Exp).then_inc(lam_exps, 1)
            act.wait_ge(offs_sq_ready, 1)
            act.activation(gauss[:, :], offsets_sq[:, :], ACT.Exp, scale=-2.0).then_inc(gauss_ready, 1)
            act.wait_ge(wq1T_ready, 1)
            act.activation(wq1T[:, :], ps[0:C, TAIL_A, 0:C + 1], ACT.Copy, scale=SCALE).then_inc(wq1T_copied, 1)
            act.wait_ge(zeros_set, 3)
            copy_qk(0, 0)
            copy_v(0, 0)
            schedule(act, iteration)

            act.wait_ge(g_shift_ready, 1)
            act.activation(g_exp[:, :, :], g_shift[:, :, :], ACT.Exp).then_inc(g_exp_ready, 1)

            def gelus(t):
                for n in range(NE * CH):
                    act.wait_ge(up_ready, t * NE * CH + n + 1)
                    if n >= 4 or not is_first(t):
                        act.wait_ge(down_done, t * NE * CH + n - 3)
                    act.activation(hidden[n % 4][:, :], up_ps[n % 4], ACT.Gelu).then_inc(gelu_ready, 1)

            gelus(0)
            with act.Fori(1, NFT) as t:
                gelus(t)

        @blk.vector
        def _(dve):
            def gn_stats_of(k, u):
                dve.wait_ge(xT_ready, nth(k, u))
                dve.bn_stats(gn_stats[:, :], xT_ps).then_inc(gn_stat_step, 1)
                met(dve)
                dve.wait_ge(gn_stat_step, nth(k, u))
                dve.bn_aggr(gn_mv[:, :], gn_stats[:, :]).then_inc(gn_stats_ready, 1)

            def gn_spread_of(k, u):
                dve.wait_ge(gmean_ready, nth(k, u))
                dve.tensor_copy(gn_mean[:, :], gmean_ps).then_inc(gn_mean_ready, 1)
                dve.wait_ge(gn_mean_ready, nth(k, u))
                dve.tensor_tensor(gn_dif[:, :], gn_mv[:, 0:1], gn_mean[:, :], ALU.subtract).then_inc(gn_dif_ready, 1)
                dve.wait_ge(gn_dif_ready, nth(k, u))
                dve.scalar_tensor_tensor(gn_spread[:, :], gn_dif[:, :], gn_dif[:, 0:1], gn_mv[:, 1:2],
                                         ALU.mult, ALU.add).then_inc(spread_ready, 1)

            def gn_var_of(k, u):
                dve.wait_ge(gvar_ready, nth(k, u))
                dve.tensor_scalar(gn_var[:, :], gvar_ps, GN_EPS, None, ALU.add).then_inc(gn_var_ready, 1)

            def gn_apply(k, u):
                dve.wait_ge(gn_rstd_ready, nth(k, u))
                dve.wait_ge(v_ready, nth(k, u) - 1)
                dve.tensor_scalar(xh[0:C, :], xT_ps, gn_mean[:, 0:1], gn_rstd[:, 0:1], ALU.subtract, ALU.mult)\
                    .then_inc(xh_ready, 1)

            def split_heads(k, u):
                dve.wait_ge(qk_copied, nth(k, u))
                if not is_first(k):
                    dve.wait_ge(scores_ready, 2 * nth(k, u) - 4)
                for h in range(NH):
                    last = dve.tensor_scalar(k_heads[u][:, h, :], qk[u][:, 1, :], head_of[:, h:h + 1], None, ALU.mult)
                last.then_inc(k_heads_ready, 1)

            def shift(k, u, p):
                done = 2 * (2 * k + u) + p
                dve.wait_ge(scores_ready, done + 1)
                dve.tensor_reduce(score_max[:, :].rearrange("p (b h) -> p b h", b=2), s_ps, AX.X, ALU.max)\
                    .then_inc(max_ready, 1)
                dve.wait_ge(max_ready, done + 1)
                if not (is_first(k) and u == 0):
                    dve.wait_ge(pT_ready, done - 1)
                dve.tensor_tensor(shifted[p][:, :, :].rearrange("p (b h) s -> p b h s", b=2), s_ps,
                                  score_max[:, :].rearrange("p (b h) -> p b h", b=2).unsqueeze(3)
                                  .broadcast_to([128, 2, HP, T]), ALU.subtract).then_inc(shifted_ready, 1)

            def normalise(k, u):
                dve.wait_ge(oT1_ready, nth(k, u))
                dve.reciprocal(o_rden[:, :], oT1_ps[:, :, HD]).then_inc(o_rden_ready, 1)
                dve.wait_ge(o_rden_ready, nth(k, u))
                dve.wait_ge(oT2_ready, nth(k, u) - 1)
                dve.tensor_tensor(o_norm[:, :, :], oT1_ps[:, :, 0:HD],
                                  o_rden[:, :].unsqueeze(2).broadcast_to([128, NP * NH, HD]), ALU.mult)\
                    .then_inc(o_norm_ready, 1)

            def residual1(k, u):
                dve.wait_ge(y0_ready, nth(k, u))
                dve.wait_ge(xres_loaded[u], 16 * 4 * (k + 1))
                dve.tensor_tensor(t1[u][:, :, :], y0_ps, x_res[u][:, :, :], ALU.add).then_inc(t1_ready, 1)
                dve.wait_ge(t1_ready, nth(k, u))
                for p in range(NP):
                    last = dve.bn_stats(ln1_stats[:, p, :], t1[u][:, p, :])
                last.then_inc(ln1_bn_ready, 1)
                met(dve)
                dve.wait_ge(ln1_bn_ready, nth(k, u))
                for p in range(NP):
                    last = dve.bn_aggr(ln1_mv[:, p, :], ln1_stats[:, p, :])
                last.then_inc(ln1_mv_ready, 1)

            def norm1(k, u):
                dve.wait_ge(ln1_rstd_ready, nth(k, u))
                dve.wait_ge(h1T_ready, nth(k, u) - 1)
                for p in range(NP):
                    last = dve.tensor_scalar(h1[:, p, :], t1[u][:, p, :], ln1_mv[:, p, 0:1], ln1_rstd[:, p:p + 1],
                                             ALU.subtract, ALU.mult)
                last.then_inc(h1_ready, 1)

            def kv_negative(k, u):
                dve.wait_ge(kv_ready, nth(k, u))
                dve.wait_ge(kv_exp_ready, nth(k, u) - 1)
                dve.tensor_scalar(kv_neg[:, :, :], kv_ps, 0.0, None, ALU.min).then_inc(kv_neg_ready, 1)

            def features(k, u):
                dve.wait_ge(kv_exp_ready, nth(k, u))
                dve.wait_ge(attn_ready, nth(k, u) - 1)
                dve.scalar_tensor_tensor(feat[:, :, :], kv_ps, 0.0, kv_exp[:, :, :], ALU.max, ALU.add)\
                    .then_inc(feat_ready, 1)

            def mask_attn(k, u):
                dve.wait_ge(attn_ready, nth(k, u))
                dve.wait_ge(aproj_ready, nth(k, u) - 1)
                dve.tensor_tensor(attn_sb[:, :], attn_ps, attn_mask[:, :], ALU.mult).then_inc(attn_masked, 1)

            def copy_fold(k, u):
                dve.wait_ge(fold_ready, nth(k, u))
                dve.wait_ge(y1_ready, nth(k, u) - 1)
                dve.tensor_tensor(fold_w[:, :], fold_ps, bproj1[:, :], ALU.add).then_inc(fold_copied, 1)

            def residual2(k, u):
                pair = (2 * k + u) * NP
                dve.wait_ge(y1_ready, nth(k, u))
                dve.tensor_tensor(t2_all[:, bass.ds(pair, NP), :], y1_ps, t1[u][:, :, :], ALU.add).then_inc(t2_ready, 1)
                met(dve)
                dve.wait_ge(t2_ready, nth(k, u))
                for p in range(NP):
                    last = dve.bn_stats(ln2_stats[:, p, :], t2_all[:, bass.ds(pair + p, 1), :].rearrange("p a c -> p (a c)"))
                last.then_inc(ln2_bn_ready, 1)
                met(dve)
                dve.wait_ge(ln2_bn_ready, nth(k, u))
                for p in range(NP):
                    last = dve.bn_aggr(ln2_mv[:, p, :], ln2_stats[:, p, :])
                last.then_inc(ln2_mv_ready, 1)

            def norm2(k, u):
                pair = (2 * k + u) * NP
                dve.wait_ge(ln2_rstd_ready, nth(k, u))
                dve.wait_ge(h2T_ready, nth(k, u) - 1)
                for p in range(NP):
                    last = dve.tensor_scalar(h2[:, p, :],
                                             t2_all[:, bass.ds(pair + p, 1), :].rearrange("p a c -> p (a c)"),
                                             ln2_mv[:, p, 0:1], ln2_rstd[:, p:p + 1], ALU.subtract, ALU.mult)
                last.then_inc(h2_ready, 1)

            def copy_gate(k, u):
                dve.wait_ge(gate_ready, nth(k, u))
                dve.tensor_copy(scores[:, bass.ds((2 * k + u) * NP, NP), :], gate_ps).then_inc(gate_copied, 1)

            def iteration(k, u, front, attn, tail_a, tail_b):
                kf, uf = (k, 1) if u == 0 else (k + 1, 0)
                ka, ua = before(k, u)
                kb, ub = k - 1, u
                if front:
                    gn_stats_of(kf, uf)
                if tail_b:
                    mask_attn(kb, ub)
                if front:
                    gn_spread_of(kf, uf)
                if tail_b:
                    copy_fold(kb, ub)
                if attn:
                    shift(k, u, 0)
                if front:
                    gn_var_of(kf, uf)
                if tail_b:
                    residual2(kb, ub)
                if front:
                    gn_apply(kf, uf)
                if tail_b:
                    norm2(kb, ub)
                if front:
                    split_heads(kf, uf)
                if tail_b:
                    copy_gate(kb, ub)
                if tail_a:
                    normalise(ka, ua)
                if attn:
                    shift(k, u, 1)
                if tail_a:
                    residual1(ka, ua)
                    norm1(ka, ua)
                    kv_negative(ka, ua)
                    features(ka, ua)

            for u in range(2):
                dve.memset(v_heads[u][:, :, :, :], 0.0).then_inc(setup_step, 1)
            dve.memset(bproj1[:, :], 0.0).then_inc(zeros_set, 1)
            dve.wait_ge(setup_step, 2)
            for u in range(2):
                for odd in range(2):
                    last = dve.memset(v_heads[u][odd * T:(odd + 1) * T, :, :, odd * 16 + HD:odd * 16 + HD + 1], 1.0)
                last.then_inc(zeros_set, 1)
            dve.wait_ge(pool_const, 19)
            gn_stats_of(0, 0)
            gn_spread_of(0, 0)
            gn_var_of(0, 0)
            dve.wait_ge(consts_ready, 5)
            gn_apply(0, 0)
            dve.tensor_copy(offsets_f[:, :], offsets[:, :]).then_inc(setup_step, 1)
            dve.wait_ge(setup_step, 3)
            dve.tensor_tensor(offsets_sq[:, :], offsets_f[:, :], offsets_f[:, :], ALU.mult).then_inc(offs_sq_ready, 1)
            dve.wait_ge(weights_loaded, 16 * 14)
            dve.tensor_tensor(lam_prod[:, :, :], lam_in[:, 0:4:2, :], lam_in[:, 1:4:2, :], ALU.mult)\
                .then_inc(setup_step, 1)
            dve.wait_ge(setup_step, 4)
            dve.tensor_reduce(lam_sum[:, :], lam_prod[:, :, :], AX.X, ALU.add).then_inc(lam_sums, 1)
            dve.wait_ge(lam_exps, 1)
            dve.tensor_tensor(lam_dif[:, :], lam_exp[:, 1:2], lam_exp[:, 0:1], ALU.subtract).then_inc(setup_step, 1)
            dve.wait_ge(setup_step, 5)
            dve.tensor_scalar(lam_keep[:, :], lam_dif[:, :], 1.0 - LAMBDA_INIT, None, ALU.add)\
                .then_inc(lam_keep_ready, 1)
            dve.wait_ge(lam_col_ready, 1)
            dve.tensor_copy(lam_col[:, :], ps[0:C, TAIL_B, 0:1]).then_inc(lam_col_copied, 1)
            dve.wait_ge(lam_col_copied, 1)
            dve.wait_ge(gauss_ready, 1)
            dve.scalar_tensor_tensor(attn_mask[:, :], gauss[:, :], lam_col[:, 0:1], block[:, :], ALU.mult, ALU.mult)\
                .then_inc(setup_step, 1)
            dve.wait_ge(setup_step, 6)
            split_heads(0, 0)
            schedule(dve, iteration)

            steps = [0]

            def link(ins):
                steps[0] += 1
                ins.then_inc(g_step, 1)
                dve.wait_ge(g_step, steps[0])

            def over_experts(v):
                return v.unsqueeze(2).broadcast_to([128, NPA, NE])

            dve.wait_ge(gate_copied, B)
            link(dve.tensor_reduce(g_max[:, :], scores[:, :, :], AX.X, ALU.max))
            dve.tensor_tensor(g_shift[:, :, :], scores[:, :, :], over_experts(g_max[:, :]), ALU.subtract)\
                .then_inc(g_shift_ready, 1)
            dve.wait_ge(g_exp_ready, 1)
            link(dve.tensor_reduce(g_sum[:, :], g_exp[:, :, :], AX.X, ALU.add))
            link(dve.reciprocal(g_rsum[:, :], g_sum[:, :]))
            link(dve.tensor_tensor(g_prob[:, :, :], g_exp[:, :, :], over_experts(g_rsum[:, :]), ALU.mult))
            others = g_prob[:, :, :].unsqueeze(2).broadcast_to([128, NPA, NE, NE])
            own = g_prob[:, :, :].unsqueeze(3).broadcast_to([128, NPA, NE, NE])
            link(dve.tensor_tensor(g_above[:, :, :, :], others, own, ALU.is_gt))
            link(dve.tensor_tensor(g_equal[:, :, :, :], others, own, ALU.is_equal))
            ge = g_equal[:, :, :, :].rearrange("p n a b -> p n (a b)")
            ga = g_above[:, :, :, :].rearrange("p n a b -> p n (a b)")
            low = lower[:, :, :].rearrange("p a b -> p (a b)").unsqueeze(1).broadcast_to([128, NPA, NE * NE])
            link(dve.tensor_tensor(ge, ge, low, ALU.mult))
            link(dve.tensor_tensor(ga, ga, ge, ALU.add))
            link(dve.tensor_reduce(g_rank[:, :], g_above[:, :, :, :].rearrange("p n a b -> p (n a) b"), AX.X, ALU.add))
            probs_flat = g_prob[:, :, :].rearrange("p n e -> p (n e)")
            link(dve.scalar_tensor_tensor(g_mix[:, :], g_rank[:, :], 1.5, probs_flat, ALU.is_lt, ALU.mult))
            mix3 = g_mix[:, :].rearrange("p (n e) -> p n e", e=NE)
            link(dve.tensor_reduce(g_sum[:, :], mix3, AX.X, ALU.add))
            link(dve.tensor_scalar(g_sum[:, :], g_sum[:, :], 1e-9, None, ALU.add))
            link(dve.reciprocal(g_rsum[:, :], g_sum[:, :]))
            dve.tensor_tensor(mix3, mix3, over_experts(g_rsum[:, :]), ALU.mult).then_inc(g_mix_ready, 1)
            dve.wait_ge(mixT_ready, 1)
            dve.tensor_copy(mixT[:, :, :], mixT_ps).then_inc(mixT_copied, 1)

            dve.wait_ge(experts_loaded, 16 * 4)

            def mix_tile(t, k, u):
                acc = y_acc[u][:, :].rearrange("p (t n) -> p t n", n=TP)
                scaled = y_scaled[:, :].rearrange("p (t n) -> p t n", n=TP)
                dve.wait_ge(mix_loaded[u], 16 * (k + 1))
                step = 0
                for e in range(NE):
                    dve.wait_ge(down_done, (t * NE + e + 1) * CH)
                    if e == 0 and (not isinstance(t, int) or t >= 2):
                        dve.wait_ge(final_ready, t - 1)
                    dve.scalar_tensor_tensor(acc if e == 0 else scaled,
                                             down_ps[e % 2].rearrange("p (t n) -> p t n", n=TP), down_b[:, e:e + 1],
                                             mix_rows[u][:, :, e, :], ALU.add, ALU.mult).then_inc(scaled_step, 1)
                    step += 1
                    if e:
                        dve.wait_ge(scaled_step, 7 * t + step)
                        dve.tensor_tensor(acc, acc, scaled, ALU.add).then_inc(scaled_step, 1)
                        step += 1
                        dve.wait_ge(scaled_step, 7 * t + step)

            def finish_tile(t, k, u):
                dve.wait_ge(final_ready, t + 1)
                if not isinstance(t, int) or t >= 2:
                    dve.wait_ge(out_stored[u], 16 * 8 * k)
                dve.tensor_tensor(out_sb[u][:, :, :], final_ps, t2_all[:, bass.ds(t * FP, FP), :], ALU.add)\
                    .then_inc(out_ready, 1)

            mix_tile(0, 0, 0)
            finish_tile(0, 0, 0)
            mix_tile(1, 0, 1)
            with dve.Fori(1, NFT // 2) as k:
                finish_tile(2 * k - 1, k - 1, 1)
                mix_tile(2 * k, k, 0)
                finish_tile(2 * k, k, 0)
                mix_tile(2 * k + 1, k, 1)
            finish_tile(NFT - 1, NFT // 2 - 1, 1)


_INS = ['x', 'L0_conv_w_qkv', 'L0_conv_b_qkv', 'L0_conv_w_proj', 'L0_conv_b_proj', 'L1_attn_qkv_w', 'L1_attn_qkv_b',
        'L1_attn_proj_w', 'L1_attn_proj_b', 'L1_attn_lambda_k1', 'L1_attn_lambda_v1', 'L1_attn_lambda_k2',
        'L1_attn_lambda_v2', 'L1_ffn_gate_w', 'L1_ffn_gate_b', 'L1_ffn_w1', 'L1_ffn_b1', 'L1_ffn_w2', 'L1_ffn_b2']
_OUT = ((B, HI, WI, C), 'float32')


def kernel(**inputs):
    import concourse.bacc as bacc
    from concourse.bass_utils import run_bass_kernel_spmd

    nc = bacc.Bacc("TRN2", target_bir_lowering=False, num_devices=1)
    arrays, args = {}, []
    for name in _INS:
        a = np.ascontiguousarray(inputs[name])
        arrays[f"in_{name}"] = a
        args.append(nc.dram_tensor(f"in_{name}", a.shape, mybir.dt.from_np(a.dtype), kind="ExternalInput").ap())
    args.append(nc.dram_tensor("out_0", _OUT[0], mybir.dt.from_np(np.dtype(_OUT[1])), kind="ExternalOutput").ap())
    build(nc, *args)
    r = run_bass_kernel_spmd(nc, [arrays], core_ids=[0])
    return r.results[0]["out_0"]
```

```python
from contextlib import ExitStack
import math

import numpy as np
import concourse.bass as bass
from concourse import mybir

F32 = mybir.dt.float32
F32R = mybir.dt.float32r
I32 = mybir.dt.int32
BF16 = mybir.dt.bfloat16
ALU = mybir.AluOpType
ACT = mybir.ActivationFunctionType
AX = mybir.AxisListType

B, HI, WI, C = 32, 16, 16, 96
WS = 8
NH, HD = 12, 8
T = WS * WS
TP = 2 * T
IM = 2
NB = B // IM
NI = HI * WI // TP
NP = IM * NI
N = IM * HI * WI
NIT = HI * WI
NW = N // T
NWI = NIT // T
HP = NH // 2
PARTS = 3
SLOTS = 6
KROWS = 2 * SLOTS * HD
MROWS = 2 * NH
GC = C // 32
SCALE = HD ** -0.5
LAMBDA_INIT = 0.8 - 0.6 * math.exp(-0.3)
GN_EPS, LN_EPS = 1e-5, 1e-5
NE, HID = 4, 4 * C
CH = HID // 128
FT = 512
NFT = NB * N // FT
FP = FT // TP
NPA = NB * NP
VW = 32


def build(nc, x, w0, b0, wp0, bp0, w1a, b1a, wp1, bp1, lk1, lv1, lk2, lv2, gw, gb, ew1, eb1, ew2, eb2, out):
    with ExitStack() as ctx:
        def sb(name, shape, dt=F32):
            return ctx.enter_context(nc.sbuf_tensor(name, shape, dt))

        def sem(name):
            return ctx.enter_context(nc.semaphore(name))

        ident = sb("ident", [128, 128])
        group_mean = sb("group_mean", [C, C])
        head_of = sb("head_of", [C, NH])
        head_rows = sb("head_rows", [NH, C])
        block = sb("block", [C, C])
        offsets = sb("offsets", [C, C], I32)
        offsets_f = sb("offsets_f", [C, C])
        offsets_sq = sb("offsets_sq", [C, C])
        gauss = sb("gauss", [C, C])
        attn_mask = sb("attn_mask", [C, C])
        lower = sb("lower", [128, NE, NE])
        minus_half = sb("minus_half", [128, NP])
        ln_eps = sb("ln_eps", [128, NP])
        wqkv0 = sb("wqkv0", [C + 1, 3 * C])
        wqk0 = sb("wqk0", [C + 1, 2, C])
        ident_b = sb("ident_b", [128, 128], BF16)
        pair_rows = sb("pair_rows", [KROWS, 2])
        head_keys = sb("head_keys", [MROWS, HP, 2, T], BF16)
        wproj0 = sb("wproj0", [C + 1, C])
        wqkv1 = sb("wqkv1", [C + 1, 3 * C])
        wq1T = sb("wq1T", [C, C + 1])
        wproj1 = sb("wproj1", [C, C])
        bproj1 = sb("bproj1", [C + 1, C])
        gate_w = sb("gate_w", [C + 1, NE])
        up_w = sb("up_w", [C + 1, NE, HID])
        down_w = sb("down_w", [128, NE, CH, C])
        down_b = sb("down_b", [C, NE])
        lam_in = sb("lam_in", [NH, 4, HD])
        lam_prod = sb("lam_prod", [NH, 2, HD])
        lam_sum = sb("lam_sum", [NH, 2])
        lam_exp = sb("lam_exp", [NH, 2])
        lam_dif = sb("lam_dif", [NH, 1])
        lam_keep = sb("lam_keep", [NH, 1])
        lam_col = sb("lam_col", [C, 1])

        t2_all = sb("t2_all", [128, NPA, C])
        h2T_all = sb("h2T_all", [C + 1, NB * N])
        scores = sb("scores", [128, NPA, NE])


        phase1 = ExitStack()

        def sb1(name, shape, dt=F32):
            return phase1.enter_context(nc.sbuf_tensor(name, shape, dt))

        x_in = [sb1(f"x_in{u}", [128, NP, C]) for u in range(2)]
        x_res = [sb1(f"x_res{u}", [128, NP, C]) for u in range(2)]
        xT = sb1("xT", [C, N])
        gn_stats = sb1("gn_stats", [C, IM, 6])
        gn_mv = sb1("gn_mv", [C, IM, 2])
        gn_mean = sb1("gn_mean", [C, IM])
        gn_dif = sb1("gn_dif", [C, IM])
        gn_sq = sb1("gn_sq", [C, IM])
        gn_spread = sb1("gn_spread", [C, IM])
        gn_var = sb1("gn_var", [C, IM])
        gn_rstd = sb1("gn_rstd", [C, IM])
        xh = [sb1(f"xh{u}", [C + 1, N]) for u in range(2)]
        parts = [sb1(f"parts{n}", [C, PARTS, N], BF16) for n in range(2)]
        rest = [sb1(f"rest{n}", [C, N]) for n in range(2)]
        q_packed = [sb1(f"q_packed{u}", [KROWS + MROWS, HP, N], BF16) for u in range(2)]
        k_packed = sb1("k_packed", [KROWS, HP, N], BF16)
        k_split = [sb1(f"k_split{u}", [KROWS + MROWS, HP, NW, 2, T], BF16) for u in range(2)]
        v_heads = [sb1(f"v_heads{u}", [128, NW, HP, VW]) for u in range(2)]
        neg_max = sb1("neg_max", [128, NH])
        neg_max_parts = sb1("neg_max_parts", [128, MROWS], BF16)
        probs = [sb1(f"probs{p}", [128, HP, TP]) for p in range(2)]
        o_sb = sb1("o_sb", [C, IM, 2 * NIT])
        o_rden = sb1("o_rden", [128, NI * NH])
        o_norm = sb1("o_norm", [128, NP * NH, HD])
        oT_sb = sb1("oT_sb", [C + 1, N])
        t1 = [sb1(f"t1_{u}", [128, NP, C]) for u in range(2)]
        ln1_stats = sb1("ln1_stats", [128, NP, 6])
        ln1_mv = sb1("ln1_mv", [128, NP, 2])
        ln1_var = sb1("ln1_var", [128, NP])
        ln1_rstd = sb1("ln1_rstd", [128, NP])
        h1 = sb1("h1", [128, NP, C])
        h1T = [sb1(f"h1T{u}", [C + 1, N]) for u in range(2)]
        kv_neg = sb1("kv_neg", [128, NP, 2 * C])
        kv_exp = sb1("kv_exp", [128, NP, 2 * C])
        feat = sb1("feat", [128, NP, 2 * C])
        attn_sb = sb1("attn_sb", [C, IM, C])
        attn_proj = sb1("attn_proj", [C, IM, C])
        fold_w = sb1("fold_w", [C + 1, IM, C])
        ln2_stats = sb1("ln2_stats", [128, NP, 6])
        ln2_mv = sb1("ln2_mv", [128, NP, 2])
        ln2_var = sb1("ln2_var", [128, NP])
        ln2_rstd = sb1("ln2_rstd", [128, NP])
        h2 = sb1("h2", [128, NP, C])
        h2T = sb1("h2T", [C + 1, N])
        phase1.close()

        g_max = sb("g_max", [128, NPA])
        g_shift = sb("g_shift", [128, NPA, NE])
        g_exp = sb("g_exp", [128, NPA, NE])
        g_sum = sb("g_sum", [128, NPA])
        g_rsum = sb("g_rsum", [128, NPA])
        g_prob = sb("g_prob", [128, NPA, NE])
        g_above = sb("g_above", [128, NPA, NE, NE])
        g_equal = sb("g_equal", [128, NPA, NE, NE])
        g_rank = sb("g_rank", [128, NPA * NE])
        g_mix = sb("g_mix", [128, NPA * NE])
        mixT = sb("mixT", [128, 2, 128])
        mix_rows = [sb(f"mix_rows{u}", [C, FP, NE, 128]) for u in range(2)]
        up_parts = [sb(f"up_part{n}", [C + 1, NE, HID], F32R) for n in range(2)]
        down_parts = [sb(f"down_part{n}", [128, NE, CH, C], F32R) for n in range(2)]
        in_parts = [[sb(f"in_part{n}_{u}", [C + 1, FT], F32R) for n in range(2)] for u in range(2)]
        hidden = [sb(f"hidden{n}", [128, FT]) for n in range(4)]
        hidden_parts = [[sb(f"hidden_part{p}_{n}", [128, FT], F32R) for p in range(2)] for n in range(4)]
        y_scaled = sb("y_scaled", [C, FT])
        y_acc = [sb(f"y_acc{u}", [C, FT]) for u in range(2)]
        out_sb = [sb(f"out_sb{u}", [128, FP, C]) for u in range(2)]
        mix_dram = nc.dram_tensor("mix_dram", [NPA, NE, 128], F32, kind="Internal").ap()

        parts_dram = nc.dram_tensor("parts_dram", [2, 2, PARTS, C, N], BF16, kind="Internal").ap()

        ps = ctx.enter_context(nc.psum_tensor("ps", [128, 8, 512], F32))
        FRONT, TAIL_A, TAIL_B, OUT_B = 0, 1, 2, 7
        S_BANKS, P_BANKS = 3, 5
        xT_ps = ps[0:C, FRONT, :]
        gmean_ps = ps[0:C, FRONT, 0:IM]
        gvar_ps = ps[0:C, FRONT, IM:2 * IM]
        qk_ps = ps[0:C, FRONT, :]
        v_ps = ps[:, FRONT, 0:NW * HP * HD].rearrange("p (w a d) -> p w a d", w=NW, d=HD)
        s_ps = ps[:, S_BANKS:S_BANKS + 2, 0:HP * T].rearrange("p b (h s) -> p b h s", s=T)
        pT_ps = ps[:, P_BANKS:P_BANKS + 2, 0:3 * TP]
        max_ps = ps[KROWS:KROWS + MROWS, P_BANKS, 3 * TP:3 * TP + TP // 2].bitcast(BF16)
        o_ps = ps[0:C, OUT_B, :]
        oT1_ps = ps[:, TAIL_A, 0:NI * NH * 16].rearrange("p (h d) -> p h d", d=16)
        oT2_ps = ps[0:C, TAIL_A, :]
        y0_ps = ps[:, TAIL_A, 0:NP * C].rearrange("p (q c) -> p q c", q=NP)
        h1T_ps = ps[0:C, TAIL_A, :]
        kv_ps = [ps[:, bank, 0:NI * 2 * C].rearrange("p (q c) -> p q c", q=NI) for bank in (TAIL_A, TAIL_B)]
        attn_ps = ps[0:C, TAIL_B, 0:IM * C].rearrange("p (i c) -> p i c", i=IM)
        aproj_ps = ps[0:C, TAIL_B, 0:IM * C].rearrange("p (i c) -> p i c", i=IM)
        fold_ps = ps[0:C + 1, TAIL_B, 0:IM * C].rearrange("p (i c) -> p i c", i=IM)
        y1_ps = ps[:, TAIL_B, 0:NP * C].rearrange("p (q c) -> p q c", q=NP)
        h2T_ps = ps[0:C, TAIL_B, :]
        gate_ps = ps[:, TAIL_B, 0:NP * NE].rearrange("p (q e) -> p q e", q=NP)
        up_ps = [ps[:, n, :] for n in range(4)]
        down_ps = [ps[0:C, 4 + n, :] for n in range(2)]
        final_ps = ps[:, 6, 0:FP * C].rearrange("p (q c) -> p q c", q=FP)
        mixT_ps = ps[:, 7, 0:256].rearrange("p (q c) -> p q c", q=2)

        weights_loaded = sem("weights_loaded")
        experts_loaded = sem("experts_loaded")
        x_loaded = [sem(f"x_loaded{u}") for u in range(2)]
        parts_stored = sem("parts_stored")
        packed_loaded = sem("packed_loaded")
        mix_stored = sem("mix_stored")
        mix_loaded = [sem(f"mix_loaded{u}") for u in range(2)]
        out_stored = [sem(f"out_stored{u}") for u in range(2)]
        pool_const = sem("pool_const")
        zeros_set = sem("zeros_set")
        consts_ready = sem("consts_ready")
        setup_step = sem("setup_step")
        lam_sums = sem("lam_sums")
        lam_exps = sem("lam_exps")
        offs_sq_ready = sem("offs_sq_ready")
        gauss_ready = sem("gauss_ready")
        wq1T_ready = sem("wq1T_ready")
        lam_keep_ready = sem("lam_keep_ready")
        lam_col_ready = sem("lam_col_ready")
        lam_col_copied = sem("lam_col_copied")
        wq1T_copied = sem("wq1T_copied")
        wqk0_ready = sem("wqk0_ready")
        kpad_step = sem("kpad_step")
        kpad_loaded = sem("kpad_loaded")
        h2T_ones = sem("h2T_ones")
        xT_ready = sem("xT_ready")
        xT_copied = sem("xT_copied")
        gn_stat_step = sem("gn_stat_step")
        gn_stats_ready = sem("gn_stats_ready")
        gmean_ready = sem("gmean_ready")
        gn_mean_ready = sem("gn_mean_ready")
        gn_dif_ready = sem("gn_dif_ready")
        gn_sq_ready = sem("gn_sq_ready")
        spread_ready = sem("spread_ready")
        gvar_ready = sem("gvar_ready")
        gn_var_ready = sem("gn_var_ready")
        gn_rstd_ready = sem("gn_rstd_ready")
        xh_ready = sem("xh_ready")
        x_kept = sem("x_kept")
        q_ready = sem("q_ready")
        q_part1 = sem("q_part1")
        q_rest = sem("q_rest")
        q_part2 = sem("q_part2")
        q_part3 = sem("q_part3")
        k_ready = sem("k_ready")
        k_part1 = sem("k_part1")
        k_rest = sem("k_rest")
        k_part2 = sem("k_part2")
        k_part3 = sem("k_part3")
        k_split_ready = sem("k_split_ready")
        v_ready = sem("v_ready")
        v_copied = sem("v_copied")
        scores_ready = sem("scores_ready")
        neg_max_ready = sem("neg_max_ready")
        max_part1 = sem("max_part1")
        max_part2 = sem("max_part2")
        max_ready = sem("max_ready")
        max_packed = sem("max_packed")
        shifted_ready = sem("shifted_ready")
        probs_ready = sem("probs_ready")
        pv_done = sem("pv_done")
        o_copied = sem("o_copied")
        oT1_ready = sem("oT1_ready")
        o_rden_ready = sem("o_rden_ready")
        o_norm_ready = sem("o_norm_ready")
        oT2_ready = sem("oT2_ready")
        oT_copied = sem("oT_copied")
        y0_ready = sem("y0_ready")
        t1_ready = sem("t1_ready")
        ln1_bn_ready = sem("ln1_bn_ready")
        ln1_mv_ready = sem("ln1_mv_ready")
        ln1_var_ready = sem("ln1_var_ready")
        ln1_rstd_ready = sem("ln1_rstd_ready")
        h1_ready = sem("h1_ready")
        h1T_ready = sem("h1T_ready")
        h1T_copied = sem("h1T_copied")
        kv_ready = sem("kv_ready")
        kv_neg_ready = sem("kv_neg_ready")
        kv_exp_ready = sem("kv_exp_ready")
        feat_ready = sem("feat_ready")
        attn_ready = sem("attn_ready")
        attn_masked = sem("attn_masked")
        aproj_ready = sem("aproj_ready")
        aproj_copied = sem("aproj_copied")
        fold_ready = sem("fold_ready")
        fold_copied = sem("fold_copied")
        y1_ready = sem("y1_ready")
        t2_ready = sem("t2_ready")
        ln2_bn_ready = sem("ln2_bn_ready")
        ln2_mv_ready = sem("ln2_mv_ready")
        ln2_var_ready = sem("ln2_var_ready")
        ln2_rstd_ready = sem("ln2_rstd_ready")
        h2_ready = sem("h2_ready")
        h2T_ready = sem("h2T_ready")
        h2T_copied = sem("h2T_copied")
        h2T_kept = sem("h2T_kept")
        gate_ready = sem("gate_ready")
        gate_copied = sem("gate_copied")
        g_step = sem("g_step")
        g_shift_ready = sem("g_shift_ready")
        g_exp_ready = sem("g_exp_ready")
        g_mix_ready = sem("g_mix_ready")
        mixT_ready = sem("mixT_ready")
        mixT_copied = sem("mixT_copied")
        weight_part1 = sem("weight_part1")
        weight_part2 = sem("weight_part2")
        in_part1 = sem("in_part1")
        in_part2 = sem("in_part2")
        up_ready = sem("up_ready")
        hidden_ready = sem("hidden_ready")
        hidden_part1 = sem("hidden_part1")
        hidden_part2 = sem("hidden_part2")
        down_done = sem("down_done")
        scaled_step = sem("scaled_step")
        final_ready = sem("final_ready")
        out_ready = sem("out_ready")

        blk = ctx.enter_context(nc.Block())

        def nth(k, u):
            return 2 * k + u + 1

        def met(eng):
            eng.wait_ge(pool_const, 22)

        def is_first(t):
            return isinstance(t, int) and t == 0

        def after(k, u, n):
            return k + (u + n) // 2, (u + n) % 2

        def schedule(eng, iteration):
            def one(b):
                iteration(b // 2, b % 2, b + 2 < NB, b + 1 < NB, b < NB, 1 <= b <= NB, b >= 2)
            for b in range(2):
                one(b)
            with eng.Fori(1, NB // 2 - 1) as k:
                for u in range(2):
                    iteration(k, u, True, True, True, True, True)
            for b in range(NB - 2, NB + 2):
                one(b)

        @blk.sync
        def _(sp):
            def load(dst, src, s):
                sp.dma_start(dst, src).then_inc(s, 16)

            def load_block(dst, k, u, s):
                for im in range(IM):
                    for wr in range(NI):
                        for wc in range(2):
                            src = x[bass.ds(IM * (2 * k + u) + im, 1), wr * WS:(wr + 1) * WS, wc * WS:(wc + 1) * WS, :]
                            load(dst[wc * T:(wc + 1) * T, im * NI + wr, :], src.rearrange("b i j c -> (b i) j c"), s)

            def pack(k, u):
                n = nth(k, u)
                for s, part3 in enumerate((q_part3, k_part3)):
                    if s == 1:
                        if not is_first(k):
                            sp.wait_ge(shifted_ready, NP * (n - 2))
                        if not (is_first(k) and u == 0):
                            sp.wait_ge(k_split_ready, n - 1)
                    sp.wait_ge(part3, n)
                    sp.dma_start(parts_dram[u, s, :, :, :].rearrange("a c n -> c a n"), parts[s][:, :, :])\
                        .then_inc(parts_stored, 16)
                sp.wait_ge(parts_stored, 32 * n)
                half = SLOTS * HD
                for s, dst in enumerate((q_packed[u], k_packed)):
                    for part, slot, count in ((0, 0, 3), (1, 3, 2), (2, 5, 1)):
                        for odd in range(2):
                            src = parts_dram[u, s, :, odd * C // 2:(odd + 1) * C // 2, :]\
                                .rearrange("a (d h) n -> a d (h n)", d=HD)
                            src = src[part:part + 1].broadcast_to([count, HD, HP * N]) if s == 0 else src[0:count]
                            at = odd * half + slot * HD
                            load(dst[at:at + count * HD, :, :].rearrange("p h n -> p (h n)"), src, packed_loaded)

            load_block(x_in[0], 0, 0, x_loaded[0])
            load(wqkv0[0:C, :], w0, weights_loaded)
            load(wqkv0[C:C + 1, :], b0.rearrange("(a n) -> a n", a=1), weights_loaded)
            load_block(x_in[1], 0, 1, x_loaded[1])
            load(wproj0[0:C, :], wp0, weights_loaded)
            load(wproj0[C:C + 1, :], bp0.rearrange("(a n) -> a n", a=1), weights_loaded)
            load(wqkv1[0:C, :], w1a, weights_loaded)
            load(wqkv1[C:C + 1, :], b1a.rearrange("(a n) -> a n", a=1), weights_loaded)
            load(wproj1[:, :], wp1, weights_loaded)
            for n, a in enumerate((lk1, lv1, lk2, lv2)):
                load(lam_in[:, n, :], a, weights_loaded)
            load(gate_w[0:C, :], gw, weights_loaded)
            load(gate_w[C:C + 1, :], gb.rearrange("(a n) -> a n", a=1), weights_loaded)
            sp.wait_ge(kpad_step, 3)
            for u in range(2):
                for hp in range(HP):
                    one = head_keys[:, hp, :, :].rearrange("p b s -> p (b s)").unsqueeze(1)
                    load(k_split[u][KROWS:KROWS + MROWS, hp, :, :, :].rearrange("p w b s -> p w (b s)"),
                         one.broadcast_to([MROWS, NW, 2 * T]), kpad_loaded)
            sp.wait_ge(zeros_set, 3)
            load(bproj1[C:C + 1, :], bp1.rearrange("(a n) -> a n", a=1), weights_loaded)
            pack(0, 0)
            load(up_w[0:C, :, :], ew1.rearrange("e c n -> c e n"), experts_loaded)
            load(up_w[C:C + 1, :, :], eb1.rearrange("(a e) n -> a e n", a=1), experts_loaded)
            load(down_w[:, :, :, :].rearrange("p e c n -> p (e c) n"),
                 ew2.rearrange("e (c p) n -> p (e c) n", p=128), experts_loaded)
            sp.dma_start(down_b[:, :], eb2.rearrange("e n -> n e"), allow_slow_non_contiguous=True)\
                .then_inc(experts_loaded, 16)

            def fetch(k, u):
                met(sp)
                sp.wait_ge(x_kept, nth(k, u) - 2)
                sp.wait_ge(xT_ready, nth(k, u) - 2)
                load_block(x_in[u], k, u, x_loaded[u])

            fetch(1, 0)
            pack(0, 1)
            fetch(1, 1)
            with sp.Fori(1, NB // 2 - 1) as k:
                for u in range(2):
                    pack(k, u)
                    fetch(k + 1, u)
            pack(NB // 2 - 1, 0)
            pack(NB // 2 - 1, 1)

            sp.wait_ge(mixT_copied, 1)
            mix_v = mix_dram.rearrange("(b t) e n -> (t e) b n", b=2)
            sp.dma_start(mix_v, mixT[:, :, :]).then_inc(mix_stored, 16)
            sp.wait_ge(mix_stored, 16)

            def load_mix(t, u):
                src = mix_dram[bass.ds(t * FP, FP), :, :].rearrange("(a t) e n -> a (t e n)", a=1)
                load(mix_rows[u][:, :, :, :].rearrange("p t e n -> p (t e n)"), src.broadcast_to([C, FP * NE * 128]),
                     mix_loaded[u])

            def store(k, u):
                sp.wait_ge(out_ready, nth(k, u))
                for im in range(2):
                    for wc in range(2):
                        for wr in range(2):
                            dst = out[bass.ds(2 * (2 * k + u) + im, 1), wr * WS:(wr + 1) * WS,
                                      wc * WS:(wc + 1) * WS, :]
                            sp.dma_start(dst.rearrange("b i j c -> (b i) j c"),
                                         out_sb[u][wc * T:(wc + 1) * T, im * NI + wr, :]).then_inc(out_stored[u], 16)

            load_mix(0, 0)
            load_mix(1, 1)
            for u in range(2):
                sp.wait_ge(scaled_step, 7 * (u + 1))
                load_mix(2 + u, u)
                store(0, u)
            with sp.Fori(1, NFT // 2 - 1) as k:
                for u in range(2):
                    sp.wait_ge(scaled_step, 7 * nth(k, u))
                    load_mix(2 * k + u + 2, u)
                    store(k, u)
            for u in range(2):
                store(NFT // 2 - 1, u)
            for u in range(2):
                sp.wait_ge(out_stored[u], 16 * 8 * (NFT // 2))

        @blk.gpsimd
        def _(pool):
            pool.memset(ident[:, :], 0.0).then_inc(pool_const, 1)
            pool.memset(group_mean[:, :], 1.0 / GC).then_inc(pool_const, 1)
            pool.memset(head_of[:, :], 1.0).then_inc(pool_const, 1)
            pool.memset(head_rows[:, :], 1.0).then_inc(pool_const, 1)
            pool.memset(block[:, :], 1.0).then_inc(pool_const, 1)
            pool.memset(lower[:, :, :], 1.0).then_inc(pool_const, 1)
            pool.iota(offsets[:, :], pattern=[[-1, C]], base=0, channel_multiplier=1).then_inc(pool_const, 1)
            pool.memset(minus_half[:, :], -0.5).then_inc(pool_const, 1)
            pool.memset(ln_eps[:, :], LN_EPS).then_inc(pool_const, 1)
            pool.memset(pair_rows[:, :], 1.0).then_inc(pool_const, 1)
            pool.wait_ge(pool_const, 10)

            def keep(t, view, pattern, base, mult, n):
                pool.affine_select(out=view, in_=view, compare_op=ALU.is_ge, fill=0.0, base=base,
                                   pattern=pattern, channel_multiplier=mult).then_inc(pool_const, 1)

            pool.affine_select(out=ident[:, :], in_=ident[:, :], compare_op=ALU.not_equal, fill=1.0, base=0,
                               pattern=[[-1, 128]], channel_multiplier=1).then_inc(pool_const, 1)
            groups = group_mean[:, :].rearrange("p (g c) -> p g c", c=GC)
            blocks = block[:, :].rearrange("p (h d) -> p h d", d=HD)
            keep(group_mean, groups, [[-GC, C // GC], [0, GC]], 0, 1, 0)
            keep(head_of, head_of[:, :], [[-HD, NH]], 0, 1, 0)
            keep(head_rows, head_rows[:, :], [[1, C]], 0, -HD, 0)
            keep(block, blocks, [[-HD, NH], [0, HD]], 0, 1, 0)
            keep(lower, lower[:, :, :], [[1, NE], [-1, NE]], -1, 0, 0)
            keep(pair_rows, pair_rows[:, 0:1], [[0, 1]], KROWS // 2 - 1, -1, 0)
            keep(pair_rows, pair_rows[:, 1:2], [[0, 1]], -KROWS // 2, 1, 0)
            pool.wait_ge(pool_const, 18)
            keep(group_mean, groups, [[GC, C // GC], [0, GC]], GC - 1, -1, 0)
            keep(head_of, head_of[:, :], [[HD, NH]], HD - 1, -1, 0)
            keep(head_rows, head_rows[:, :], [[-1, C]], HD - 1, HD, 0)
            keep(block, blocks, [[HD, NH], [0, HD]], HD - 1, -1, 0)
            pool.wait_ge(pool_const, 22)
            pool.memset(xh[0][C:C + 1, :], 1.0).then_inc(consts_ready, 1)
            pool.memset(xh[1][C:C + 1, :], 1.0).then_inc(consts_ready, 1)
            pool.memset(oT_sb[C:C + 1, :], 1.0).then_inc(consts_ready, 1)
            pool.memset(h1T[0][C:C + 1, :], 1.0).then_inc(consts_ready, 1)
            pool.memset(h1T[1][C:C + 1, :], 1.0).then_inc(consts_ready, 1)
            pool.memset(h2T[C:C + 1, :], 1.0).then_inc(consts_ready, 1)
            pool.memset(head_keys[:, :, :, :], 0.0).then_inc(kpad_step, 1)
            for part in range(2):
                pool.wait_ge(kpad_step, part + 1)
                pool.affine_select(out=head_keys[:, :, :, :], in_=head_keys[:, :, :, :], compare_op=ALU.not_equal,
                                   fill=1.0, base=-part * NH, pattern=[[-2, HP], [-1, 2], [0, T]],
                                   channel_multiplier=1).then_inc(kpad_step, 1)

            def gn_rstd_of(k, u):
                pool.wait_ge(gn_var_ready, nth(k, u))
                pool.tensor_tensor(gn_rstd[:, :], gn_var[:, :], minus_half[0:C, 0:IM], ALU.pow)\
                    .then_inc(gn_rstd_ready, 1)

            def third_part(k, u, s):
                pool.wait_ge((q_part2, k_part2)[s], nth(k, u))
                pool.tensor_tensor(parts[s][:, 2, :], rest[s][:, :], parts[s][:, 1, :], ALU.subtract)\
                    .then_inc((q_part3, k_part3)[s], 1)

            def ln_rstd(k, u, mv, var, rstd, mv_ready, var_ready, rstd_ready):
                pool.wait_ge(mv_ready, nth(k, u))
                pool.tensor_tensor(var[:, :], mv[:, :, 1], ln_eps[:, :], ALU.add).then_inc(var_ready, 1)
                pool.wait_ge(var_ready, nth(k, u))
                pool.tensor_tensor(rstd[:, :], var[:, :], minus_half[:, :], ALU.pow).then_inc(rstd_ready, 1)

            def iteration(k, u, norm, project, attend, tail_a, tail_b):
                if project:
                    third_part(*after(k, u, 1), 0)
                    third_part(*after(k, u, 1), 1)
                if tail_b:
                    ln_rstd(*after(k, u, -2), ln2_mv, ln2_var, ln2_rstd, ln2_mv_ready, ln2_var_ready, ln2_rstd_ready)
                if tail_a:
                    ln_rstd(*after(k, u, -1), ln1_mv, ln1_var, ln1_rstd, ln1_mv_ready, ln1_var_ready, ln1_rstd_ready)
                if norm:
                    gn_rstd_of(*after(k, u, 2))
                if tail_b:
                    kb, ub = after(k, u, -2)
                    pool.wait_ge(h2T_copied, nth(kb, ub))
                    pool.tensor_copy(h2T_all[0:C, bass.ds((2 * kb + ub) * N, N)], h2T[0:C, :]).then_inc(h2T_kept, 1)

            gn_rstd_of(0, 0)
            third_part(0, 0, 0)
            third_part(0, 0, 1)
            gn_rstd_of(0, 1)
            pool.memset(h2T_all[C:C + 1, :], 1.0).then_inc(h2T_ones, 1)
            schedule(pool, iteration)

            pool.wait_ge(experts_loaded, 16 * 4)
            pool.wait_ge(h2T_kept, NB)
            pool.wait_ge(gate_copied, NB)
            for n, (w, w_parts) in enumerate(((up_w, up_parts), (down_w, down_parts))):
                w, first, second = [v[:].rearrange(("p e n -> p (e n)", "p e c n -> p (e c n)")[n])
                                    for v in (w, *w_parts)]
                pool.tensor_copy(first, w).then_inc(weight_part1, 1)
                pool.wait_ge(weight_part1, n + 1)
                pool.tensor_tensor(second, w, first.bitcast(F32), ALU.subtract).then_inc(weight_part2, 1)

            def input_parts(t, u):
                first, second = in_parts[u]
                pool.wait_ge(in_part1, t + 1)
                pool.tensor_tensor(second[:, :], h2T_all[:, bass.ds(t * FT, FT)], first[:, :].bitcast(F32),
                                   ALU.subtract).then_inc(in_part2, 1)

            input_parts(0, 0)
            input_parts(1, 1)
            with pool.Fori(1, NFT // 2) as k:
                for u in range(2):
                    input_parts(2 * k + u, u)

        @blk.tensor
        def _(pe):
            def x_transpose(k, u):
                pe.wait_ge(x_loaded[u], 16 * 2 * NP * (k + 1))
                pe.wait_ge(v_copied, 2 * (nth(k, u) - 1))
                for p in range(NP):
                    last = pe.transpose(xT_ps[:, p * TP:(p + 1) * TP], x_in[u][:, p, :], ident[:, :])
                last.then_inc(xT_ready, 1)

            def gmean(k, u):
                pe.wait_ge(gn_stats_ready, nth(k, u))
                pe.matmul(gmean_ps, group_mean[:, :], gn_mv[:, :, 0], start=True, stop=True).then_inc(gmean_ready, 1)

            def gvar(k, u):
                pe.wait_ge(spread_ready, nth(k, u))
                pe.matmul(gvar_ps, group_mean[:, :], gn_spread[:, :], start=True, stop=True).then_inc(gvar_ready, 1)

            def q_proj(k, u):
                pe.wait_ge(xh_ready, nth(k, u))
                pe.matmul(qk_ps, wqk0[:, 0, :], xh[u][:, :], start=True, stop=True).then_inc(q_ready, 1)

            def k_proj(k, u):
                pe.wait_ge(q_rest, nth(k, u))
                pe.matmul(qk_ps, wqk0[:, 1, :], xh[u][:, :], start=True, stop=True).then_inc(k_ready, 1)

            def v_proj(k, u, half):
                pe.wait_ge(k_rest, nth(k, u))
                if half:
                    pe.wait_ge(v_copied, 2 * nth(k, u) - 1)
                wv = wqkv0[:, 2 * C:3 * C].rearrange("p (a b d) -> p a b d", b=2, d=HD)
                for w in range(half * NWI, (half + 1) * NWI):
                    for odd in range(2):
                        last = pe.matmul(v_ps[odd * T:(odd + 1) * T, w, :, :], xh[u][:, w * T:(w + 1) * T],
                                         wv[:, :, odd, :], start=True, stop=True)
                last.then_inc(v_ready, 1)

            def scores_of(k, u, p):
                done = NP * (2 * k + u) + p
                if p == 0:
                    pe.wait_ge(k_split_ready, nth(k, u))
                    pe.wait_ge(packed_loaded, 16 * 12 * nth(k, u))
                pe.wait_ge(neg_max_ready, done)
                for w2 in range(2):
                    w = 2 * p + w2
                    for hp in range(HP):
                        last = pe.matmul(s_ps[w2 * T:(w2 + 1) * T, hp // 3, 2 * (hp % 3):2 * (hp % 3) + 2, :],
                                         q_packed[u][0:KROWS, hp, w * T:(w + 1) * T],
                                         k_split[u][0:KROWS, hp, w, :, :], start=True, stop=True)
                last.then_inc(scores_ready, 1)

            def max_transpose(k, u, p):
                done = NP * (2 * k + u) + p
                pe.wait_ge(max_part2, done + 1)
                pe.wait_ge(probs_ready, done)
                pe.transpose(max_ps, neg_max_parts[:, :], ident_b[:, :]).then_inc(max_ready, 1)

            def shifted_scores(k, u, p):
                pe.wait_ge(max_packed, NP * (2 * k + u) + p + 1)
                for hp in range(HP):
                    for w2 in range(2):
                        w = 2 * p + w2
                        at = (hp % 3) * TP + w2 * T
                        last = pe.matmul(pT_ps[:, hp // 3, at:at + T],
                                         k_split[u][:, hp, w, :, :].rearrange("p b s -> p (b s)"),
                                         q_packed[u][:, hp, w * T:(w + 1) * T], start=True, stop=True)
                last.then_inc(shifted_ready, 1)

            def pv(k, u, p):
                done = NP * (2 * k + u) + p
                pe.wait_ge(probs_ready, done + 1)
                pe.wait_ge(v_copied, 2 * (2 * k + u) + p // NI + 1)
                if p % NI == 0:
                    pe.wait_ge(o_copied, IM * (2 * k + u) + p // NI)
                for w2 in range(2):
                    w = 2 * p + w2
                    at = (w % NWI) * T
                    for hp in range(HP):
                        g, r = hp % 3, hp // 3
                        last = pe.matmul(o_ps[g * VW:(g + 1) * VW, r * NIT + at:r * NIT + at + T],
                                         v_heads[u][:, w, hp, :], probs[p % 2][:, hp, w2 * T:(w2 + 1) * T],
                                         start=True, stop=True)
                last.then_inc(pv_done, 1)

            def oT1(k, u, im):
                done = IM * (2 * k + u) + im
                pe.wait_ge(o_copied, done + 1)
                if im:
                    pe.wait_ge(o_norm_ready, done)
                elif not (is_first(k) and u == 0):
                    pe.wait_ge(feat_ready, done - 1)
                for p in range(NI):
                    for r in range(2):
                        last = pe.transpose(ps[:, TAIL_A, (2 * p + r) * C:(2 * p + r + 1) * C],
                                            o_sb[:, im, r * NIT + p * TP:r * NIT + (p + 1) * TP], ident[0:C, 0:C])
                last.then_inc(oT1_ready, 1)

            def oT2(k, u):
                pe.wait_ge(o_norm_ready, IM * nth(k, u))
                for p in range(NP):
                    last = pe.transpose(oT2_ps[:, p * TP:(p + 1) * TP],
                                        o_norm[:, p * NH:(p + 1) * NH, :].rearrange("p h d -> p (h d)"), ident[:, :])
                last.then_inc(oT2_ready, 1)

            def y0(k, u):
                pe.wait_ge(oT_copied, nth(k, u))
                for p in range(NP):
                    last = pe.matmul(y0_ps[:, p, :], oT_sb[:, p * TP:(p + 1) * TP], wproj0[:, :],
                                     start=True, stop=True)
                last.then_inc(y0_ready, 1)

            def h1_transpose(k, u):
                pe.wait_ge(h1_ready, nth(k, u))
                for p in range(NP):
                    last = pe.transpose(h1T_ps[:, p * TP:(p + 1) * TP], h1[:, p, :], ident[:, :])
                last.then_inc(h1T_ready, 1)

            def kv(k, u, im):
                pe.wait_ge(h1T_copied, nth(k, u))
                if im:
                    pe.wait_ge(gate_copied, nth(k, u) - 1)
                for p in range(NI):
                    at = (im * NI + p) * TP
                    last = pe.matmul(kv_ps[im][:, p, :], h1T[u][:, at:at + TP], wqkv1[:, C:3 * C],
                                     start=True, stop=True)
                last.then_inc(kv_ready, 1)

            def attn_sum(k, u):
                pe.wait_ge(feat_ready, IM * nth(k, u))
                for im in range(IM):
                    for p in range(NI):
                        f = feat[:, im * NI + p, :]
                        last = pe.matmul(attn_ps[:, im, :], f[:, C:2 * C], f[:, 0:C], start=p == 0, stop=p == NI - 1)
                last.then_inc(attn_ready, 1)

            def attn_times_proj(k, u):
                pe.wait_ge(attn_masked, nth(k, u))
                for im in range(IM):
                    last = pe.matmul(aproj_ps[:, im, :], attn_sb[:, im, :], wproj1[:, :], start=True, stop=True)
                last.then_inc(aproj_ready, 1)

            def fold(k, u):
                pe.wait_ge(aproj_copied, nth(k, u))
                pe.matmul(fold_ps, wq1T[:, :], attn_proj[:, :, :], start=True, stop=True).then_inc(fold_ready, 1)

            def y1(k, u):
                pe.wait_ge(fold_copied, nth(k, u))
                for p in range(NP):
                    last = pe.matmul(y1_ps[:, p, :], h1T[u][:, p * TP:(p + 1) * TP], fold_w[:, p // NI, :],
                                     start=True, stop=True)
                last.then_inc(y1_ready, 1)

            def h2_transpose(k, u):
                pe.wait_ge(h2_ready, nth(k, u))
                for p in range(NP):
                    last = pe.transpose(h2T_ps[:, p * TP:(p + 1) * TP], h2[:, p, :], ident[:, :])
                last.then_inc(h2T_ready, 1)

            def gate(k, u):
                pe.wait_ge(h2T_copied, nth(k, u))
                for p in range(NP):
                    last = pe.matmul(gate_ps[:, p, :], h2T[:, p * TP:(p + 1) * TP], gate_w[:, :],
                                     start=True, stop=True)
                last.then_inc(gate_ready, 1)

            def iteration(k, u, norm, project, attend, tail_a, tail_b):
                n, j, a, b = after(k, u, 2), after(k, u, 1), after(k, u, -1), after(k, u, -2)

                def when(there, step, *args):
                    if there:
                        step(*args)

                when(attend, scores_of, k, u, 0)
                when(project, q_proj, *j)
                when(tail_a, shifted_scores, *a, 3)
                when(tail_b, attn_sum, *b)
                when(tail_a, pv, *a, 2)
                when(project, k_proj, *j)
                when(attend, max_transpose, k, u, 0)
                when(tail_b, attn_times_proj, *b)
                when(tail_a, oT1, *a, 0)

                when(attend, scores_of, k, u, 1)
                when(tail_b, fold, *b)
                when(attend, shifted_scores, k, u, 0)
                when(project, v_proj, *j, 0)
                when(tail_a, pv, *a, 3)
                when(tail_b, y1, *b)
                when(attend, max_transpose, k, u, 1)
                when(project, v_proj, *j, 1)
                when(tail_a, oT1, *a, 1)

                when(attend, scores_of, k, u, 2)
                when(tail_a, oT2, *a)
                when(attend, shifted_scores, k, u, 1)
                when(norm, x_transpose, *n)
                when(attend, pv, k, u, 0)
                when(tail_a, y0, *a)
                when(tail_b, h2_transpose, *b)
                when(attend, max_transpose, k, u, 2)
                when(norm, gmean, *n)

                when(attend, scores_of, k, u, 3)
                when(tail_b, gate, *b)
                when(attend, shifted_scores, k, u, 2)
                when(norm, gvar, *n)
                when(attend, pv, k, u, 1)
                when(tail_a, h1_transpose, *a)
                when(attend, max_transpose, k, u, 3)
                when(tail_a, kv, *a, 0)
                when(tail_a, kv, *a, 1)

            pe.wait_ge(pool_const, 22)
            x_transpose(0, 0)
            gmean(0, 0)
            gvar(0, 0)
            pe.wait_ge(weights_loaded, 16 * 14)
            pe.wait_ge(consts_ready, 6)
            pe.wait_ge(wqk0_ready, 1)
            pe.transpose(ps[0:C, TAIL_A, 0:C + 1], wqkv1[:, 0:C], ident[0:C + 1, 0:C + 1]).then_inc(wq1T_ready, 1)
            q_proj(0, 0)
            k_proj(0, 0)
            pe.wait_ge(lam_keep_ready, 1)
            pe.matmul(ps[0:C, TAIL_B, 0:1], head_rows[:, :], lam_keep[:, :], start=True, stop=True)\
                .then_inc(lam_col_ready, 1)
            v_proj(0, 0, 0)
            v_proj(0, 0, 1)
            x_transpose(0, 1)
            gmean(0, 1)
            gvar(0, 1)
            pe.wait_ge(wq1T_copied, 1)
            pe.wait_ge(lam_col_copied, 1)
            pe.wait_ge(kpad_loaded, 16 * 2 * HP)
            schedule(pe, iteration)

            def product(out, w_parts, x_parts, start, stop):
                pe.matmul(out, w_parts[0], x_parts[0], start=start, stop=False)
                pe.matmul(out, w_parts[1], x_parts[0], start=False, stop=False)
                return pe.matmul(out, w_parts[0], x_parts[1], start=False, stop=stop)

            def up(t, u, n):
                e, c = n // CH, n % CH
                if n == 0:
                    pe.wait_ge(in_part2, t + 1)
                if n >= 4 or not is_first(t):
                    pe.wait_ge(hidden_part1, t * NE * CH + n - 3)
                product(up_ps[n % 4], [w[:, e, c * 128:(c + 1) * 128] for w in up_parts],
                        [h[:, :] for h in in_parts[u]], True, True).then_inc(up_ready, 1)

            def down(t, n):
                e, c = n // CH, n % CH
                pe.wait_ge(hidden_part2, t * NE * CH + n + 1)
                if c == 0 and (e >= 2 or not is_first(t)):
                    step = (1, 2, 4, 6)[(e + 2) % 4]
                    pe.wait_ge(scaled_step, 7 * t + step - (7 if e < 2 else 0))
                product(down_ps[e % 2], [w[:, e, c, :] for w in down_parts], [h[:, :] for h in hidden_parts[n % 4]],
                        c == 0, c == CH - 1).then_inc(down_done, 1)

            def final(t, u):
                pe.wait_ge(scaled_step, 7 * (t + 1))
                if not is_first(t):
                    pe.wait_ge(out_ready, t)
                for p in range(FP):
                    last = pe.transpose(final_ps[:, p, :], y_acc[u][:, p * TP:(p + 1) * TP], ident[0:C, 0:C])
                last.then_inc(final_ready, 1)

            def mix_transpose():
                pe.wait_ge(g_mix_ready, 1)
                for b in range(2):
                    last = pe.transpose(mixT_ps[:, b, :], g_mix[:, b * 128:(b + 1) * 128], ident[:, :])
                last.then_inc(mixT_ready, 1)

            def tile(t, u, first):
                for n in range(NE * CH):
                    up(t, u, n)
                    if n == 2 and first:
                        mix_transpose()
                    if n >= 2:
                        down(t, n - 2)
                    elif not first:
                        down(t - 1, n - 2 + NE * CH)
                    if n == 5 and not first:
                        final(t - 1, 1 - u)

            pe.wait_ge(weight_part2, 2)
            pe.wait_ge(gate_copied, NB)
            tile(0, 0, True)
            tile(1, 1, False)
            with pe.Fori(1, NFT // 2) as k:
                for u in range(2):
                    tile(2 * k + u, u, False)
            down(NFT - 1, NE * CH - 2)
            down(NFT - 1, NE * CH - 1)
            final(NFT - 1, 1)

        @blk.scalar
        def _(act):
            def copy_xT(k, u):
                act.wait_ge(xT_ready, nth(k, u))
                act.wait_ge(xh_ready, nth(k, u) - 1)
                act.activation(xT[:, :], xT_ps, ACT.Copy).then_inc(xT_copied, 1)

            def first_part(k, u, s):
                act.wait_ge((q_ready, k_ready)[s], nth(k, u))
                act.wait_ge(parts_stored, 32 * (nth(k, u) - 1))
                act.activation(parts[s][:, 0, :], qk_ps, ACT.Copy).then_inc((q_part1, k_part1)[s], 1)

            def second_part(k, u, s):
                act.wait_ge((q_rest, k_rest)[s], nth(k, u))
                act.activation(parts[s][:, 1, :], rest[s][:, :], ACT.Copy).then_inc((q_part2, k_part2)[s], 1)

            def copy_v(k, u, half):
                act.wait_ge(v_ready, 2 * (2 * k + u) + half + 1)
                if not is_first(k):
                    act.wait_ge(pv_done, NP * (nth(k, u) - 2))
                ws = slice(half * NWI, (half + 1) * NWI)
                for odd in range(2):
                    last = act.activation(v_heads[u][odd * T:(odd + 1) * T, ws, :, odd * 16:odd * 16 + HD],
                                          v_ps[odd * T:(odd + 1) * T, ws, :, :], ACT.Copy)
                last.then_inc(v_copied, 1)

            def pack_max(k, u, p):
                act.wait_ge(max_ready, NP * (2 * k + u) + p + 1)
                act.activation(q_packed[u][KROWS:KROWS + MROWS, :, p * TP:(p + 1) * TP],
                               max_ps.unsqueeze(1).broadcast_to([MROWS, HP, TP]), ACT.Copy).then_inc(max_packed, 1)

            def exp_probs(k, u, p):
                done = NP * (2 * k + u) + p
                act.wait_ge(shifted_ready, done + 1)
                if not (is_first(k) and u == 0 and p < 2):
                    act.wait_ge(pv_done, done - 1)
                act.activation(probs[p % 2][:, :, :].rearrange("p (b h) t -> p b (h t)", b=2), pT_ps, ACT.Exp,
                               scale=SCALE).then_inc(probs_ready, 1)

            def copy_o(k, u, im):
                done = IM * (2 * k + u) + im
                act.wait_ge(pv_done, NI * (done + 1))
                if not (is_first(k) and u == 0):
                    act.wait_ge(oT1_ready, done - 1)
                act.activation(o_sb[:, im, :], o_ps, ACT.Copy).then_inc(o_copied, 1)

            def copy_oT(k, u):
                act.wait_ge(oT2_ready, nth(k, u))
                act.wait_ge(y0_ready, nth(k, u) - 1)
                act.activation(oT_sb[0:C, :], oT2_ps, ACT.Copy).then_inc(oT_copied, 1)

            def copy_h1T(k, u):
                act.wait_ge(h1T_ready, nth(k, u))
                if not is_first(k):
                    act.wait_ge(y1_ready, nth(k, u) - 2)
                act.activation(h1T[u][0:C, :], h1T_ps, ACT.Copy).then_inc(h1T_copied, 1)

            def keep_x(k, u):
                act.wait_ge(x_loaded[u], 16 * 2 * NP * (k + 1))
                if not is_first(k):
                    act.wait_ge(t1_ready, nth(k, u) - 2)
                act.activation(x_res[u][:, :, :], x_in[u][:, :, :], ACT.Copy).then_inc(x_kept, 1)

            def exp_kv(k, u, im):
                done = IM * (2 * k + u) + im
                act.wait_ge(kv_neg_ready, done + 1)
                if not (is_first(k) and u == 0):
                    act.wait_ge(feat_ready, done - 1)
                pairs = slice(im * NI, (im + 1) * NI)
                act.activation(kv_exp[:, pairs, :], kv_neg[:, pairs, :], ACT.Exp).then_inc(kv_exp_ready, 1)

            def copy_aproj(k, u):
                act.wait_ge(aproj_ready, nth(k, u))
                act.wait_ge(fold_ready, nth(k, u) - 1)
                act.activation(attn_proj[:, :, :], aproj_ps, ACT.Copy).then_inc(aproj_copied, 1)

            def copy_h2T(k, u):
                act.wait_ge(h2T_ready, nth(k, u))
                act.wait_ge(gate_ready, nth(k, u) - 1)
                act.wait_ge(h2T_kept, nth(k, u) - 1)
                act.activation(h2T[0:C, :], h2T_ps, ACT.Copy).then_inc(h2T_copied, 1)

            def iteration(k, u, norm, project, attend, tail_a, tail_b):
                n, j, a, b = after(k, u, 2), after(k, u, 1), after(k, u, -1), after(k, u, -2)

                def when(there, step, *args):
                    if there:
                        step(*args)

                when(project, first_part, *j, 0)
                when(tail_a, exp_probs, *a, 3)
                when(project, second_part, *j, 0)
                when(project, first_part, *j, 1)
                when(attend, pack_max, k, u, 0)
                when(tail_b, copy_aproj, *b)
                when(project, second_part, *j, 1)

                when(attend, exp_probs, k, u, 0)
                when(project, copy_v, *j, 0)
                when(tail_a, copy_o, *a, 1)
                when(attend, pack_max, k, u, 1)
                when(project, copy_v, *j, 1)

                when(tail_a, copy_oT, *a)
                when(attend, exp_probs, k, u, 1)
                when(norm, copy_xT, *n)
                when(tail_b, copy_h2T, *b)
                when(attend, pack_max, k, u, 2)

                when(attend, exp_probs, k, u, 2)
                when(attend, copy_o, k, u, 0)
                when(tail_a, copy_h1T, *a)
                when(attend, pack_max, k, u, 3)
                when(tail_a, exp_kv, *a, 0)
                when(tail_a, exp_kv, *a, 1)
                when(project, keep_x, *j)

            copy_xT(0, 0)
            for s in range(2):
                first_part(0, 0, s)
                second_part(0, 0, s)
            act.wait_ge(lam_sums, 1)
            act.activation(lam_exp[:, :], lam_sum[:, :], ACT.Exp).then_inc(lam_exps, 1)
            act.wait_ge(offs_sq_ready, 1)
            act.activation(gauss[:, :], offsets_sq[:, :], ACT.Exp, scale=-2.0).then_inc(gauss_ready, 1)
            act.wait_ge(wq1T_ready, 1)
            act.activation(wq1T[:, :], ps[0:C, TAIL_A, 0:C + 1], ACT.Copy, scale=SCALE).then_inc(wq1T_copied, 1)
            act.wait_ge(zeros_set, 3)
            copy_v(0, 0, 0)
            copy_v(0, 0, 1)
            keep_x(0, 0)
            copy_xT(0, 1)
            schedule(act, iteration)

            act.wait_ge(g_shift_ready, 1)
            act.activation(g_exp[:, :, :], g_shift[:, :, :], ACT.Exp).then_inc(g_exp_ready, 1)

            def input_part(t, u):
                if not (isinstance(t, int) and t < 2):
                    act.wait_ge(up_ready, (t - 1) * NE * CH)
                act.activation(in_parts[u][0][:, :], h2T_all[:, bass.ds(t * FT, FT)], ACT.Copy).then_inc(in_part1, 1)

            def tile(t, u):
                for n in range(NE * CH):
                    act.wait_ge(up_ready, t * NE * CH + n + 1)
                    if n >= 4 or not is_first(t):
                        act.wait_ge(down_done, t * NE * CH + n - 3)
                    act.activation(hidden[n % 4][:, :], up_ps[n % 4], ACT.Gelu).then_inc(hidden_ready, 1)
                    act.activation(hidden_parts[n % 4][0][:, :], up_ps[n % 4], ACT.Gelu).then_inc(hidden_part1, 1)
                    if n == 3 and not (isinstance(t, int) and (t == 0 or t == NFT - 1)):
                        input_part(t + 1, 1 - u)

            act.wait_ge(h2T_kept, NB)
            act.wait_ge(h2T_ones, 1)
            input_part(0, 0)
            input_part(1, 1)
            tile(0, 0)
            tile(1, 1)
            with act.Fori(1, NFT // 2 - 1) as k:
                for u in range(2):
                    tile(2 * k + u, u)
            tile(NFT - 2, 0)
            tile(NFT - 1, 1)

        @blk.vector
        def _(dve):
            def gn_stats_of(k, u):
                dve.wait_ge(xT_copied, nth(k, u))
                for im in range(IM):
                    last = dve.bn_stats(gn_stats[:, im, :], xT[:, im * NIT:(im + 1) * NIT])
                last.then_inc(gn_stat_step, 1)
                met(dve)
                dve.wait_ge(gn_stat_step, nth(k, u))
                for im in range(IM):
                    last = dve.bn_aggr(gn_mv[:, im, :], gn_stats[:, im, :])
                last.then_inc(gn_stats_ready, 1)

            def gn_spread_of(k, u):
                dve.wait_ge(gmean_ready, nth(k, u))
                dve.tensor_copy(gn_mean[:, :], gmean_ps).then_inc(gn_mean_ready, 1)
                dve.wait_ge(gn_mean_ready, nth(k, u))
                dve.tensor_tensor(gn_dif[:, :], gn_mv[:, :, 0], gn_mean[:, :], ALU.subtract).then_inc(gn_dif_ready, 1)
                dve.wait_ge(gn_dif_ready, nth(k, u))
                dve.tensor_tensor(gn_sq[:, :], gn_dif[:, :], gn_dif[:, :], ALU.mult).then_inc(gn_sq_ready, 1)
                dve.wait_ge(gn_sq_ready, nth(k, u))
                dve.tensor_tensor(gn_spread[:, :], gn_sq[:, :], gn_mv[:, :, 1], ALU.add).then_inc(spread_ready, 1)

            def gn_var_of(k, u):
                dve.wait_ge(gvar_ready, nth(k, u))
                dve.tensor_scalar(gn_var[:, :], gvar_ps, GN_EPS, None, ALU.add).then_inc(gn_var_ready, 1)

            def gn_apply(k, u):
                dve.wait_ge(gn_rstd_ready, nth(k, u))
                if not is_first(k):
                    dve.wait_ge(v_ready, 2 * (nth(k, u) - 2))
                for im in range(IM):
                    cols = slice(im * NIT, (im + 1) * NIT)
                    last = dve.tensor_scalar(xh[u][0:C, cols], xT[:, cols], gn_mean[:, im:im + 1],
                                             gn_rstd[:, im:im + 1], ALU.subtract, ALU.mult)
                last.then_inc(xh_ready, 1)

            def rest_of(k, u, s):
                dve.wait_ge((q_part1, k_part1)[s], nth(k, u))
                dve.wait_ge((q_part3, k_part3)[s], nth(k, u) - 1)
                dve.tensor_tensor(rest[s][:, :], qk_ps, parts[s][:, 0, :], ALU.subtract)\
                    .then_inc((q_rest, k_rest)[s], 1)

            def split_keys(k, u):
                dve.wait_ge(packed_loaded, 16 * 12 * nth(k, u))
                if not is_first(k):
                    dve.wait_ge(shifted_ready, NP * (nth(k, u) - 2))
                src = k_packed[:, :, :].rearrange("p h (w s) -> p (h w) s", s=T)
                dst = k_split[u][0:KROWS, :, :, :, :].rearrange("p h w b s -> p (h w) b s")
                for odd in range(2):
                    last = dve.tensor_scalar(dst[:, :, odd, :], src, pair_rows[:, odd:odd + 1], None, ALU.mult)
                last.then_inc(k_split_ready, 1)

            def maxima(k, u, p):
                done = NP * (2 * k + u) + p
                dve.wait_ge(scores_ready, done + 1)
                dve.tensor_reduce(neg_max[:, :].rearrange("p (b h) -> p b h", b=2), s_ps, AX.X, ALU.max, negate=True)\
                    .then_inc(neg_max_ready, 1)
                dve.wait_ge(neg_max_ready, done + 1)
                dve.wait_ge(max_ready, done)
                dve.tensor_copy(neg_max_parts[:, 0:NH], neg_max[:, :]).then_inc(max_part1, 1)
                dve.wait_ge(max_part1, done + 1)
                dve.tensor_tensor(neg_max_parts[:, NH:2 * NH], neg_max[:, :], neg_max_parts[:, 0:NH], ALU.subtract)\
                    .then_inc(max_part2, 1)

            def normalise(k, u, im):
                done = IM * (2 * k + u) + im
                dve.wait_ge(oT1_ready, done + 1)
                dve.reciprocal(o_rden[:, :], oT1_ps[:, :, HD]).then_inc(o_rden_ready, 1)
                dve.wait_ge(o_rden_ready, done + 1)
                dve.wait_ge(oT2_ready, nth(k, u) - 1)
                dve.tensor_tensor(o_norm[:, im * NI * NH:(im + 1) * NI * NH, :], oT1_ps[:, :, 0:HD],
                                  o_rden[:, :].unsqueeze(2).broadcast_to([128, NI * NH, HD]), ALU.mult)\
                    .then_inc(o_norm_ready, 1)

            def residual1(k, u):
                dve.wait_ge(y0_ready, nth(k, u))
                dve.wait_ge(x_kept, nth(k, u))
                dve.tensor_tensor(t1[u][:, :, :], y0_ps, x_res[u][:, :, :], ALU.add).then_inc(t1_ready, 1)
                dve.wait_ge(t1_ready, nth(k, u))
                for p in range(NP):
                    last = dve.bn_stats(ln1_stats[:, p, :], t1[u][:, p, :])
                last.then_inc(ln1_bn_ready, 1)
                met(dve)
                dve.wait_ge(ln1_bn_ready, nth(k, u))
                for p in range(NP):
                    last = dve.bn_aggr(ln1_mv[:, p, :], ln1_stats[:, p, :])
                last.then_inc(ln1_mv_ready, 1)

            def norm1(k, u):
                dve.wait_ge(ln1_rstd_ready, nth(k, u))
                dve.wait_ge(h1T_ready, nth(k, u) - 1)
                for p in range(NP):
                    last = dve.tensor_scalar(h1[:, p, :], t1[u][:, p, :], ln1_mv[:, p, 0:1], ln1_rstd[:, p:p + 1],
                                             ALU.subtract, ALU.mult)
                last.then_inc(h1_ready, 1)

            def kv_negative(k, u, im):
                done = IM * (2 * k + u) + im
                dve.wait_ge(kv_ready, done + 1)
                if not (is_first(k) and u == 0):
                    dve.wait_ge(kv_exp_ready, done - 1)
                dve.tensor_scalar(kv_neg[:, im * NI:(im + 1) * NI, :], kv_ps[im], 0.0, None, ALU.min)\
                    .then_inc(kv_neg_ready, 1)

            def features(k, u, im):
                pairs = slice(im * NI, (im + 1) * NI)
                dve.wait_ge(kv_exp_ready, IM * (2 * k + u) + im + 1)
                dve.wait_ge(attn_ready, nth(k, u) - 1)
                dve.scalar_tensor_tensor(feat[:, pairs, :], kv_ps[im], 0.0, kv_exp[:, pairs, :], ALU.max, ALU.add)\
                    .then_inc(feat_ready, 1)

            def mask_attn(k, u):
                dve.wait_ge(attn_ready, nth(k, u))
                dve.wait_ge(aproj_ready, nth(k, u) - 1)
                dve.tensor_tensor(attn_sb[:, :, :], attn_ps, attn_mask[:, :].unsqueeze(1).broadcast_to([C, IM, C]),
                                  ALU.mult).then_inc(attn_masked, 1)

            def copy_fold(k, u):
                dve.wait_ge(fold_ready, nth(k, u))
                dve.wait_ge(y1_ready, nth(k, u) - 1)
                dve.tensor_tensor(fold_w[:, :, :], fold_ps, bproj1[:, :].unsqueeze(1).broadcast_to([C + 1, IM, C]),
                                  ALU.add).then_inc(fold_copied, 1)

            def residual2(k, u):
                pair = (2 * k + u) * NP
                dve.wait_ge(y1_ready, nth(k, u))
                dve.tensor_tensor(t2_all[:, bass.ds(pair, NP), :], y1_ps, t1[u][:, :, :], ALU.add).then_inc(t2_ready, 1)
                met(dve)
                dve.wait_ge(t2_ready, nth(k, u))
                for p in range(NP):
                    last = dve.bn_stats(ln2_stats[:, p, :], t2_all[:, bass.ds(pair + p, 1), :].rearrange("p a c -> p (a c)"))
                last.then_inc(ln2_bn_ready, 1)
                met(dve)
                dve.wait_ge(ln2_bn_ready, nth(k, u))
                for p in range(NP):
                    last = dve.bn_aggr(ln2_mv[:, p, :], ln2_stats[:, p, :])
                last.then_inc(ln2_mv_ready, 1)

            def norm2(k, u):
                pair = (2 * k + u) * NP
                dve.wait_ge(ln2_rstd_ready, nth(k, u))
                dve.wait_ge(h2T_ready, nth(k, u) - 1)
                for p in range(NP):
                    last = dve.tensor_scalar(h2[:, p, :],
                                             t2_all[:, bass.ds(pair + p, 1), :].rearrange("p a c -> p (a c)"),
                                             ln2_mv[:, p, 0:1], ln2_rstd[:, p:p + 1], ALU.subtract, ALU.mult)
                last.then_inc(h2_ready, 1)

            def copy_gate(k, u):
                dve.wait_ge(gate_ready, nth(k, u))
                dve.tensor_copy(scores[:, bass.ds((2 * k + u) * NP, NP), :], gate_ps).then_inc(gate_copied, 1)

            def iteration(k, u, norm, project, attend, tail_a, tail_b):
                n, j, a, b = after(k, u, 2), after(k, u, 1), after(k, u, -1), after(k, u, -2)

                def when(there, step, *args):
                    if there:
                        step(*args)

                when(attend, maxima, k, u, 0)
                when(project, rest_of, *j, 0)
                when(tail_b, mask_attn, *b)
                when(project, rest_of, *j, 1)

                when(tail_b, copy_fold, *b)
                when(attend, maxima, k, u, 1)
                when(tail_a, normalise, *a, 0)
                when(tail_b, residual2, *b)

                when(tail_a, normalise, *a, 1)
                when(attend, maxima, k, u, 2)
                when(tail_b, norm2, *b)
                when(norm, gn_stats_of, *n)
                when(tail_a, residual1, *a)

                when(norm, gn_spread_of, *n)
                when(attend, maxima, k, u, 3)
                when(tail_a, norm1, *a)
                when(tail_b, copy_gate, *b)
                when(norm, gn_var_of, *n)
                when(norm, gn_apply, *n)
                when(project, split_keys, *j)
                for im in range(IM):
                    when(tail_a, kv_negative, *a, im)
                for im in range(IM):
                    when(tail_a, features, *a, im)

            for u in range(2):
                dve.memset(v_heads[u][:, :, :, :], 0.0).then_inc(setup_step, 1)
            dve.memset(bproj1[:, :], 0.0).then_inc(zeros_set, 1)
            dve.wait_ge(setup_step, 2)
            for u in range(2):
                for odd in range(2):
                    last = dve.memset(v_heads[u][odd * T:(odd + 1) * T, :, :, odd * 16 + HD:odd * 16 + HD + 1], 1.0)
                last.then_inc(zeros_set, 1)
            dve.wait_ge(pool_const, 22)
            gn_stats_of(0, 0)
            gn_spread_of(0, 0)
            gn_var_of(0, 0)
            dve.wait_ge(consts_ready, 6)
            gn_apply(0, 0)
            dve.tensor_copy(ident_b[:, :], ident[:, :])
            dve.wait_ge(weights_loaded, 16 * 14)
            for s in range(2):
                last = dve.tensor_copy(wqk0[:, s, :].rearrange("p (b d a) -> p b d a", b=2, d=HD),
                                       wqkv0[:, s * C:(s + 1) * C].rearrange("p (a b d) -> p b d a", b=2, d=HD))
            last.then_inc(wqk0_ready, 1)
            rest_of(0, 0, 0)
            rest_of(0, 0, 1)
            dve.tensor_copy(offsets_f[:, :], offsets[:, :]).then_inc(setup_step, 1)
            dve.wait_ge(setup_step, 3)
            dve.tensor_tensor(offsets_sq[:, :], offsets_f[:, :], offsets_f[:, :], ALU.mult).then_inc(offs_sq_ready, 1)
            dve.wait_ge(weights_loaded, 16 * 14)
            dve.tensor_tensor(lam_prod[:, :, :], lam_in[:, 0:4:2, :], lam_in[:, 1:4:2, :], ALU.mult)\
                .then_inc(setup_step, 1)
            dve.wait_ge(setup_step, 4)
            dve.tensor_reduce(lam_sum[:, :], lam_prod[:, :, :], AX.X, ALU.add).then_inc(lam_sums, 1)
            dve.wait_ge(lam_exps, 1)
            dve.tensor_tensor(lam_dif[:, :], lam_exp[:, 1:2], lam_exp[:, 0:1], ALU.subtract).then_inc(setup_step, 1)
            dve.wait_ge(setup_step, 5)
            dve.tensor_scalar(lam_keep[:, :], lam_dif[:, :], 1.0 - LAMBDA_INIT, None, ALU.add)\
                .then_inc(lam_keep_ready, 1)
            dve.wait_ge(lam_col_ready, 1)
            dve.tensor_copy(lam_col[:, :], ps[0:C, TAIL_B, 0:1]).then_inc(lam_col_copied, 1)
            dve.wait_ge(lam_col_copied, 1)
            dve.wait_ge(gauss_ready, 1)
            dve.scalar_tensor_tensor(attn_mask[:, :], gauss[:, :], lam_col[:, 0:1], block[:, :], ALU.mult, ALU.mult)\
                .then_inc(setup_step, 1)
            dve.wait_ge(setup_step, 6)
            gn_stats_of(0, 1)
            gn_spread_of(0, 1)
            gn_var_of(0, 1)
            gn_apply(0, 1)
            split_keys(0, 0)
            schedule(dve, iteration)

            steps = [0]

            def link(ins):
                steps[0] += 1
                ins.then_inc(g_step, 1)
                dve.wait_ge(g_step, steps[0])

            def over_experts(v):
                return v.unsqueeze(2).broadcast_to([128, NPA, NE])

            dve.wait_ge(gate_copied, NB)
            link(dve.tensor_reduce(g_max[:, :], scores[:, :, :], AX.X, ALU.max))
            dve.tensor_tensor(g_shift[:, :, :], scores[:, :, :], over_experts(g_max[:, :]), ALU.subtract)\
                .then_inc(g_shift_ready, 1)
            dve.wait_ge(g_exp_ready, 1)
            link(dve.tensor_reduce(g_sum[:, :], g_exp[:, :, :], AX.X, ALU.add))
            link(dve.reciprocal(g_rsum[:, :], g_sum[:, :]))
            link(dve.tensor_tensor(g_prob[:, :, :], g_exp[:, :, :], over_experts(g_rsum[:, :]), ALU.mult))
            others = g_prob[:, :, :].unsqueeze(2).broadcast_to([128, NPA, NE, NE])
            own = g_prob[:, :, :].unsqueeze(3).broadcast_to([128, NPA, NE, NE])
            link(dve.tensor_tensor(g_above[:, :, :, :], others, own, ALU.is_gt))
            link(dve.tensor_tensor(g_equal[:, :, :, :], others, own, ALU.is_equal))
            ge = g_equal[:, :, :, :].rearrange("p n a b -> p n (a b)")
            ga = g_above[:, :, :, :].rearrange("p n a b -> p n (a b)")
            low = lower[:, :, :].rearrange("p a b -> p (a b)").unsqueeze(1).broadcast_to([128, NPA, NE * NE])
            link(dve.tensor_tensor(ge, ge, low, ALU.mult))
            link(dve.tensor_tensor(ga, ga, ge, ALU.add))
            link(dve.tensor_reduce(g_rank[:, :], g_above[:, :, :, :].rearrange("p n a b -> p (n a) b"), AX.X, ALU.add))
            probs_flat = g_prob[:, :, :].rearrange("p n e -> p (n e)")
            link(dve.scalar_tensor_tensor(g_mix[:, :], g_rank[:, :], 1.5, probs_flat, ALU.is_lt, ALU.mult))
            mix3 = g_mix[:, :].rearrange("p (n e) -> p n e", e=NE)
            link(dve.tensor_reduce(g_sum[:, :], mix3, AX.X, ALU.add))
            link(dve.tensor_scalar(g_sum[:, :], g_sum[:, :], 1e-9, None, ALU.add))
            link(dve.reciprocal(g_rsum[:, :], g_sum[:, :]))
            dve.tensor_tensor(mix3, mix3, over_experts(g_rsum[:, :]), ALU.mult).then_inc(g_mix_ready, 1)
            dve.wait_ge(mixT_ready, 1)
            dve.tensor_copy(mixT[:, :, :], mixT_ps).then_inc(mixT_copied, 1)

            dve.wait_ge(experts_loaded, 16 * 4)

            def mix_expert(t, k, u, e):
                acc = y_acc[u][:, :].rearrange("p (t n) -> p t n", n=TP)
                scaled = y_scaled[:, :].rearrange("p (t n) -> p t n", n=TP)
                if e == 0:
                    dve.wait_ge(mix_loaded[u], 16 * (k + 1))
                dve.wait_ge(down_done, (t * NE + e + 1) * CH)
                if e == 0 and (not isinstance(t, int) or t >= 2):
                    dve.wait_ge(final_ready, t - 1)
                dve.scalar_tensor_tensor(acc if e == 0 else scaled,
                                         down_ps[e % 2].rearrange("p (t n) -> p t n", n=TP), down_b[:, e:e + 1],
                                         mix_rows[u][:, :, e, :], ALU.add, ALU.mult).then_inc(scaled_step, 1)
                if e:
                    dve.wait_ge(scaled_step, 7 * t + 2 * e)
                    dve.tensor_tensor(acc, acc, scaled, ALU.add).then_inc(scaled_step, 1)
                    dve.wait_ge(scaled_step, 7 * t + 2 * e + 1)

            def finish_tile(t, k, u):
                dve.wait_ge(final_ready, t + 1)
                if not isinstance(t, int) or t >= 2:
                    dve.wait_ge(out_stored[u], 16 * 8 * k)
                dve.tensor_tensor(out_sb[u][:, :, :], final_ps, t2_all[:, bass.ds(t * FP, FP), :], ALU.add)\
                    .then_inc(out_ready, 1)

            def tile(t, k, u, first):
                for n in range(NE * CH):
                    dve.wait_ge(hidden_part1, t * NE * CH + n + 1)
                    dve.wait_ge(hidden_ready, t * NE * CH + n + 1)
                    if n >= 4 or not is_first(t):
                        dve.wait_ge(down_done, t * NE * CH + n - 3)
                    dve.tensor_tensor(hidden_parts[n % 4][1][:, :], hidden[n % 4][:, :],
                                      hidden_parts[n % 4][0][:, :].bitcast(F32), ALU.subtract)\
                        .then_inc(hidden_part2, 1)
                    if n % CH == 1 and n > 1:
                        mix_expert(t, k, u, n // CH - 1)
                    elif n == 1 and not first:
                        mix_expert(t - 1, k - 1 + u, 1 - u, NE - 1)
                    if n == 8 and not first:
                        finish_tile(t - 1, k - 1 + u, 1 - u)

            tile(0, 0, 0, True)
            tile(1, 0, 1, False)
            with dve.Fori(1, NFT // 2) as k:
                for u in range(2):
                    tile(2 * k + u, k, u, False)
            mix_expert(NFT - 1, NFT // 2 - 1, 1, NE - 1)
            finish_tile(NFT - 1, NFT // 2 - 1, 1)


_INS = ['x', 'L0_conv_w_qkv', 'L0_conv_b_qkv', 'L0_conv_w_proj', 'L0_conv_b_proj', 'L1_attn_qkv_w', 'L1_attn_qkv_b',
        'L1_attn_proj_w', 'L1_attn_proj_b', 'L1_attn_lambda_k1', 'L1_attn_lambda_v1', 'L1_attn_lambda_k2',
        'L1_attn_lambda_v2', 'L1_ffn_gate_w', 'L1_ffn_gate_b', 'L1_ffn_w1', 'L1_ffn_b1', 'L1_ffn_w2', 'L1_ffn_b2']
_OUT = ((B, HI, WI, C), 'float32')


def kernel(**inputs):
    import concourse.bacc as bacc
    from concourse.bass_utils import run_bass_kernel_spmd

    nc = bacc.Bacc("TRN2", target_bir_lowering=False, num_devices=1)
    arrays, args = {}, []
    for name in _INS:
        a = np.ascontiguousarray(inputs[name])
        arrays[f"in_{name}"] = a
        args.append(nc.dram_tensor(f"in_{name}", a.shape, mybir.dt.from_np(a.dtype), kind="ExternalInput").ap())
    args.append(nc.dram_tensor("out_0", _OUT[0], mybir.dt.from_np(np.dtype(_OUT[1])), kind="ExternalOutput").ap())
    build(nc, *args)
    r = run_bass_kernel_spmd(nc, [arrays], core_ids=[0])
    return r.results[0]["out_0"]
```

```python
from contextlib import ExitStack
import math

import numpy as np
import concourse.bass as bass
from concourse import mybir

F32 = mybir.dt.float32
F32R = mybir.dt.float32r
I32 = mybir.dt.int32
BF16 = mybir.dt.bfloat16
ALU = mybir.AluOpType
ACT = mybir.ActivationFunctionType
AX = mybir.AxisListType

B, HI, WI, C = 32, 16, 16, 96
WS = 8
NH, HD = 12, 8
T = WS * WS
TP = 2 * T
IM = 2
NB = B // IM
NI = HI * WI // TP
NP = IM * NI
N = IM * HI * WI
NIT = HI * WI
NW = N // T
NWI = NIT // T
HP = NH // 2
PARTS = 3
SLOTS = 6
KROWS = 2 * SLOTS * HD
MROWS = 2 * NH
GC = C // 32
SCALE = HD ** -0.5
LAMBDA_INIT = 0.8 - 0.6 * math.exp(-0.3)
GN_EPS, LN_EPS = 1e-5, 1e-5
NE, HID = 4, 4 * C
CH = HID // 128
FT = 512
NFT = NB * N // FT
FP = FT // TP
NPA = NB * NP
LAG = 3
GATE_GROUPS = (slice(0, NPA - 2 * NP), slice(NPA - 2 * NP, NPA))
VW = 32


def build(nc, x, w0, b0, wp0, bp0, w1a, b1a, wp1, bp1, lk1, lv1, lk2, lv2, gw, gb, ew1, eb1, ew2, eb2, out):
    with ExitStack() as ctx:
        def sb(name, shape, dt=F32):
            return ctx.enter_context(nc.sbuf_tensor(name, shape, dt))

        def sem(name):
            return ctx.enter_context(nc.semaphore(name))

        ident = sb("ident", [128, 128])
        group_mean = sb("group_mean", [C, C])
        head_of = sb("head_of", [C, NH])
        head_rows = sb("head_rows", [NH, C])
        block = sb("block", [C, C])
        offsets = sb("offsets", [C, C], I32)
        offsets_f = sb("offsets_f", [C, C])
        offsets_sq = sb("offsets_sq", [C, C])
        gauss = sb("gauss", [C, C])
        attn_mask = sb("attn_mask", [C, C])
        lower = sb("lower", [128, NE, NE])
        minus_half = sb("minus_half", [128, NP])
        ln_eps = sb("ln_eps", [128, NP])
        wqkv0 = sb("wqkv0", [C + 1, 3 * C])
        wqk0 = sb("wqk0", [C + 1, 2, C])
        ident_b = sb("ident_b", [128, 128], BF16)
        pair_rows = sb("pair_rows", [KROWS, 2])
        head_keys = sb("head_keys", [MROWS, HP, 2, T], BF16)
        wproj0 = sb("wproj0", [C + 1, C])
        wqkv1 = sb("wqkv1", [C + 1, 3 * C])
        wq1T = sb("wq1T", [C, C + 1])
        wproj1 = sb("wproj1", [C, C])
        bproj1 = sb("bproj1", [C + 1, C])
        gate_w = sb("gate_w", [C + 1, NE])
        up_parts = [sb(f"up_part{n}", [C + 1, NE, HID], F32R) for n in range(2)]
        down_parts = [sb(f"down_part{n}", [128, NE, CH, C], F32R) for n in range(2)]
        down_b = sb("down_b", [C, NE])
        lam_in = sb("lam_in", [NH, 4, HD])
        lam_prod = sb("lam_prod", [NH, 2, HD])
        lam_sum = sb("lam_sum", [NH, 2])
        lam_exp = sb("lam_exp", [NH, 2])
        lam_dif = sb("lam_dif", [NH, 1])
        lam_keep = sb("lam_keep", [NH, 1])
        lam_col = sb("lam_col", [C, 1])

        t2_all = sb("t2_all", [128, NPA, C])
        up_w = t2_all[0:C + 1, NPA // 2:NPA // 2 + NE * HID // C, :].rearrange("p (e h) c -> p e (h c)", e=NE)
        down_w = t2_all[:, NPA // 2 + NE * HID // C:NPA // 2 + NE * HID // C + NE * CH, :]\
            .rearrange("p (e c) n -> p e c n", e=NE)
        h2T_all = sb("h2T_all", [C + 1, NB * N])
        scores = sb("scores", [128, NPA, NE])


        parts_room = sb("parts_room", [128, 2, PARTS * N // 2])
        parts = [parts_room[0:C, n, :].bitcast(BF16).rearrange("c (a n) -> c a n", a=PARTS) for n in range(2)]
        rest_room = sb("rest_room", [128, 2, N])
        rest = [rest_room[0:C, n, :] for n in range(2)]
        g_shift, g_exp, g_prob = [parts_room[:, 0, n * NPA * NE:(n + 1) * NPA * NE].rearrange("p (n e) -> p n e", e=NE)
                                  for n in range(3)]
        g_rank = parts_room[:, 1, 0:NPA * NE].rearrange("p (n e) -> p n e", e=NE)
        g_mix = parts_room[:, 1, NPA * NE:2 * NPA * NE]
        g_max, g_sum, g_rsum = [parts_room[:, 1, at:at + NPA] for at in range(2 * NPA * NE, 2 * NPA * NE + 3 * NPA, NPA)]
        g_above, g_equal = [rest_room[:, n, :].bitcast(BF16).rearrange("p (n a b) -> p n a b", a=NE, b=NE)
                            for n in range(2)]

        phase1 = ExitStack()

        def sb1(name, shape, dt=F32):
            return phase1.enter_context(nc.sbuf_tensor(name, shape, dt))

        x_in = [sb1(f"x_in{u}", [128, NP, C]) for u in range(2)]
        x_res = [sb1(f"x_res{u}", [128, NP, C]) for u in range(2)]
        xT = sb1("xT", [C, N])
        gn_stats = sb1("gn_stats", [C, IM, 6])
        gn_mv = sb1("gn_mv", [C, IM, 2])
        gn_mean = sb1("gn_mean", [C, IM])
        gn_dif = sb1("gn_dif", [C, IM])
        gn_sq = sb1("gn_sq", [C, IM])
        gn_spread = sb1("gn_spread", [C, IM])
        gn_var = sb1("gn_var", [C, IM])
        gn_rstd = sb1("gn_rstd", [C, IM])
        xh = [sb1(f"xh{u}", [C + 1, N]) for u in range(2)]
        q_packed = [sb1(f"q_packed{u}", [KROWS + MROWS, HP, N], BF16) for u in range(2)]
        k_packed = sb1("k_packed", [KROWS, HP, N], BF16)
        k_split = [sb1(f"k_split{u}", [KROWS + MROWS, HP, NW, 2, T], BF16) for u in range(2)]
        v_heads = [sb1(f"v_heads{u}", [128, NW, HP, VW]) for u in range(2)]
        neg_max = sb1("neg_max", [128, NH])
        neg_max_parts = sb1("neg_max_parts", [128, MROWS], BF16)
        probs = [sb1(f"probs{p}", [128, HP, TP]) for p in range(2)]
        o_sb = sb1("o_sb", [C, IM, 2 * NIT])
        o_rden = sb1("o_rden", [128, NI * NH])
        o_norm = sb1("o_norm", [128, NP * NH, HD])
        oT_sb = sb1("oT_sb", [C + 1, N])
        t1 = [sb1(f"t1_{u}", [128, NP, C]) for u in range(2)]
        ln1_stats = sb1("ln1_stats", [128, NP, 6])
        ln1_mv = sb1("ln1_mv", [128, NP, 2])
        ln1_var = sb1("ln1_var", [128, NP])
        ln1_rstd = sb1("ln1_rstd", [128, NP])
        h1 = sb1("h1", [128, NP, C])
        h1T = [sb1(f"h1T{u}", [C + 1, N]) for u in range(2)]
        kv_neg = sb1("kv_neg", [128, NP, 2 * C])
        kv_exp = sb1("kv_exp", [128, NP, 2 * C])
        feat = sb1("feat", [128, NP, 2 * C])
        attn_sb = sb1("attn_sb", [C, IM, C])
        attn_proj = sb1("attn_proj", [C, IM, C])
        fold_w = sb1("fold_w", [C + 1, IM, C])
        ln2_stats = sb1("ln2_stats", [128, NP, 6])
        ln2_mv = sb1("ln2_mv", [128, NP, 2])
        ln2_var = sb1("ln2_var", [128, NP])
        ln2_rstd = sb1("ln2_rstd", [128, NP])
        h2 = sb1("h2", [128, NP, C])
        h2T = sb1("h2T", [C + 1, N])
        phase1.close()

        mixT = sb("mixT", [128, 2, 128])
        mix_rows = [sb(f"mix_rows{u}", [C, FP, NE, 128]) for u in range(2)]
        in_parts = [[sb(f"in_part{n}_{u}", [C + 1, FT], F32R) for n in range(2)] for u in range(2)]
        hidden = [sb(f"hidden{n}", [128, FT]) for n in range(4)]
        hidden_parts = [[sb(f"hidden_part{p}_{n}", [128, FT], F32R) for p in range(2)] for n in range(4)]
        y_scaled = sb("y_scaled", [C, FT])
        y_acc = [sb(f"y_acc{u}", [C, FT]) for u in range(2)]
        out_sb = [sb(f"out_sb{u}", [128, FP, C]) for u in range(2)]
        mix_dram = nc.dram_tensor("mix_dram", [NPA, NE, 128], F32, kind="Internal").ap()

        parts_dram = nc.dram_tensor("parts_dram", [2, 2, PARTS, C, N], BF16, kind="Internal").ap()

        ps = ctx.enter_context(nc.psum_tensor("ps", [128, 8, 512], F32))
        FRONT, TAIL_A, TAIL_B, OUT_B = 0, 1, 2, 7
        S_BANKS, P_BANKS = 3, 5
        xT_ps = ps[0:C, FRONT, :]
        gmean_ps = ps[0:C, FRONT, 0:IM]
        gvar_ps = ps[0:C, FRONT, IM:2 * IM]
        qk_ps = ps[0:C, FRONT, :]
        v_ps = ps[:, FRONT, 0:NW * HP * HD].rearrange("p (w a d) -> p w a d", w=NW, d=HD)
        s_ps = ps[:, S_BANKS:S_BANKS + 2, 0:HP * T].rearrange("p b (h s) -> p b h s", s=T)
        pT_ps = ps[:, P_BANKS:P_BANKS + 2, 0:3 * TP]
        max_ps = ps[KROWS:KROWS + MROWS, P_BANKS, 3 * TP:3 * TP + TP // 2].bitcast(BF16)
        o_ps = ps[0:C, OUT_B, :]
        oT1_ps = ps[:, TAIL_A, 0:NI * NH * 16].rearrange("p (h d) -> p h d", d=16)
        oT2_ps = ps[0:C, TAIL_A, :]
        y0_ps = ps[:, TAIL_A, 0:NP * C].rearrange("p (q c) -> p q c", q=NP)
        h1T_ps = ps[0:C, TAIL_A, :]
        kv_ps = [ps[:, bank, 0:NI * 2 * C].rearrange("p (q c) -> p q c", q=NI) for bank in (TAIL_A, TAIL_B)]
        attn_ps = ps[0:C, TAIL_B, 0:IM * C].rearrange("p (i c) -> p i c", i=IM)
        aproj_ps = ps[0:C, TAIL_B, 0:IM * C].rearrange("p (i c) -> p i c", i=IM)
        fold_ps = ps[0:C + 1, TAIL_B, 0:IM * C].rearrange("p (i c) -> p i c", i=IM)
        y1_ps = ps[:, TAIL_B, 0:NP * C].rearrange("p (q c) -> p q c", q=NP)
        h2T_ps = ps[0:C, TAIL_B, :]
        gate_ps = ps[:, TAIL_B, 0:NP * NE].rearrange("p (q e) -> p q e", q=NP)
        up_ps = [ps[:, bank, :] for bank in (FRONT, S_BANKS, S_BANKS + 1, TAIL_A)]
        down_ps = [ps[0:C, P_BANKS + n, :] for n in range(2)]
        final_ps = ps[:, TAIL_B, 0:FP * C].rearrange("p (q c) -> p q c", q=FP)
        mixT_ps = ps[:, OUT_B, 0:TP]

        wqkv0_loaded = sem("wqkv0_loaded")
        lam_loaded = sem("lam_loaded")
        weights_loaded = sem("weights_loaded")
        experts_loaded = sem("experts_loaded")
        x_loaded = [sem(f"x_loaded{u}") for u in range(2)]
        parts_stored = sem("parts_stored")
        packed_loaded = sem("packed_loaded")
        mix_stored = sem("mix_stored")
        mix_loaded = [sem(f"mix_loaded{u}") for u in range(2)]
        out_stored = [sem(f"out_stored{u}") for u in range(2)]
        pool_const = sem("pool_const")
        zeros_set = sem("zeros_set")
        consts_ready = sem("consts_ready")
        setup_step = sem("setup_step")
        lam_sums = sem("lam_sums")
        lam_exps = sem("lam_exps")
        offs_sq_ready = sem("offs_sq_ready")
        gauss_ready = sem("gauss_ready")
        wq1T_ready = sem("wq1T_ready")
        lam_keep_ready = sem("lam_keep_ready")
        lam_col_ready = sem("lam_col_ready")
        lam_col_copied = sem("lam_col_copied")
        wq1T_copied = sem("wq1T_copied")
        wqk0_ready = sem("wqk0_ready")
        kpad_step = sem("kpad_step")
        kpad_loaded = sem("kpad_loaded")
        h2T_ones = sem("h2T_ones")
        ident_ready = sem("ident_ready")
        xT_ready = sem("xT_ready")
        xT_copied = sem("xT_copied")
        gn_stat_step = sem("gn_stat_step")
        gn_stats_ready = sem("gn_stats_ready")
        gmean_ready = sem("gmean_ready")
        gn_mean_ready = sem("gn_mean_ready")
        gn_dif_ready = sem("gn_dif_ready")
        gn_sq_ready = sem("gn_sq_ready")
        spread_ready = sem("spread_ready")
        gvar_ready = sem("gvar_ready")
        gn_var_ready = sem("gn_var_ready")
        gn_rstd_ready = sem("gn_rstd_ready")
        xh_ready = sem("xh_ready")
        x_kept = sem("x_kept")
        q_ready = sem("q_ready")
        q_part1 = sem("q_part1")
        q_rest = sem("q_rest")
        q_part2 = sem("q_part2")
        q_part3 = sem("q_part3")
        k_ready = sem("k_ready")
        k_part1 = sem("k_part1")
        k_rest = sem("k_rest")
        k_part2 = sem("k_part2")
        k_part3 = sem("k_part3")
        k_split_ready = sem("k_split_ready")
        v_ready = sem("v_ready")
        v_copied = sem("v_copied")
        scores_ready = sem("scores_ready")
        neg_max_ready = sem("neg_max_ready")
        max_part1 = sem("max_part1")
        max_part2 = sem("max_part2")
        max_ready = sem("max_ready")
        max_packed = sem("max_packed")
        shifted_ready = sem("shifted_ready")
        probs_ready = sem("probs_ready")
        pv_done = sem("pv_done")
        o_copied = sem("o_copied")
        oT1_ready = sem("oT1_ready")
        o_rden_ready = sem("o_rden_ready")
        o_norm_ready = sem("o_norm_ready")
        oT2_ready = sem("oT2_ready")
        oT_copied = sem("oT_copied")
        y0_ready = sem("y0_ready")
        t1_ready = sem("t1_ready")
        ln1_bn_ready = sem("ln1_bn_ready")
        ln1_mv_ready = sem("ln1_mv_ready")
        ln1_var_ready = sem("ln1_var_ready")
        ln1_rstd_ready = sem("ln1_rstd_ready")
        h1_ready = sem("h1_ready")
        h1T_ready = sem("h1T_ready")
        h1T_copied = sem("h1T_copied")
        kv_ready = sem("kv_ready")
        kv_neg_ready = sem("kv_neg_ready")
        kv_exp_ready = sem("kv_exp_ready")
        feat_ready = sem("feat_ready")
        attn_ready = sem("attn_ready")
        attn_masked = sem("attn_masked")
        aproj_ready = sem("aproj_ready")
        aproj_copied = sem("aproj_copied")
        fold_ready = sem("fold_ready")
        fold_copied = sem("fold_copied")
        y1_ready = sem("y1_ready")
        t2_ready = sem("t2_ready")
        ln2_bn_ready = sem("ln2_bn_ready")
        ln2_mv_ready = sem("ln2_mv_ready")
        ln2_var_ready = sem("ln2_var_ready")
        ln2_rstd_ready = sem("ln2_rstd_ready")
        h2_ready = sem("h2_ready")
        h2T_ready = sem("h2T_ready")
        h2T_copied = sem("h2T_copied")
        h2T_kept = sem("h2T_kept")
        gate_ready = sem("gate_ready")
        gate_copied = sem("gate_copied")
        g_step = sem("g_step")
        g_shift_ready = sem("g_shift_ready")
        g_exp_ready = sem("g_exp_ready")
        g_mix_ready = sem("g_mix_ready")
        mixT_ready = sem("mixT_ready")
        mixT_copied = sem("mixT_copied")
        weight_part1 = sem("weight_part1")
        weight_part2 = sem("weight_part2")
        in_part1 = sem("in_part1")
        in_part2 = sem("in_part2")
        up_ready = sem("up_ready")
        hidden_ready = sem("hidden_ready")
        hidden_part1 = sem("hidden_part1")
        hidden_part2 = sem("hidden_part2")
        down_done = sem("down_done")
        scaled_step = sem("scaled_step")
        final_ready = sem("final_ready")
        out_ready = sem("out_ready")

        blk = ctx.enter_context(nc.Block())

        def nth(k, u):
            return 2 * k + u + 1

        def met(eng):
            eng.wait_ge(pool_const, 22)

        def is_first(t):
            return isinstance(t, int) and t == 0

        def after(k, u, n):
            return k + (u + n) // 2, (u + n) % 2

        def flat_weights(n):
            pattern = ("p e n -> p (e n)", "p e c n -> p (e c n)")[n]
            parts_of = (up_parts, down_parts)[n]
            return [v.rearrange(pattern) for v in ((up_w, down_w)[n], parts_of[0][:], parts_of[1][:])]

        def schedule(eng, iteration, also=None):
            def one(b):
                iteration(b // 2, b % 2, b + 2 < NB, b + 1 < NB, b < NB, 1 <= b <= NB, b >= 2)
                if also and b == 1:
                    also()
            for b in range(2):
                one(b)
            with eng.Fori(1, NB // 2 - 1) as k:
                for u in range(2):
                    iteration(k, u, True, True, True, True, True)
            for b in range(NB - 2, NB + 1):
                one(b)

        @blk.sync
        def _(sp):
            def load(dst, src, s):
                sp.dma_start(dst, src).then_inc(s, 16)

            def load_block(dst, k, u, s):
                for im in range(IM):
                    for wr in range(NI):
                        for wc in range(2):
                            src = x[bass.ds(IM * (2 * k + u) + im, 1), wr * WS:(wr + 1) * WS, wc * WS:(wc + 1) * WS, :]
                            load(dst[wc * T:(wc + 1) * T, im * NI + wr, :], src.rearrange("b i j c -> (b i) j c"), s)

            def pack(k, u):
                n = nth(k, u)
                for s, part3 in enumerate((q_part3, k_part3)):
                    if s == 1:
                        if not is_first(k):
                            sp.wait_ge(shifted_ready, NP * (n - 2))
                        if not (is_first(k) and u == 0):
                            sp.wait_ge(k_split_ready, n - 1)
                    sp.wait_ge(part3, n)
                    sp.dma_start(parts_dram[u, s, :, :, :].rearrange("a c n -> c a n"), parts[s][:, :, :])\
                        .then_inc(parts_stored, 16)
                sp.wait_ge(parts_stored, 32 * n)
                half = SLOTS * HD
                for s, dst in enumerate((q_packed[u], k_packed)):
                    for part, slot, count in ((0, 0, 3), (1, 3, 2), (2, 5, 1)):
                        for odd in range(2):
                            src = parts_dram[u, s, :, odd * C // 2:(odd + 1) * C // 2, :]\
                                .rearrange("a (d h) n -> a d (h n)", d=HD)
                            src = src[part:part + 1].broadcast_to([count, HD, HP * N]) if s == 0 else src[0:count]
                            at = odd * half + slot * HD
                            load(dst[at:at + count * HD, :, :].rearrange("p h n -> p (h n)"), src, packed_loaded)

            load_block(x_in[0], 0, 0, x_loaded[0])
            load(wqkv0[0:C, :], w0, wqkv0_loaded)
            load(wqkv0[C:C + 1, :], b0.rearrange("(a n) -> a n", a=1), wqkv0_loaded)
            load_block(x_in[1], 0, 1, x_loaded[1])
            for n, a in enumerate((lk1, lv1, lk2, lv2)):
                load(lam_in[:, n, :], a, lam_loaded)
            sp.wait_ge(kpad_step, 3)
            for u in range(2):
                for hp in range(HP):
                    one = head_keys[:, hp, :, :].rearrange("p b s -> p (b s)").unsqueeze(1)
                    load(k_split[u][KROWS:KROWS + MROWS, hp, :, :, :].rearrange("p w b s -> p w (b s)"),
                         one.broadcast_to([MROWS, NW, 2 * T]), kpad_loaded)
            load(wproj0[0:C, :], wp0, weights_loaded)
            load(wproj0[C:C + 1, :], bp0.rearrange("(a n) -> a n", a=1), weights_loaded)
            load(wqkv1[0:C, :], w1a, weights_loaded)
            load(wqkv1[C:C + 1, :], b1a.rearrange("(a n) -> a n", a=1), weights_loaded)
            load(wproj1[:, :], wp1, weights_loaded)
            load(gate_w[0:C, :], gw, weights_loaded)
            load(gate_w[C:C + 1, :], gb.rearrange("(a n) -> a n", a=1), weights_loaded)
            sp.wait_ge(zeros_set, 3)
            load(bproj1[C:C + 1, :], bp1.rearrange("(a n) -> a n", a=1), weights_loaded)
            pack(0, 0)

            def fetch(k, u):
                met(sp)
                sp.wait_ge(x_kept, nth(k, u) - 2)
                sp.wait_ge(xT_ready, nth(k, u) - 2)
                load_block(x_in[u], k, u, x_loaded[u])

            fetch(1, 0)
            pack(0, 1)
            fetch(1, 1)
            load(up_w[0:C, :, :], ew1.rearrange("e c n -> c e n"), experts_loaded)
            load(up_w[C:C + 1, :, :], eb1.rearrange("(a e) n -> a e n", a=1), experts_loaded)
            load(down_w[:, :, :, :].rearrange("p e c n -> p (e c) n"),
                 ew2.rearrange("e (c p) n -> p (e c) n", p=128), experts_loaded)
            sp.dma_start(down_b[:, :], eb2.rearrange("e n -> n e"), allow_slow_non_contiguous=True)\
                .then_inc(experts_loaded, 16)

            with sp.Fori(1, NB // 2 - 1) as k:
                for u in range(2):
                    pack(k, u)
                    fetch(k + 1, u)
            pack(NB // 2 - 1, 0)
            pack(NB // 2 - 1, 1)

            def store_mix(half):
                sp.wait_ge(mixT_copied, half + 1)
                sp.dma_start(mix_dram[half * NPA // 2:(half + 1) * NPA // 2, :, :].rearrange("t e n -> (t e) n"),
                             mixT[:, half, :]).then_inc(mix_stored, 16)
                sp.wait_ge(mix_stored, 16 * (half + 1))

            def load_mix(t, u):
                src = mix_dram[bass.ds(t * FP, FP), :, :].rearrange("(a t) e n -> a (t e n)", a=1)
                load(mix_rows[u][:, :, :, :].rearrange("p t e n -> p (t e n)"), src.broadcast_to([C, FP * NE * 128]),
                     mix_loaded[u])

            def store(k, u):
                sp.wait_ge(out_ready, nth(k, u))
                for im in range(2):
                    for wc in range(2):
                        for wr in range(2):
                            dst = out[bass.ds(2 * (2 * k + u) + im, 1), wr * WS:(wr + 1) * WS,
                                      wc * WS:(wc + 1) * WS, :]
                            sp.dma_start(dst.rearrange("b i j c -> (b i) j c"),
                                         out_sb[u][wc * T:(wc + 1) * T, im * NI + wr, :]).then_inc(out_stored[u], 16)

            store_mix(0)
            load_mix(0, 0)
            load_mix(1, 1)
            for u in range(2):
                sp.wait_ge(scaled_step, 7 * (u + 1))
                load_mix(2 + u, u)
                store(0, u)
            store_mix(1)
            with sp.Fori(1, NFT // 2 - 1) as k:
                for u in range(2):
                    sp.wait_ge(scaled_step, 7 * nth(k, u))
                    load_mix(2 * k + u + 2, u)
                    store(k, u)
            for u in range(2):
                store(NFT // 2 - 1, u)
            for u in range(2):
                sp.wait_ge(out_stored[u], 16 * 8 * (NFT // 2))

        @blk.gpsimd
        def _(pool):
            pool.memset(ident[:, :], 0.0).then_inc(pool_const, 1)
            pool.memset(group_mean[:, :], 1.0 / GC).then_inc(pool_const, 1)
            pool.memset(head_of[:, :], 1.0).then_inc(pool_const, 1)
            pool.memset(head_rows[:, :], 1.0).then_inc(pool_const, 1)
            pool.memset(block[:, :], 1.0).then_inc(pool_const, 1)
            pool.memset(lower[:, :, :], 1.0).then_inc(pool_const, 1)
            pool.iota(offsets[:, :], pattern=[[-1, C]], base=0, channel_multiplier=1).then_inc(pool_const, 1)
            pool.memset(minus_half[:, :], -0.5).then_inc(pool_const, 1)
            pool.memset(ln_eps[:, :], LN_EPS).then_inc(pool_const, 1)
            pool.memset(pair_rows[:, :], 1.0).then_inc(pool_const, 1)
            pool.wait_ge(pool_const, 10)

            def keep(t, view, pattern, base, mult, n):
                pool.affine_select(out=view, in_=view, compare_op=ALU.is_ge, fill=0.0, base=base,
                                   pattern=pattern, channel_multiplier=mult).then_inc(pool_const, 1)

            pool.affine_select(out=ident[:, :], in_=ident[:, :], compare_op=ALU.not_equal, fill=1.0, base=0,
                               pattern=[[-1, 128]], channel_multiplier=1).then_inc(pool_const, 1)
            groups = group_mean[:, :].rearrange("p (g c) -> p g c", c=GC)
            blocks = block[:, :].rearrange("p (h d) -> p h d", d=HD)
            keep(group_mean, groups, [[-GC, C // GC], [0, GC]], 0, 1, 0)
            keep(head_of, head_of[:, :], [[-HD, NH]], 0, 1, 0)
            keep(head_rows, head_rows[:, :], [[1, C]], 0, -HD, 0)
            keep(block, blocks, [[-HD, NH], [0, HD]], 0, 1, 0)
            keep(lower, lower[:, :, :], [[1, NE], [-1, NE]], -1, 0, 0)
            keep(pair_rows, pair_rows[:, 0:1], [[0, 1]], KROWS // 2 - 1, -1, 0)
            keep(pair_rows, pair_rows[:, 1:2], [[0, 1]], -KROWS // 2, 1, 0)
            pool.wait_ge(pool_const, 18)
            keep(group_mean, groups, [[GC, C // GC], [0, GC]], GC - 1, -1, 0)
            keep(head_of, head_of[:, :], [[HD, NH]], HD - 1, -1, 0)
            keep(head_rows, head_rows[:, :], [[-1, C]], HD - 1, HD, 0)
            keep(block, blocks, [[HD, NH], [0, HD]], HD - 1, -1, 0)
            pool.wait_ge(pool_const, 22)
            pool.memset(xh[0][C:C + 1, :], 1.0).then_inc(consts_ready, 1)
            pool.memset(xh[1][C:C + 1, :], 1.0).then_inc(consts_ready, 1)
            pool.memset(oT_sb[C:C + 1, :], 1.0).then_inc(consts_ready, 1)
            pool.memset(h1T[0][C:C + 1, :], 1.0).then_inc(consts_ready, 1)
            pool.memset(h1T[1][C:C + 1, :], 1.0).then_inc(consts_ready, 1)
            pool.memset(h2T[C:C + 1, :], 1.0).then_inc(consts_ready, 1)
            pool.memset(head_keys[:, :, :, :], 0.0).then_inc(kpad_step, 1)
            for part in range(2):
                pool.wait_ge(kpad_step, part + 1)
                pool.affine_select(out=head_keys[:, :, :, :], in_=head_keys[:, :, :, :], compare_op=ALU.not_equal,
                                   fill=1.0, base=-part * NH, pattern=[[-2, HP], [-1, 2], [0, T]],
                                   channel_multiplier=1).then_inc(kpad_step, 1)

            def gn_rstd_of(k, u):
                pool.wait_ge(gn_var_ready, nth(k, u))
                pool.tensor_tensor(gn_rstd[:, :], gn_var[:, :], minus_half[0:C, 0:IM], ALU.pow)\
                    .then_inc(gn_rstd_ready, 1)

            def third_part(k, u, s):
                pool.wait_ge((q_part2, k_part2)[s], nth(k, u))
                pool.tensor_tensor(parts[s][:, 2, :], rest[s][:, :], parts[s][:, 1, :], ALU.subtract)\
                    .then_inc((q_part3, k_part3)[s], 1)

            def ln_rstd(k, u, mv, var, rstd, mv_ready, var_ready, rstd_ready):
                pool.wait_ge(mv_ready, nth(k, u))
                pool.tensor_tensor(var[:, :], mv[:, :, 1], ln_eps[:, :], ALU.add).then_inc(var_ready, 1)
                pool.wait_ge(var_ready, nth(k, u))
                pool.tensor_tensor(rstd[:, :], var[:, :], minus_half[:, :], ALU.pow).then_inc(rstd_ready, 1)

            def input_parts(t, u):
                first, second = in_parts[u]
                pool.wait_ge(in_part1, t + 1)
                pool.tensor_tensor(second[:, :], h2T_all[:, bass.ds(t * FT, FT)], first[:, :].bitcast(F32),
                                   ALU.subtract).then_inc(in_part2, 1)

            def iteration(k, u, ahead2, ahead1, here, back1, back2):
                if ahead1:
                    third_part(*after(k, u, 1), 0)
                    third_part(*after(k, u, 1), 1)
                if back1 and not here:
                    input_parts(0, 0)
                    input_parts(1, 1)
                if ahead2:
                    gn_rstd_of(*after(k, u, 2))
                if back2:
                    ln_rstd(*after(k, u, -2), ln2_mv, ln2_var, ln2_rstd, ln2_mv_ready, ln2_var_ready, ln2_rstd_ready)
                if back1:
                    ln_rstd(*after(k, u, -1), ln1_mv, ln1_var, ln1_rstd, ln1_mv_ready, ln1_var_ready, ln1_rstd_ready)
                if back2:
                    kb, ub = after(k, u, -2)
                    pool.wait_ge(h2T_copied, nth(kb, ub))
                    pool.tensor_copy(h2T_all[0:C, bass.ds((2 * kb + ub) * N, N)], h2T[0:C, :]).then_inc(h2T_kept, 1)

            def weight_second_part(n):
                w, first, second = flat_weights(n)
                pool.wait_ge(weight_part1, n + 1)
                pool.tensor_tensor(second, w, first.bitcast(F32), ALU.subtract).then_inc(weight_part2, 1)

            gn_rstd_of(0, 0)
            pool.memset(h2T_all[C:C + 1, :], 1.0).then_inc(h2T_ones, 1)
            third_part(0, 0, 0)
            third_part(0, 0, 1)
            gn_rstd_of(0, 1)
            schedule(pool, iteration, lambda: (weight_second_part(0), weight_second_part(1)))
            iteration(NB // 2, 1, False, False, False, False, True)
            with pool.Fori(1, NFT // 2) as k:
                for u in range(2):
                    input_parts(2 * k + u, u)

        @blk.tensor
        def _(pe):
            def x_transpose(k, u):
                pe.wait_ge(x_loaded[u], 16 * 2 * NP * (k + 1))
                pe.wait_ge(v_copied, 2 * (nth(k, u) - 1))
                for p in range(NP):
                    last = pe.transpose(xT_ps[:, p * TP:(p + 1) * TP], x_in[u][:, p, :], ident[:, :])
                last.then_inc(xT_ready, 1)

            def gmean(k, u):
                pe.wait_ge(gn_stats_ready, nth(k, u))
                pe.matmul(gmean_ps, group_mean[:, :], gn_mv[:, :, 0], start=True, stop=True).then_inc(gmean_ready, 1)

            def gvar(k, u):
                pe.wait_ge(spread_ready, nth(k, u))
                pe.matmul(gvar_ps, group_mean[:, :], gn_spread[:, :], start=True, stop=True).then_inc(gvar_ready, 1)

            def q_proj(k, u):
                pe.wait_ge(xh_ready, nth(k, u))
                pe.matmul(qk_ps, wqk0[:, 0, :], xh[u][:, :], start=True, stop=True).then_inc(q_ready, 1)

            def k_proj(k, u):
                pe.wait_ge(q_rest, nth(k, u))
                pe.matmul(qk_ps, wqk0[:, 1, :], xh[u][:, :], start=True, stop=True).then_inc(k_ready, 1)

            def v_proj(k, u, half):
                pe.wait_ge(k_rest, nth(k, u))
                if half:
                    pe.wait_ge(v_copied, 2 * nth(k, u) - 1)
                wv = wqkv0[:, 2 * C:3 * C].rearrange("p (a b d) -> p a b d", b=2, d=HD)
                for w in range(half * NWI, (half + 1) * NWI):
                    for odd in range(2):
                        last = pe.matmul(v_ps[odd * T:(odd + 1) * T, w, :, :], xh[u][:, w * T:(w + 1) * T],
                                         wv[:, :, odd, :], start=True, stop=True)
                last.then_inc(v_ready, 1)

            def scores_of(k, u, p):
                done = NP * (2 * k + u) + p
                if p == 0:
                    pe.wait_ge(k_split_ready, nth(k, u))
                    pe.wait_ge(packed_loaded, 16 * 12 * nth(k, u))
                pe.wait_ge(neg_max_ready, done)
                for w2 in range(2):
                    w = 2 * p + w2
                    for hp in range(HP):
                        last = pe.matmul(s_ps[w2 * T:(w2 + 1) * T, hp // 3, 2 * (hp % 3):2 * (hp % 3) + 2, :],
                                         q_packed[u][0:KROWS, hp, w * T:(w + 1) * T],
                                         k_split[u][0:KROWS, hp, w, :, :], start=True, stop=True)
                last.then_inc(scores_ready, 1)

            def max_transpose(k, u, p):
                done = NP * (2 * k + u) + p
                pe.wait_ge(max_part2, done + 1)
                pe.wait_ge(probs_ready, done)
                pe.transpose(max_ps, neg_max_parts[:, :], ident_b[:, :]).then_inc(max_ready, 1)

            def shifted_scores(k, u, p):
                pe.wait_ge(max_packed, NP * (2 * k + u) + p + 1)
                if is_first(k) and u == 0 and p == 0:
                    pe.wait_ge(kpad_loaded, 16 * 2 * HP)
                for hp in range(HP):
                    for w2 in range(2):
                        w = 2 * p + w2
                        at = (hp % 3) * TP + w2 * T
                        last = pe.matmul(pT_ps[:, hp // 3, at:at + T],
                                         k_split[u][:, hp, w, :, :].rearrange("p b s -> p (b s)"),
                                         q_packed[u][:, hp, w * T:(w + 1) * T], start=True, stop=True)
                last.then_inc(shifted_ready, 1)

            def pv(k, u, p):
                done = NP * (2 * k + u) + p
                pe.wait_ge(probs_ready, done + 1)
                pe.wait_ge(v_copied, 2 * (2 * k + u) + p // NI + 1)
                if p % NI == 0:
                    pe.wait_ge(o_copied, IM * (2 * k + u) + p // NI)
                for w2 in range(2):
                    w = 2 * p + w2
                    at = (w % NWI) * T
                    for hp in range(HP):
                        g, r = hp % 3, hp // 3
                        last = pe.matmul(o_ps[g * VW:(g + 1) * VW, r * NIT + at:r * NIT + at + T],
                                         v_heads[u][:, w, hp, :], probs[p % 2][:, hp, w2 * T:(w2 + 1) * T],
                                         start=True, stop=True)
                last.then_inc(pv_done, 1)

            def oT1(k, u, im):
                done = IM * (2 * k + u) + im
                pe.wait_ge(o_copied, done + 1)
                if im:
                    pe.wait_ge(o_norm_ready, done)
                elif not (is_first(k) and u == 0):
                    pe.wait_ge(feat_ready, done - 1)
                for p in range(NI):
                    for r in range(2):
                        last = pe.transpose(ps[:, TAIL_A, (2 * p + r) * C:(2 * p + r + 1) * C],
                                            o_sb[:, im, r * NIT + p * TP:r * NIT + (p + 1) * TP], ident[0:C, 0:C])
                last.then_inc(oT1_ready, 1)

            def oT2(k, u):
                pe.wait_ge(o_norm_ready, IM * nth(k, u))
                for p in range(NP):
                    last = pe.transpose(oT2_ps[:, p * TP:(p + 1) * TP],
                                        o_norm[:, p * NH:(p + 1) * NH, :].rearrange("p h d -> p (h d)"), ident[:, :])
                last.then_inc(oT2_ready, 1)

            def y0(k, u):
                pe.wait_ge(oT_copied, nth(k, u))
                for p in range(NP):
                    last = pe.matmul(y0_ps[:, p, :], oT_sb[:, p * TP:(p + 1) * TP], wproj0[:, :],
                                     start=True, stop=True)
                last.then_inc(y0_ready, 1)

            def h1_transpose(k, u):
                pe.wait_ge(h1_ready, nth(k, u))
                for p in range(NP):
                    last = pe.transpose(h1T_ps[:, p * TP:(p + 1) * TP], h1[:, p, :], ident[:, :])
                last.then_inc(h1T_ready, 1)

            def kv(k, u, im):
                pe.wait_ge(h1T_copied, nth(k, u))
                if im:
                    pe.wait_ge(gate_copied, nth(k, u) - 1)
                for p in range(NI):
                    at = (im * NI + p) * TP
                    last = pe.matmul(kv_ps[im][:, p, :], h1T[u][:, at:at + TP], wqkv1[:, C:3 * C],
                                     start=True, stop=True)
                last.then_inc(kv_ready, 1)

            def attn_sum(k, u):
                pe.wait_ge(feat_ready, IM * nth(k, u))
                for im in range(IM):
                    for p in range(NI):
                        f = feat[:, im * NI + p, :]
                        last = pe.matmul(attn_ps[:, im, :], f[:, C:2 * C], f[:, 0:C], start=p == 0, stop=p == NI - 1)
                last.then_inc(attn_ready, 1)

            def attn_times_proj(k, u):
                pe.wait_ge(attn_masked, nth(k, u))
                for im in range(IM):
                    last = pe.matmul(aproj_ps[:, im, :], attn_sb[:, im, :], wproj1[:, :], start=True, stop=True)
                last.then_inc(aproj_ready, 1)

            def fold(k, u):
                pe.wait_ge(aproj_copied, nth(k, u))
                pe.matmul(fold_ps, wq1T[:, :], attn_proj[:, :, :], start=True, stop=True).then_inc(fold_ready, 1)

            def y1(k, u):
                pe.wait_ge(fold_copied, nth(k, u))
                for p in range(NP):
                    last = pe.matmul(y1_ps[:, p, :], h1T[u][:, p * TP:(p + 1) * TP], fold_w[:, p // NI, :],
                                     start=True, stop=True)
                last.then_inc(y1_ready, 1)

            def h2_transpose(k, u):
                pe.wait_ge(h2_ready, nth(k, u))
                for p in range(NP):
                    last = pe.transpose(h2T_ps[:, p * TP:(p + 1) * TP], h2[:, p, :], ident[:, :])
                last.then_inc(h2T_ready, 1)

            def gate(k, u):
                pe.wait_ge(h2T_copied, nth(k, u))
                for p in range(NP):
                    last = pe.matmul(gate_ps[:, p, :], h2T[:, p * TP:(p + 1) * TP], gate_w[:, :],
                                     start=True, stop=True)
                last.then_inc(gate_ready, 1)

            def product(out, w_parts, x_parts, start, stop):
                pe.matmul(out, w_parts[0], x_parts[0], start=start, stop=False)
                pe.matmul(out, w_parts[1], x_parts[0], start=False, stop=False)
                return pe.matmul(out, w_parts[0], x_parts[1], start=False, stop=stop)

            def up(t, u, n):
                e, c = n // CH, n % CH
                if n == 0:
                    pe.wait_ge(in_part2, t + 1)
                if is_first(t) and n == 0:
                    pe.wait_ge(weight_part2, 2)
                if n >= 4 or not is_first(t):
                    pe.wait_ge(hidden_part1, t * NE * CH + n - 3)
                product(up_ps[n % 4], [w[:, e, c * 128:(c + 1) * 128] for w in up_parts],
                        [h[:, :] for h in in_parts[u]], True, True).then_inc(up_ready, 1)

            def iteration(k, u, ahead2, ahead1, here, back1, back2):
                two_on, one_on, one_back, two_back = [after(k, u, n) for n in (2, 1, -1, -2)]

                def when(there, step, *args):
                    if there:
                        step(*args)

                when(here, scores_of, k, u, 0)
                when(back2, kv, *two_back, 1)
                when(ahead1, v_proj, *one_on, 0)
                when(back1, pv, *one_back, 3)
                when(here, scores_of, k, u, 1)
                when(here, max_transpose, k, u, 0)
                when(back1, oT1, *one_back, 0)
                when(ahead1, v_proj, *one_on, 1)
                when(here, scores_of, k, u, 2)
                when(back2, attn_sum, *two_back)
                when(ahead2, x_transpose, *two_on)
                when(back1, oT1, *one_back, 1)
                when(here, shifted_scores, k, u, 0)
                when(back2, attn_times_proj, *two_back)
                when(here, scores_of, k, u, 3)
                when(here, max_transpose, k, u, 1)
                when(back2, fold, *two_back)
                when(back1, oT2, *one_back)
                when(ahead2, gmean, *two_on)
                when(back2, y1, *two_back)
                when(ahead2, gvar, *two_on)
                when(here, shifted_scores, k, u, 1)
                when(back1, y0, *one_back)
                when(here, max_transpose, k, u, 2)
                when(here, pv, k, u, 0)
                when(here, shifted_scores, k, u, 2)
                when(here, pv, k, u, 1)
                when(ahead2, q_proj, *two_on)
                when(back2, h2_transpose, *two_back)
                when(here, max_transpose, k, u, 3)
                when(here, pv, k, u, 2)
                when(back1, h1_transpose, *one_back)
                when(back2, gate, *two_back)
                when(ahead2, k_proj, *two_on)
                when(here, shifted_scores, k, u, 3)
                when(back1, kv, *one_back, 0)

            pe.wait_ge(pool_const, 22)
            x_transpose(0, 0)
            gmean(0, 0)
            gvar(0, 0)
            pe.wait_ge(consts_ready, 6)
            pe.wait_ge(wqk0_ready, 1)
            q_proj(0, 0)
            k_proj(0, 0)
            v_proj(0, 0, 0)
            v_proj(0, 0, 1)
            pe.wait_ge(lam_keep_ready, 1)
            pe.matmul(ps[0:C, TAIL_B, 0:1], head_rows[:, :], lam_keep[:, :], start=True, stop=True)\
                .then_inc(lam_col_ready, 1)
            x_transpose(0, 1)
            gmean(0, 1)
            gvar(0, 1)
            q_proj(0, 1)
            pe.wait_ge(weights_loaded, 16 * 8)
            pe.transpose(ps[0:C, TAIL_A, 0:C + 1], wqkv1[:, 0:C], ident[0:C + 1, 0:C + 1]).then_inc(wq1T_ready, 1)
            k_proj(0, 1)
            pe.wait_ge(ident_ready, 1)
            pe.wait_ge(wq1T_copied, 1)
            pe.wait_ge(lam_col_copied, 1)
            schedule(pe, iteration)

            def down(t, n):
                e, c = n // CH, n % CH
                pe.wait_ge(hidden_part2, t * NE * CH + n + 1)
                if c == 0 and (e >= 2 or not is_first(t)):
                    step = (1, 2, 4, 6)[(e + 2) % 4]
                    pe.wait_ge(scaled_step, 7 * t + step - (7 if e < 2 else 0))
                product(down_ps[e % 2], [w[:, e, c, :] for w in down_parts], [h[:, :] for h in hidden_parts[n % 4]],
                        c == 0, c == CH - 1).then_inc(down_done, 1)

            def final(t, u):
                pe.wait_ge(scaled_step, 7 * (t + 1))
                if not is_first(t):
                    pe.wait_ge(out_ready, t)
                for p in range(FP):
                    last = pe.transpose(final_ps[:, p, :], y_acc[u][:, p * TP:(p + 1) * TP], ident[0:C, 0:C])
                last.then_inc(final_ready, 1)

            def mix_transpose(half):
                pe.wait_ge(g_mix_ready, half + 1)
                pe.transpose(mixT_ps, g_mix[:, half * 128:(half + 1) * 128], ident[:, :]).then_inc(mixT_ready, 1)

            def first_tile():
                last_block = (NB // 2 - 1, 1)
                kv(*last_block, 1)
                for n in range(NE * CH):
                    up(0, 0, n)
                    if n == 0:
                        attn_sum(*last_block)
                    if n == 1:
                        attn_times_proj(*last_block)
                        mix_transpose(0)
                    if n == 2:
                        fold(*last_block)
                    if n == 4:
                        y1(*last_block)
                    if n == 7:
                        h2_transpose(*last_block)
                    if n == 8:
                        gate(*last_block)
                    if n >= LAG:
                        down(0, n - LAG)

            def tile(t, u, second):
                for n in range(NE * CH):
                    up(t, u, n)
                    if n >= LAG:
                        down(t, n - LAG)
                    else:
                        down(t - 1, n - LAG + NE * CH)
                    if n == 6:
                        final(t - 1, 1 - u)
                    if n == 10 and second:
                        mix_transpose(1)

            pe.wait_ge(probs_ready, NB * NP)
            pe.wait_ge(v_copied, NB * IM)
            first_tile()
            tile(1, 1, True)
            with pe.Fori(1, NFT // 2) as k:
                for u in range(2):
                    tile(2 * k + u, u, False)
            for n in range(NE * CH - LAG, NE * CH):
                down(NFT - 1, n)
            final(NFT - 1, 1)

        @blk.scalar
        def _(act):
            def weight_first_part(n):
                w, first, _ = flat_weights(n)
                act.wait_ge(experts_loaded, 16 * 4)
                act.activation(first, w, ACT.Copy).then_inc(weight_part1, 1)

            def copy_xT(k, u):
                act.wait_ge(xT_ready, nth(k, u))
                act.wait_ge(xh_ready, nth(k, u) - 1)
                act.activation(xT[:, :], xT_ps, ACT.Copy).then_inc(xT_copied, 1)

            def first_part(k, u, s):
                act.wait_ge((q_ready, k_ready)[s], nth(k, u))
                act.wait_ge(parts_stored, 32 * (nth(k, u) - 1))
                act.activation(parts[s][:, 0, :], qk_ps, ACT.Copy).then_inc((q_part1, k_part1)[s], 1)

            def second_part(k, u, s):
                act.wait_ge((q_rest, k_rest)[s], nth(k, u))
                act.activation(parts[s][:, 1, :], rest[s][:, :], ACT.Copy).then_inc((q_part2, k_part2)[s], 1)

            def copy_v(k, u, half):
                act.wait_ge(v_ready, 2 * (2 * k + u) + half + 1)
                if not is_first(k):
                    act.wait_ge(pv_done, NP * (nth(k, u) - 2))
                ws = slice(half * NWI, (half + 1) * NWI)
                for odd in range(2):
                    last = act.activation(v_heads[u][odd * T:(odd + 1) * T, ws, :, odd * 16:odd * 16 + HD],
                                          v_ps[odd * T:(odd + 1) * T, ws, :, :], ACT.Copy)
                last.then_inc(v_copied, 1)

            def pack_max(k, u, p):
                act.wait_ge(max_ready, NP * (2 * k + u) + p + 1)
                act.activation(q_packed[u][KROWS:KROWS + MROWS, :, p * TP:(p + 1) * TP],
                               max_ps.unsqueeze(1).broadcast_to([MROWS, HP, TP]), ACT.Copy).then_inc(max_packed, 1)

            def exp_probs(k, u, p):
                done = NP * (2 * k + u) + p
                act.wait_ge(shifted_ready, done + 1)
                if not (is_first(k) and u == 0 and p < 2):
                    act.wait_ge(pv_done, done - 1)
                act.activation(probs[p % 2][:, :, :].rearrange("p (b h) t -> p b (h t)", b=2), pT_ps, ACT.Exp,
                               scale=SCALE).then_inc(probs_ready, 1)

            def copy_o(k, u, im):
                done = IM * (2 * k + u) + im
                act.wait_ge(pv_done, NI * (done + 1))
                if not (is_first(k) and u == 0):
                    act.wait_ge(oT1_ready, done - 1)
                act.activation(o_sb[:, im, :], o_ps, ACT.Copy).then_inc(o_copied, 1)

            def copy_oT(k, u):
                act.wait_ge(oT2_ready, nth(k, u))
                act.wait_ge(y0_ready, nth(k, u) - 1)
                act.activation(oT_sb[0:C, :], oT2_ps, ACT.Copy).then_inc(oT_copied, 1)

            def copy_h1T(k, u):
                act.wait_ge(h1T_ready, nth(k, u))
                if not is_first(k):
                    act.wait_ge(y1_ready, nth(k, u) - 2)
                act.activation(h1T[u][0:C, :], h1T_ps, ACT.Copy).then_inc(h1T_copied, 1)

            def keep_x(k, u):
                act.wait_ge(x_loaded[u], 16 * 2 * NP * (k + 1))
                if not is_first(k):
                    act.wait_ge(t1_ready, nth(k, u) - 2)
                act.activation(x_res[u][:, :, :], x_in[u][:, :, :], ACT.Copy).then_inc(x_kept, 1)

            def exp_kv(k, u, im):
                done = IM * (2 * k + u) + im
                act.wait_ge(kv_neg_ready, done + 1)
                act.wait_ge(feat_ready, IM * (2 * k + u))
                pairs = slice(im * NI, (im + 1) * NI)
                act.activation(kv_exp[:, pairs, :], kv_neg[:, pairs, :], ACT.Exp).then_inc(kv_exp_ready, 1)

            def copy_aproj(k, u):
                act.wait_ge(aproj_ready, nth(k, u))
                act.wait_ge(fold_ready, nth(k, u) - 1)
                act.activation(attn_proj[:, :, :], aproj_ps, ACT.Copy).then_inc(aproj_copied, 1)

            def copy_h2T(k, u):
                act.wait_ge(h2T_ready, nth(k, u))
                act.wait_ge(gate_ready, nth(k, u) - 1)
                act.wait_ge(h2T_kept, nth(k, u) - 1)
                act.activation(h2T[0:C, :], h2T_ps, ACT.Copy).then_inc(h2T_copied, 1)

            def input_part(t, u):
                if is_first(t):
                    act.wait_ge(h2T_kept, 2)
                    act.wait_ge(h2T_ones, 1)
                if not (isinstance(t, int) and t < 2):
                    act.wait_ge(up_ready, (t - 1) * NE * CH)
                act.activation(in_parts[u][0][:, :], h2T_all[:, bass.ds(t * FT, FT)], ACT.Copy).then_inc(in_part1, 1)

            def exp_gate(group):
                act.wait_ge(g_shift_ready, group + 1)
                pairs = GATE_GROUPS[group]
                act.activation(g_exp[:, pairs, :], g_shift[:, pairs, :], ACT.Exp).then_inc(g_exp_ready, 1)

            def iteration(k, u, ahead2, ahead1, here, back1, back2):
                two_on, one_on, one_back, two_back = [after(k, u, n) for n in (2, 1, -1, -2)]

                drained = back1 and not here

                def when(there, step, *args):
                    if there:
                        step(*args)

                when(back1, exp_probs, *one_back, 3)
                when(back2, exp_kv, *two_back, 0)
                when(ahead1, second_part, *one_on, 0)
                when(ahead1, second_part, *one_on, 1)
                when(ahead1, copy_v, *one_on, 0)
                when(back2, exp_kv, *two_back, 1)
                when(here, pack_max, k, u, 0)
                when(ahead1, copy_v, *one_on, 1)
                when(back1, copy_o, *one_back, 1)
                when(drained, exp_gate, 0)
                when(drained, input_part, 0, 0)
                when(drained, input_part, 1, 1)
                when(ahead2, copy_xT, *two_on)
                when(here, exp_probs, k, u, 0)
                when(back2, copy_aproj, *two_back)
                when(here, pack_max, k, u, 1)
                when(back1, copy_oT, *one_back)
                when(here, exp_probs, k, u, 1)
                when(here, pack_max, k, u, 2)
                when(here, exp_probs, k, u, 2)
                when(ahead1, keep_x, *one_on)
                when(here, copy_o, k, u, 0)
                when(ahead2, first_part, *two_on, 0)
                when(back2, copy_h2T, *two_back)
                when(here, pack_max, k, u, 3)
                when(back1, copy_h1T, *one_back)
                when(ahead2, first_part, *two_on, 1)

            copy_xT(0, 0)
            for s in range(2):
                first_part(0, 0, s)
                second_part(0, 0, s)
            act.wait_ge(lam_sums, 1)
            act.activation(lam_exp[:, :], lam_sum[:, :], ACT.Exp).then_inc(lam_exps, 1)
            act.wait_ge(offs_sq_ready, 1)
            act.activation(gauss[:, :], offsets_sq[:, :], ACT.Exp, scale=-2.0).then_inc(gauss_ready, 1)
            act.wait_ge(zeros_set, 3)
            copy_v(0, 0, 0)
            copy_v(0, 0, 1)
            copy_xT(0, 1)
            first_part(0, 1, 0)
            first_part(0, 1, 1)
            act.wait_ge(wq1T_ready, 1)
            act.activation(wq1T[:, :], ps[0:C, TAIL_A, 0:C + 1], ACT.Copy, scale=SCALE).then_inc(wq1T_copied, 1)
            keep_x(0, 0)
            schedule(act, iteration, lambda: (weight_first_part(0), weight_first_part(1)))

            def tile(t, u):
                for n in range(NE * CH):
                    act.wait_ge(up_ready, t * NE * CH + n + 1)
                    if n >= 4 or not is_first(t):
                        act.wait_ge(down_done, t * NE * CH + n - 3)
                    act.activation(hidden[n % 4][:, :], up_ps[n % 4], ACT.Gelu).then_inc(hidden_ready, 1)
                    act.activation(hidden_parts[n % 4][0][:, :], up_ps[n % 4], ACT.Gelu).then_inc(hidden_part1, 1)
                    if is_first(t) and n == 1:
                        copy_aproj(*last_block)
                    if is_first(t) and n == 7:
                        copy_h2T(*last_block)
                    if isinstance(t, int) and t == 1 and n == 1:
                        exp_gate(1)
                    if n == 3 and not (isinstance(t, int) and (t == 0 or t == NFT - 1)):
                        input_part(t + 1, 1 - u)

            last_block = (NB // 2 - 1, 1)
            exp_kv(*last_block, 0)
            exp_kv(*last_block, 1)
            tile(0, 0)
            act.wait_ge(h2T_kept, NB)
            tile(1, 1)
            with act.Fori(1, NFT // 2 - 1) as k:
                for u in range(2):
                    tile(2 * k + u, u)
            tile(NFT - 2, 0)
            tile(NFT - 1, 1)

        @blk.vector
        def _(dve):
            def gn_stats_of(k, u):
                dve.wait_ge(xT_copied, nth(k, u))
                for im in range(IM):
                    last = dve.bn_stats(gn_stats[:, im, :], xT[:, im * NIT:(im + 1) * NIT])
                last.then_inc(gn_stat_step, 1)
                met(dve)
                dve.wait_ge(gn_stat_step, nth(k, u))
                for im in range(IM):
                    last = dve.bn_aggr(gn_mv[:, im, :], gn_stats[:, im, :])
                last.then_inc(gn_stats_ready, 1)

            def gn_spread_of(k, u):
                dve.wait_ge(gmean_ready, nth(k, u))
                dve.tensor_copy(gn_mean[:, :], gmean_ps).then_inc(gn_mean_ready, 1)
                dve.wait_ge(gn_mean_ready, nth(k, u))
                dve.tensor_tensor(gn_dif[:, :], gn_mv[:, :, 0], gn_mean[:, :], ALU.subtract).then_inc(gn_dif_ready, 1)
                dve.wait_ge(gn_dif_ready, nth(k, u))
                dve.tensor_tensor(gn_sq[:, :], gn_dif[:, :], gn_dif[:, :], ALU.mult).then_inc(gn_sq_ready, 1)
                dve.wait_ge(gn_sq_ready, nth(k, u))
                dve.tensor_tensor(gn_spread[:, :], gn_sq[:, :], gn_mv[:, :, 1], ALU.add).then_inc(spread_ready, 1)

            def gn_var_of(k, u):
                dve.wait_ge(gvar_ready, nth(k, u))
                dve.tensor_scalar(gn_var[:, :], gvar_ps, GN_EPS, None, ALU.add).then_inc(gn_var_ready, 1)

            def gn_apply(k, u):
                dve.wait_ge(gn_rstd_ready, nth(k, u))
                if not is_first(k):
                    dve.wait_ge(v_ready, 2 * (nth(k, u) - 2))
                for im in range(IM):
                    cols = slice(im * NIT, (im + 1) * NIT)
                    last = dve.tensor_scalar(xh[u][0:C, cols], xT[:, cols], gn_mean[:, im:im + 1],
                                             gn_rstd[:, im:im + 1], ALU.subtract, ALU.mult)
                last.then_inc(xh_ready, 1)

            def rest_of(k, u, s):
                dve.wait_ge((q_part1, k_part1)[s], nth(k, u))
                dve.wait_ge((q_part3, k_part3)[s], nth(k, u) - 1)
                dve.tensor_tensor(rest[s][:, :], qk_ps, parts[s][:, 0, :], ALU.subtract)\
                    .then_inc((q_rest, k_rest)[s], 1)

            def split_keys(k, u):
                dve.wait_ge(packed_loaded, 16 * 12 * nth(k, u))
                if not is_first(k):
                    dve.wait_ge(shifted_ready, NP * (nth(k, u) - 2))
                src = k_packed[:, :, :].rearrange("p h (w s) -> p (h w) s", s=T)
                dst = k_split[u][0:KROWS, :, :, :, :].rearrange("p h w b s -> p (h w) b s")
                for odd in range(2):
                    last = dve.tensor_scalar(dst[:, :, odd, :], src, pair_rows[:, odd:odd + 1], None, ALU.mult)
                last.then_inc(k_split_ready, 1)

            def maxima(k, u, p):
                done = NP * (2 * k + u) + p
                dve.wait_ge(scores_ready, done + 1)
                dve.wait_ge(max_part2, done)
                dve.tensor_reduce(neg_max[:, :].rearrange("p (b h) -> p b h", b=2), s_ps, AX.X, ALU.max, negate=True)\
                    .then_inc(neg_max_ready, 1)

            def max_parts(k, u, p):
                done = NP * (2 * k + u) + p
                dve.wait_ge(neg_max_ready, done + 1)
                dve.wait_ge(max_ready, done)
                dve.tensor_copy(neg_max_parts[:, 0:NH], neg_max[:, :]).then_inc(max_part1, 1)
                dve.wait_ge(max_part1, done + 1)
                dve.tensor_tensor(neg_max_parts[:, NH:2 * NH], neg_max[:, :], neg_max_parts[:, 0:NH], ALU.subtract)\
                    .then_inc(max_part2, 1)

            def normalise(k, u, im):
                done = IM * (2 * k + u) + im
                dve.wait_ge(oT1_ready, done + 1)
                dve.reciprocal(o_rden[:, :], oT1_ps[:, :, HD]).then_inc(o_rden_ready, 1)
                dve.wait_ge(o_rden_ready, done + 1)
                dve.wait_ge(oT2_ready, nth(k, u) - 1)
                dve.tensor_tensor(o_norm[:, im * NI * NH:(im + 1) * NI * NH, :], oT1_ps[:, :, 0:HD],
                                  o_rden[:, :].unsqueeze(2).broadcast_to([128, NI * NH, HD]), ALU.mult)\
                    .then_inc(o_norm_ready, 1)

            def residual1(k, u):
                dve.wait_ge(y0_ready, nth(k, u))
                dve.wait_ge(x_kept, nth(k, u))
                dve.tensor_tensor(t1[u][:, :, :], y0_ps, x_res[u][:, :, :], ALU.add).then_inc(t1_ready, 1)
                dve.wait_ge(t1_ready, nth(k, u))
                for p in range(NP):
                    last = dve.bn_stats(ln1_stats[:, p, :], t1[u][:, p, :])
                last.then_inc(ln1_bn_ready, 1)
                met(dve)
                dve.wait_ge(ln1_bn_ready, nth(k, u))
                for p in range(NP):
                    last = dve.bn_aggr(ln1_mv[:, p, :], ln1_stats[:, p, :])
                last.then_inc(ln1_mv_ready, 1)

            def norm1(k, u):
                dve.wait_ge(ln1_rstd_ready, nth(k, u))
                dve.wait_ge(h1T_ready, nth(k, u) - 1)
                for p in range(NP):
                    last = dve.tensor_scalar(h1[:, p, :], t1[u][:, p, :], ln1_mv[:, p, 0:1], ln1_rstd[:, p:p + 1],
                                             ALU.subtract, ALU.mult)
                last.then_inc(h1_ready, 1)

            def kv_negative(k, u, im):
                done = IM * (2 * k + u) + im
                dve.wait_ge(kv_ready, done + 1)
                dve.wait_ge(kv_exp_ready, IM * (2 * k + u))
                dve.tensor_scalar(kv_neg[:, im * NI:(im + 1) * NI, :], kv_ps[im], 0.0, None, ALU.min)\
                    .then_inc(kv_neg_ready, 1)

            def features(k, u, im):
                pairs = slice(im * NI, (im + 1) * NI)
                dve.wait_ge(kv_exp_ready, IM * (2 * k + u) + im + 1)
                dve.wait_ge(attn_ready, nth(k, u) - 1)
                dve.scalar_tensor_tensor(feat[:, pairs, :], kv_ps[im], 0.0, kv_exp[:, pairs, :], ALU.max, ALU.add)\
                    .then_inc(feat_ready, 1)

            def mask_attn(k, u):
                dve.wait_ge(attn_ready, nth(k, u))
                dve.wait_ge(aproj_ready, nth(k, u) - 1)
                dve.tensor_tensor(attn_sb[:, :, :], attn_ps, attn_mask[:, :].unsqueeze(1).broadcast_to([C, IM, C]),
                                  ALU.mult).then_inc(attn_masked, 1)

            def copy_fold(k, u):
                dve.wait_ge(fold_ready, nth(k, u))
                dve.wait_ge(y1_ready, nth(k, u) - 1)
                dve.tensor_tensor(fold_w[:, :, :], fold_ps, bproj1[:, :].unsqueeze(1).broadcast_to([C + 1, IM, C]),
                                  ALU.add).then_inc(fold_copied, 1)

            def residual2(k, u):
                pair = (2 * k + u) * NP
                dve.wait_ge(y1_ready, nth(k, u))
                dve.tensor_tensor(t2_all[:, bass.ds(pair, NP), :], y1_ps, t1[u][:, :, :], ALU.add).then_inc(t2_ready, 1)
                met(dve)
                dve.wait_ge(t2_ready, nth(k, u))
                for p in range(NP):
                    last = dve.bn_stats(ln2_stats[:, p, :], t2_all[:, bass.ds(pair + p, 1), :].rearrange("p a c -> p (a c)"))
                last.then_inc(ln2_bn_ready, 1)
                met(dve)
                dve.wait_ge(ln2_bn_ready, nth(k, u))
                for p in range(NP):
                    last = dve.bn_aggr(ln2_mv[:, p, :], ln2_stats[:, p, :])
                last.then_inc(ln2_mv_ready, 1)

            def norm2(k, u):
                pair = (2 * k + u) * NP
                dve.wait_ge(ln2_rstd_ready, nth(k, u))
                dve.wait_ge(h2T_ready, nth(k, u) - 1)
                for p in range(NP):
                    last = dve.tensor_scalar(h2[:, p, :],
                                             t2_all[:, bass.ds(pair + p, 1), :].rearrange("p a c -> p (a c)"),
                                             ln2_mv[:, p, 0:1], ln2_rstd[:, p:p + 1], ALU.subtract, ALU.mult)
                last.then_inc(h2_ready, 1)

            def copy_gate(k, u):
                dve.wait_ge(gate_ready, nth(k, u))
                dve.tensor_copy(scores[:, bass.ds((2 * k + u) * NP, NP), :], gate_ps).then_inc(gate_copied, 1)

            steps = [0]

            def link(ins):
                steps[0] += 1
                ins.then_inc(g_step, 1)
                dve.wait_ge(g_step, steps[0])

            def over_experts(v):
                return v.unsqueeze(2).broadcast_to([*v.shape, NE])

            def gate_shift(group):
                pairs = GATE_GROUPS[group]
                dve.wait_ge(gate_copied, (NB - 2, NB)[group])
                link(dve.tensor_reduce(g_max[:, pairs], scores[:, pairs, :], AX.X, ALU.max))
                dve.tensor_tensor(g_shift[:, pairs, :], scores[:, pairs, :], over_experts(g_max[:, pairs]),
                                  ALU.subtract).then_inc(g_shift_ready, 1)

            def gate_softmax(group):
                pairs = GATE_GROUPS[group]
                dve.wait_ge(g_exp_ready, group + 1)
                link(dve.tensor_reduce(g_sum[:, pairs], g_exp[:, pairs, :], AX.X, ALU.add))
                link(dve.reciprocal(g_rsum[:, pairs], g_sum[:, pairs]))
                link(dve.tensor_tensor(g_prob[:, pairs, :], g_exp[:, pairs, :], over_experts(g_rsum[:, pairs]),
                                       ALU.mult))

            def gate_compare(group):
                pairs = GATE_GROUPS[group]
                prob = g_prob[:, pairs, :]
                others = prob.unsqueeze(2).broadcast_to([*prob.shape[:2], NE, NE])
                own = prob.unsqueeze(3).broadcast_to([*prob.shape[:2], NE, NE])
                link(dve.tensor_tensor(g_above[:, pairs, :, :], others, own, ALU.is_gt))
                link(dve.tensor_tensor(g_equal[:, pairs, :, :], others, own, ALU.is_equal))

            def gate_rank(group):
                pairs = GATE_GROUPS[group]
                ge = g_equal[:, pairs, :, :].rearrange("p n a b -> p n (a b)")
                ga = g_above[:, pairs, :, :].rearrange("p n a b -> p n (a b)")
                low = lower[:, :, :].rearrange("p a b -> p (a b)").unsqueeze(1).broadcast_to(list(ge.shape))
                link(dve.tensor_tensor(ge, ge, low, ALU.mult))
                link(dve.tensor_tensor(ga, ga, ge, ALU.add))
                link(dve.tensor_reduce(g_rank[:, pairs, :], g_above[:, pairs, :, :], AX.X, ALU.add))

            def gate_shares(group):
                pairs = GATE_GROUPS[group]
                mix = g_mix[:, :].rearrange("p (n e) -> p n e", e=NE)[:, pairs, :]
                link(dve.scalar_tensor_tensor(mix, g_rank[:, pairs, :], 1.5, g_prob[:, pairs, :], ALU.is_lt, ALU.mult))
                link(dve.tensor_reduce(g_sum[:, pairs], mix, AX.X, ALU.add))
                link(dve.tensor_scalar(g_sum[:, pairs], g_sum[:, pairs], 1e-9, None, ALU.add))
                link(dve.reciprocal(g_rsum[:, pairs], g_sum[:, pairs]))
                dve.tensor_tensor(mix, mix, over_experts(g_rsum[:, pairs]), ALU.mult).then_inc(g_mix_ready, 1)

            def copy_mix(half):
                dve.wait_ge(mixT_ready, half + 1)
                dve.tensor_copy(mixT[:, half, :], mixT_ps).then_inc(mixT_copied, 1)

            def iteration(k, u, ahead2, ahead1, here, back1, back2):
                two_on, one_on, one_back, two_back = [after(k, u, n) for n in (2, 1, -1, -2)]

                drained = back1 and not here

                def when(there, step, *args):
                    if there:
                        step(*args)

                when(here, maxima, k, u, 0)
                when(back2, features, *two_back, 0)
                when(here, max_parts, k, u, 0)
                when(back2, kv_negative, *two_back, 1)
                when(here, maxima, k, u, 1)
                when(back2, features, *two_back, 1)
                when(here, max_parts, k, u, 1)
                when(drained, gate_shift, 0)
                when(back1, normalise, *one_back, 0)
                when(here, maxima, k, u, 2)
                when(back2, mask_attn, *two_back)
                when(drained, gate_softmax, 0)
                when(back1, normalise, *one_back, 1)
                when(ahead2, gn_stats_of, *two_on)
                when(here, max_parts, k, u, 2)
                when(back2, copy_fold, *two_back)
                when(drained, gate_compare, 0)
                when(here, maxima, k, u, 3)
                when(ahead2, gn_spread_of, *two_on)
                when(back2, residual2, *two_back)
                when(ahead2, gn_var_of, *two_on)
                when(back1, residual1, *one_back)
                when(ahead2, gn_apply, *two_on)
                when(back2, norm2, *two_back)
                when(here, max_parts, k, u, 3)
                when(back1, norm1, *one_back)
                when(drained, gate_rank, 0)
                when(ahead2, rest_of, *two_on, 0)
                when(ahead1, split_keys, *one_on)
                when(back2, copy_gate, *two_back)
                when(drained, gate_shares, 0)
                when(ahead2, rest_of, *two_on, 1)
                when(back1, kv_negative, *one_back, 0)

            for u in range(2):
                dve.memset(v_heads[u][:, :, :, :], 0.0).then_inc(setup_step, 1)
            dve.memset(bproj1[:, :], 0.0).then_inc(zeros_set, 1)
            dve.wait_ge(setup_step, 2)
            for u in range(2):
                for odd in range(2):
                    last = dve.memset(v_heads[u][odd * T:(odd + 1) * T, :, :, odd * 16 + HD:odd * 16 + HD + 1], 1.0)
                last.then_inc(zeros_set, 1)
            dve.wait_ge(pool_const, 22)
            gn_stats_of(0, 0)
            gn_spread_of(0, 0)
            gn_var_of(0, 0)
            dve.wait_ge(consts_ready, 6)
            gn_apply(0, 0)
            dve.wait_ge(wqkv0_loaded, 32)
            for s in range(2):
                last = dve.tensor_copy(wqk0[:, s, :].rearrange("p (b d a) -> p b d a", b=2, d=HD),
                                       wqkv0[:, s * C:(s + 1) * C].rearrange("p (a b d) -> p b d a", b=2, d=HD))
            last.then_inc(wqk0_ready, 1)
            dve.tensor_copy(ident_b[:, :], ident[:, :]).then_inc(ident_ready, 1)
            rest_of(0, 0, 0)
            dve.tensor_copy(offsets_f[:, :], offsets[:, :]).then_inc(setup_step, 1)
            dve.wait_ge(setup_step, 3)
            dve.tensor_tensor(offsets_sq[:, :], offsets_f[:, :], offsets_f[:, :], ALU.mult).then_inc(offs_sq_ready, 1)
            dve.wait_ge(lam_loaded, 16 * 4)
            dve.tensor_tensor(lam_prod[:, :, :], lam_in[:, 0:4:2, :], lam_in[:, 1:4:2, :], ALU.mult)\
                .then_inc(setup_step, 1)
            dve.wait_ge(setup_step, 4)
            dve.tensor_reduce(lam_sum[:, :], lam_prod[:, :, :], AX.X, ALU.add).then_inc(lam_sums, 1)
            rest_of(0, 0, 1)
            dve.wait_ge(lam_exps, 1)
            dve.tensor_tensor(lam_dif[:, :], lam_exp[:, 1:2], lam_exp[:, 0:1], ALU.subtract).then_inc(setup_step, 1)
            dve.wait_ge(setup_step, 5)
            dve.tensor_scalar(lam_keep[:, :], lam_dif[:, :], 1.0 - LAMBDA_INIT, None, ALU.add)\
                .then_inc(lam_keep_ready, 1)
            gn_stats_of(0, 1)
            gn_spread_of(0, 1)
            gn_var_of(0, 1)
            gn_apply(0, 1)
            dve.wait_ge(lam_col_ready, 1)
            dve.tensor_copy(lam_col[:, :], ps[0:C, TAIL_B, 0:1]).then_inc(lam_col_copied, 1)
            dve.wait_ge(lam_col_copied, 1)
            dve.wait_ge(gauss_ready, 1)
            dve.scalar_tensor_tensor(attn_mask[:, :], gauss[:, :], lam_col[:, 0:1], block[:, :], ALU.mult, ALU.mult)\
                .then_inc(setup_step, 1)
            dve.wait_ge(setup_step, 6)
            rest_of(0, 1, 0)
            split_keys(0, 0)
            rest_of(0, 1, 1)
            schedule(dve, iteration)

            dve.wait_ge(experts_loaded, 16 * 4)

            def mix_expert(t, k, u, e):
                acc = y_acc[u][:, :].rearrange("p (t n) -> p t n", n=TP)
                scaled = y_scaled[:, :].rearrange("p (t n) -> p t n", n=TP)
                if e == 0:
                    dve.wait_ge(mix_loaded[u], 16 * (k + 1))
                dve.wait_ge(down_done, (t * NE + e + 1) * CH)
                if e == 0 and (not isinstance(t, int) or t >= 2):
                    dve.wait_ge(final_ready, t - 1)
                dve.scalar_tensor_tensor(acc if e == 0 else scaled,
                                         down_ps[e % 2].rearrange("p (t n) -> p t n", n=TP), down_b[:, e:e + 1],
                                         mix_rows[u][:, :, e, :], ALU.add, ALU.mult).then_inc(scaled_step, 1)
                if e:
                    dve.wait_ge(scaled_step, 7 * t + 2 * e)
                    dve.tensor_tensor(acc, acc, scaled, ALU.add).then_inc(scaled_step, 1)
                    dve.wait_ge(scaled_step, 7 * t + 2 * e + 1)

            def finish_tile(t, k, u):
                dve.wait_ge(final_ready, t + 1)
                if not isinstance(t, int) or t >= 2:
                    dve.wait_ge(out_stored[u], 16 * 8 * k)
                dve.tensor_tensor(out_sb[u][:, :, :], final_ps, t2_all[:, bass.ds(t * FP, FP), :], ALU.add)\
                    .then_inc(out_ready, 1)

            def hidden_rest(t, n):
                dve.wait_ge(hidden_part1, t * NE * CH + n + 1)
                dve.wait_ge(hidden_ready, t * NE * CH + n + 1)
                if n >= 4 or not is_first(t):
                    dve.wait_ge(down_done, t * NE * CH + n - 3)
                dve.tensor_tensor(hidden_parts[n % 4][1][:, :], hidden[n % 4][:, :],
                                  hidden_parts[n % 4][0][:, :].bitcast(F32), ALU.subtract).then_inc(hidden_part2, 1)

            def first_tile():
                last_block = (NB // 2 - 1, 1)
                features(*last_block, 0)
                kv_negative(*last_block, 1)
                features(*last_block, 1)
                mask_attn(*last_block)
                hidden_rest(0, 0)
                copy_mix(0)
                hidden_rest(0, 1)
                copy_fold(*last_block)
                hidden_rest(0, 2)
                hidden_rest(0, 3)
                hidden_rest(0, 4)
                residual2(*last_block)
                for n in range(5, NE * CH):
                    hidden_rest(0, n)
                    if n % CH == 2:
                        mix_expert(0, 0, 0, n // CH - 1)
                    if n == 5:
                        norm2(*last_block)
                    if n == 9:
                        copy_gate(*last_block)
                gate_shift(1)

            def tile(t, k, u, second):
                gate_steps = {3: gate_softmax, 4: gate_compare, 6: gate_rank, 7: gate_shares}
                for n in range(NE * CH):
                    hidden_rest(t, n)
                    if n % CH == 2 and n > 2:
                        mix_expert(t, k, u, n // CH - 1)
                    elif n == 2:
                        mix_expert(t - 1, k - 1 + u, 1 - u, NE - 1)
                    if n == 9:
                        finish_tile(t - 1, k - 1 + u, 1 - u)
                    if second and n in gate_steps:
                        gate_steps[n](1)
                if second:
                    copy_mix(1)

            first_tile()
            tile(1, 0, 1, True)
            with dve.Fori(1, NFT // 2) as k:
                for u in range(2):
                    tile(2 * k + u, k, u, False)
            mix_expert(NFT - 1, NFT // 2 - 1, 1, NE - 1)
            finish_tile(NFT - 1, NFT // 2 - 1, 1)


_INS = ['x', 'L0_conv_w_qkv', 'L0_conv_b_qkv', 'L0_conv_w_proj', 'L0_conv_b_proj', 'L1_attn_qkv_w', 'L1_attn_qkv_b',
        'L1_attn_proj_w', 'L1_attn_proj_b', 'L1_attn_lambda_k1', 'L1_attn_lambda_v1', 'L1_attn_lambda_k2',
        'L1_attn_lambda_v2', 'L1_ffn_gate_w', 'L1_ffn_gate_b', 'L1_ffn_w1', 'L1_ffn_b1', 'L1_ffn_w2', 'L1_ffn_b2']
_OUT = ((B, HI, WI, C), 'float32')


def kernel(**inputs):
    import concourse.bacc as bacc
    from concourse.bass_utils import run_bass_kernel_spmd

    nc = bacc.Bacc("TRN2", target_bir_lowering=False, num_devices=1)
    arrays, args = {}, []
    for name in _INS:
        a = np.ascontiguousarray(inputs[name])
        arrays[f"in_{name}"] = a
        args.append(nc.dram_tensor(f"in_{name}", a.shape, mybir.dt.from_np(a.dtype), kind="ExternalInput").ap())
    args.append(nc.dram_tensor("out_0", _OUT[0], mybir.dt.from_np(np.dtype(_OUT[1])), kind="ExternalOutput").ap())
    build(nc, *args)
    r = run_bass_kernel_spmd(nc, [arrays], core_ids=[0])
    return r.results[0]["out_0"]
```
